# Optimizing a Trainium2 kernel written in Bass

```python
import numpy as np
import jax
import jax.numpy as jnp

def _softmax(x, axis=-1):
    return jax.nn.softmax(x, axis=axis)

def _gelu(x):
    return jax.nn.gelu(x, approximate=True)

def _silu(x):
    return jax.nn.silu(x)

def _sigmoid(x):
    return jax.nn.sigmoid(x)

def _layernorm(x, axis=-1, eps=1e-05):
    m = jnp.mean(x, axis=axis, keepdims=True)
    v = jnp.var(x, axis=axis, keepdims=True)
    return (x - m) / jnp.sqrt(v + eps)

def _scatter_add(tgt, idx, src, axis=0):
    return tgt.at[idx].add(src)

def _segment_sum(src, seg, n):
    return jax.ops.segment_sum(src, seg, n)
kernel_name = 'mk_gnn_ffn_d4_gnn_r32_0ce687'

def setup_inputs(seed: int=0):
    np.random.seed(seed)
    _w = jnp.asarray

    def _rec_inputs():
        import jax
        import jax.numpy as jnp
        _gk = jax.random.key(seed)
        x = -0.0002117 + 1 * jax.random.normal(jax.random.fold_in(_gk, 1), (3125, 256), jnp.float32)
        _s = jax.random.randint(jax.random.fold_in(_gk, 2), (25000,), 0, 3125, jnp.int32)
        _d = jax.random.randint(jax.random.fold_in(_gk, 3), (25000,), 0, 3125, jnp.int32)
        _loop = jnp.arange(3125, dtype=jnp.int32)
        src = jnp.concatenate([_s, _d, _loop])
        dst = jnp.concatenate([_d, _s, _loop])
        _o = jnp.argsort(dst, stable=True)
        src = src[_o]
        dst = dst[_o]
        edge_type_8 = jax.random.randint(jax.random.fold_in(_gk, 13), (53125,), 0, 8, jnp.int32)
        edge_weight = jax.random.uniform(jax.random.fold_in(_gk, 14), (53125,), jnp.float32, 0.0, 0.999999)
        node_type_4 = jax.random.randint(jax.random.fold_in(_gk, 15), (3125,), 0, 4, jnp.int32)
        return (x, src, dst, edge_type_8, edge_weight, node_type_4)
    x, src, dst, edge_type_8, edge_weight, node_type_4 = _rec_inputs()

    def _L0_gnn_setup():
        import jax, jax.numpy as jnp
        import numpy as np
        N_NODES = 3125
        N_EDGES = 100000
        IN_FEAT = 256
        OUT_FEAT = 256
        EPS = 1e-12
        key = jax.random.key(seed)
        k1, k2, k3, k4, k5 = jax.random.split(key, 5)
        x = jax.random.normal(k1, (N_NODES, IN_FEAT), dtype=jnp.float32)
        W = jax.random.normal(k2, (IN_FEAT, OUT_FEAT), dtype=jnp.float32) / np.sqrt(IN_FEAT)
        b = jax.random.normal(k3, (OUT_FEAT,), dtype=jnp.float32) * 0.01
        src = jax.random.randint(k4, (N_EDGES,), 0, N_NODES, dtype=jnp.int32)
        dst = jax.random.randint(k5, (N_EDGES,), 0, N_NODES, dtype=jnp.int32)
        return {'x': x, 'W': W, 'b': b, 'src': src, 'dst': dst}
    _L0_gnn_all = _L0_gnn_setup()
    _L0_gnn_in = {k: v for k, v in _L0_gnn_all.items() if k in ('W', 'b')}
    del _L0_gnn_all

    def _L0_ffn_setup():
        import jax, jax.numpy as jnp
        import numpy as np
        B, S, H, F, E, K = (8, 128, 256, 512, 16, 2)
        EPS = 1e-05
        key = jax.random.key(seed)
        ks = jax.random.split(key, 9)
        sc = 0.02
        return {'x': jax.random.normal(ks[0], (B, S, H), dtype=jnp.float32), 'gate_w': jax.random.normal(ks[1], (H, E), dtype=jnp.float32) * sc, 'gate_b': jnp.zeros((E,), dtype=jnp.float32), 'w1': jax.random.normal(ks[2], (E, H, F), dtype=jnp.float32) * sc, 'b1': jnp.zeros((E, F), dtype=jnp.float32), 'w2': jax.random.normal(ks[3], (E, F, H), dtype=jnp.float32) * sc, 'b2': jnp.zeros((E, H), dtype=jnp.float32), 'gamma': jnp.ones((H,), dtype=jnp.float32), 'beta': jnp.zeros((H,), dtype=jnp.float32)}
    _L0_ffn_all = _L0_ffn_setup()
    _L0_ffn_in = {k: v for k, v in _L0_ffn_all.items() if k in ('gate_w', 'gate_b', 'w1', 'b1', 'w2', 'b2', 'gamma', 'beta')}
    del _L0_ffn_all

    def _L1_gnn_setup():
        import jax, jax.numpy as jnp
        import numpy as np
        N_NODES = 3125
        N_EDGES = 50000
        D = 256
        key = jax.random.key(seed)
        ks = jax.random.split(key, 8)
        h6_all = jax.random.normal(ks[0], (N_NODES, D), dtype=jnp.float32)
        edge_index = jax.random.randint(ks[1], (2, N_EDGES), 0, N_NODES, dtype=jnp.int64)
        edge_weight = jax.random.uniform(ks[2], (N_EDGES,), dtype=jnp.float32)
        s = 1.0 / np.sqrt(D)
        W = jax.random.normal(ks[3], (D, D), dtype=jnp.float32) * s
        b = jnp.zeros((D,), dtype=jnp.float32)
        W1 = jax.random.normal(ks[4], (D, D), dtype=jnp.float32) * s
        b1 = jnp.zeros((D,), dtype=jnp.float32)
        W2 = jax.random.normal(ks[5], (D, D), dtype=jnp.float32) * s
        b2 = jnp.zeros((D,), dtype=jnp.float32)
        return {'h6_all': h6_all, 'edge_index': edge_index, 'edge_weight': edge_weight, 'W': W, 'b': b, 'W1': W1, 'b1': b1, 'W2': W2, 'b2': b2}
    _L1_gnn_all = _L1_gnn_setup()
    _L1_gnn_in = {k: v for k, v in _L1_gnn_all.items() if k in ('W', 'b', 'W1', 'b1', 'W2', 'b2')}
    del _L1_gnn_all

    def _L1_ffn_setup():
        import jax, jax.numpy as jnp
        import numpy as np
        D_MODEL = 256
        EXPERT_DIM = 512
        NUM_EXPERTS = 8
        TOP_K = 2
        SEQ_LEN = 64
        BATCH = 2
        key = jax.random.key(seed)
        ks = jax.random.split(key, 8)
        s = 0.02
        x = jax.random.normal(ks[0], (SEQ_LEN, BATCH, D_MODEL), dtype=jnp.float32)
        Wg = jax.random.normal(ks[1], (D_MODEL, NUM_EXPERTS), dtype=jnp.float32) * s
        bg = jax.random.normal(ks[2], (NUM_EXPERTS,), dtype=jnp.float32) * s
        bias = jnp.zeros((NUM_EXPERTS,), dtype=jnp.float32)
        W1 = jax.random.normal(ks[3], (NUM_EXPERTS, D_MODEL, EXPERT_DIM), dtype=jnp.float32) * s
        b1 = jax.random.normal(ks[4], (NUM_EXPERTS, EXPERT_DIM), dtype=jnp.float32) * s
        W2 = jax.random.normal(ks[5], (NUM_EXPERTS, EXPERT_DIM, D_MODEL), dtype=jnp.float32) * s
        b2 = jax.random.normal(ks[6], (NUM_EXPERTS, D_MODEL), dtype=jnp.float32) * s
        return {'x': x, 'Wg': Wg, 'bg': bg, 'bias': bias, 'W1': W1, 'b1': b1, 'W2': W2, 'b2': b2}
    _L1_ffn_all = _L1_ffn_setup()
    _L1_ffn_in = {k: v for k, v in _L1_ffn_all.items() if k in ('Wg', 'bg', 'bias', 'W1', 'b1', 'W2', 'b2')}
    del _L1_ffn_all

    def _L2_gnn_setup():
        import jax, jax.numpy as jnp
        import numpy as np
        N, E = (50000, 25000)
        IN_DIM = OUT_DIM = 256
        T, R, H = (4, 8, 8)
        DK = OUT_DIM // H

        def typed_linear(x, node_type, W, b):
            out = jnp.zeros((x.shape[0], W.shape[2]), dtype=x.dtype)
            for t in range(W.shape[0]):
                y = x @ W[t] + b[t]
                out = jnp.where((node_type == t)[:, None], y, out)
            return out
        key = jax.random.key(seed)
        ks = jax.random.split(key, 16)
        x = jax.random.normal(ks[0], (N, IN_DIM), dtype=jnp.float32)
        node_type = jax.random.randint(ks[1], (N,), 0, T, dtype=jnp.int32)
        src = jax.random.randint(ks[2], (E,), 0, N, dtype=jnp.int32)
        dst = jnp.arange(E, dtype=jnp.int32) % N
        etype = jax.random.randint(ks[3], (E,), 0, R, dtype=jnp.int32)
        w_scale = np.sqrt(2.0 / (IN_DIM + OUT_DIM)).astype(np.float32)
        r_scale = np.sqrt(2.0 / (DK + DK)).astype(np.float32)

        def lin(k):
            return jax.random.normal(k, (T, IN_DIM, OUT_DIM), dtype=jnp.float32) * w_scale
        return {'x': x, 'node_type': node_type, 'src': src, 'dst': dst, 'etype': etype, 'Wk': lin(ks[4]), 'bk': jnp.zeros((T, OUT_DIM), jnp.float32), 'Wq': lin(ks[5]), 'bq': jnp.zeros((T, OUT_DIM), jnp.float32), 'Wv': lin(ks[6]), 'bv': jnp.zeros((T, OUT_DIM), jnp.float32), 'Wa': lin(ks[7]), 'ba': jnp.zeros((T, OUT_DIM), jnp.float32), 'rel_att': jax.random.normal(ks[8], (R, H, DK, DK), jnp.float32) * r_scale, 'rel_msg': jax.random.normal(ks[9], (R, H, DK, DK), jnp.float32) * r_scale, 'rel_pri': jnp.ones((R, H), jnp.float32), 'skip': jnp.ones((T,), jnp.float32)}
    _L2_gnn_all = _L2_gnn_setup()
    _L2_gnn_in = {k: v for k, v in _L2_gnn_all.items() if k in ('Wk', 'bk', 'Wq', 'bq', 'Wv', 'bv', 'Wa', 'ba', 'rel_att', 'rel_msg', 'rel_pri', 'skip')}
    del _L2_gnn_all

    def _L2_ffn_setup():
        import jax, jax.numpy as jnp
        import numpy as np
        BN_EPS = 0.001

        def _bn(h, g, b, m, v):
            return g * (h - m) * jax.lax.rsqrt(v + BN_EPS) + b
        key = jax.random.key(seed)
        ks = jax.random.split(key, 8)
        B, F, Df = (256, 64, 256)
        E, H, D = (8, 256, 256)
        s1 = 1.0 / np.sqrt(Df)
        s2 = 1.0 / np.sqrt(H)
        return {'x': jax.random.normal(ks[0], (B, F, Df), jnp.float32), 'Wr': jax.random.normal(ks[1], (Df, E), jnp.float32) * s1, 'br': jnp.zeros((E,), jnp.float32), 'W1': jax.random.normal(ks[2], (E, Df, H), jnp.float32) * s1, 'b1': jnp.zeros((E, H), jnp.float32), 'g1': jnp.ones((E, H), jnp.float32), 'be1': jnp.zeros((E, H), jnp.float32), 'm1': jnp.zeros((E, H), jnp.float32), 'v1': jnp.ones((E, H), jnp.float32), 'W2': jax.random.normal(ks[3], (E, H, H), jnp.float32) * s2, 'b2': jnp.zeros((E, H), jnp.float32), 'g2': jnp.ones((E, H), jnp.float32), 'be2': jnp.zeros((E, H), jnp.float32), 'm2': jnp.zeros((E, H), jnp.float32), 'v2': jnp.ones((E, H), jnp.float32), 'Wo': jax.random.normal(ks[4], (E, H, D), jnp.float32) * s2, 'bo': jnp.zeros((E, D), jnp.float32)}
    _L2_ffn_all = _L2_ffn_setup()
    _L2_ffn_in = {k: v for k, v in _L2_ffn_all.items() if k in ('Wr', 'br', 'W1', 'b1', 'g1', 'be1', 'm1', 'v1', 'W2', 'b2', 'g2', 'be2', 'm2', 'v2', 'Wo', 'bo')}
    del _L2_ffn_all

    def _L3_gnn_setup():
        import jax, jax.numpy as jnp
        import numpy as np
        N_NODES = 50000
        N_EDGES = 25000
        NEG_SLOPE = 0.2

        def gat_conv(x, W, att_src, att_dst, bias, src, dst, heads, out_ch, concat):
            n = x.shape[0]
            xh = (x @ W).reshape(n, heads, out_ch)
            a_s = jnp.einsum('nhc,hc->nh', xh, att_src)
            a_d = jnp.einsum('nhc,hc->nh', xh, att_dst)
            e = a_s[src] + a_d[dst]
            e = jnp.where(e > 0, e, NEG_SLOPE * e)
            m = jax.ops.segment_max(e, dst, num_segments=n)
            e = jnp.exp(e - m[dst])
            denom = jax.ops.segment_sum(e, dst, num_segments=n)
            alpha = e / (denom[dst] + 1e-16)
            msg = xh[src] * alpha[:, :, None]
            out = jax.ops.segment_sum(msg, dst, num_segments=n)
            out = out.reshape(n, heads * out_ch) if concat else out.mean(axis=1)
            return out + bias
        key = jax.random.key(seed)
        ks = jax.random.split(key, 16)
        x = jax.random.normal(ks[0], (N_NODES, 256), dtype=jnp.float32)
        edge_index = jax.random.randint(ks[1], (2, N_EDGES), 0, N_NODES, dtype=jnp.int32)
        s = 0.05
        return {'x': x, 'edge_index': edge_index, 'W0': jax.random.normal(ks[2], (256, 256), jnp.float32) * s, 'as0': jax.random.normal(ks[3], (4, 64), jnp.float32) * s, 'ad0': jax.random.normal(ks[4], (4, 64), jnp.float32) * s, 'b0': jnp.zeros((256,), jnp.float32), 'W1': jax.random.normal(ks[5], (256, 256), jnp.float32) * s, 'as1': jax.random.normal(ks[6], (4, 64), jnp.float32) * s, 'ad1': jax.random.normal(ks[7], (4, 64), jnp.float32) * s, 'b1': jnp.zeros((256,), jnp.float32), 'W2': jax.random.normal(ks[8], (256, 256), jnp.float32) * s, 'as2': jax.random.normal(ks[9], (1, 256), jnp.float32) * s, 'ad2': jax.random.normal(ks[10], (1, 256), jnp.float32) * s, 'b2': jnp.zeros((256,), jnp.float32)}
    _L3_gnn_all = _L3_gnn_setup()
    _L3_gnn_in = {k: v for k, v in _L3_gnn_all.items() if k in ('W0', 'as0', 'ad0', 'b0', 'W1', 'as1', 'ad1', 'b1', 'W2', 'as2', 'ad2', 'b2')}
    del _L3_gnn_all

    def _L3_ffn_setup():
        import jax, jax.numpy as jnp
        import numpy as np
        B, N, D = (16, 128, 256)
        NUM_EXPERTS, TOP_K, HEADS = (4, 2, 4)
        N_EDGES = 32768
        LN_EPS = 1e-05

        def _layernorm(x, g, b):
            mu = x.mean(-1, keepdims=True)
            var = ((x - mu) ** 2).mean(-1, keepdims=True)
            return (x - mu) * jax.lax.rsqrt(var + LN_EPS) * g + b

        def _forward(x, edge_index, W_gat, att_src, att_dst, b_gat, ln_gamma, ln_beta, W1, b1, W2, b2):
            Bc, Nc, Dc = x.shape
            M = Bc * Nc
            x_flat = x.reshape(M, Dc)
            h = (x_flat @ W_gat).reshape(M, HEADS, NUM_EXPERTS)
            loops = jnp.arange(M, dtype=edge_index.dtype)
            src = jnp.concatenate([edge_index[0], loops])
            dst = jnp.concatenate([edge_index[1], loops])
            a_src = (h * att_src).sum(-1)
            a_dst = (h * att_dst).sum(-1)
            e = jax.nn.leaky_relu(a_src[src] + a_dst[dst], negative_slope=0.2)
            e_max = jax.ops.segment_max(e, dst, num_segments=M)
            ee = jnp.exp(e - e_max[dst])
            denom = jax.ops.segment_sum(ee, dst, num_segments=M)
            alpha = ee / (denom[dst] + 1e-16)
            msg = h[src] * alpha[:, :, None]
            agg = jax.ops.segment_sum(msg, dst, num_segments=M).reshape(M, HEADS * NUM_EXPERTS) + b_gat
            scores = _layernorm(agg, ln_gamma, ln_beta).reshape(M, HEADS, NUM_EXPERTS).mean(1)
            scores = scores.reshape(Bc, Nc, NUM_EXPERTS)
            topk_s, topk_i = jax.lax.top_k(scores, TOP_K)
            w = jax.nn.softmax(topk_s, axis=-1)
            out = jnp.zeros_like(x)
            for ei in range(NUM_EXPERTS):
                g = jnp.where(topk_i == ei, w, 0.0).sum(-1)
                hh = jax.nn.gelu(x @ W1[ei] + b1[ei], approximate=False)
                out = out + g[..., None] * (hh @ W2[ei] + b2[ei])
            return out
        key = jax.random.key(seed)
        ks = jax.random.split(key, 8)
        s = 0.05
        return {'x': jax.random.normal(ks[0], (B, N, D), jnp.float32), 'W_gat': jax.random.normal(ks[1], (D, HEADS * NUM_EXPERTS), jnp.float32) * s, 'att_src': jax.random.normal(ks[2], (HEADS, NUM_EXPERTS), jnp.float32) * s, 'att_dst': jax.random.normal(ks[3], (HEADS, NUM_EXPERTS), jnp.float32) * s, 'b_gat': jnp.zeros((HEADS * NUM_EXPERTS,), jnp.float32), 'ln_gamma': jnp.ones((HEADS * NUM_EXPERTS,), jnp.float32), 'ln_beta': jnp.zeros((HEADS * NUM_EXPERTS,), jnp.float32), 'W1': jax.random.normal(ks[4], (NUM_EXPERTS, D, 2 * D), jnp.float32) * s, 'b1': jnp.zeros((NUM_EXPERTS, 2 * D), jnp.float32), 'W2': jax.random.normal(ks[5], (NUM_EXPERTS, 2 * D, D), jnp.float32) * s, 'b2': jnp.zeros((NUM_EXPERTS, D), jnp.float32), 'edge_index': jax.random.randint(ks[6], (2, N_EDGES), 0, B * N, jnp.int32)}
    _L3_ffn_all = _L3_ffn_setup()
    _L3_ffn_in = {k: v for k, v in _L3_ffn_all.items() if k in ('W_gat', 'att_src', 'att_dst', 'b_gat', 'ln_gamma', 'ln_beta', 'W1', 'b1', 'W2', 'b2', 'edge_index')}
    del _L3_ffn_all
    return {'x': x, 'src': src, 'dst': dst, 'edge_type_8': edge_type_8, 'edge_weight': edge_weight, 'node_type_4': node_type_4, 'L0_gnn_W': _L0_gnn_in['W'], 'L0_gnn_b': _L0_gnn_in['b'], 'L0_ffn_gate_w': _L0_ffn_in['gate_w'], 'L0_ffn_gate_b': _L0_ffn_in['gate_b'], 'L0_ffn_w1': _L0_ffn_in['w1'], 'L0_ffn_b1': _L0_ffn_in['b1'], 'L0_ffn_w2': _L0_ffn_in['w2'], 'L0_ffn_b2': _L0_ffn_in['b2'], 'L0_ffn_gamma': _L0_ffn_in['gamma'], 'L0_ffn_beta': _L0_ffn_in['beta'], 'L1_gnn_W': _L1_gnn_in['W'], 'L1_gnn_b': _L1_gnn_in['b'], 'L1_gnn_W1': _L1_gnn_in['W1'], 'L1_gnn_b1': _L1_gnn_in['b1'], 'L1_gnn_W2': _L1_gnn_in['W2'], 'L1_gnn_b2': _L1_gnn_in['b2'], 'L1_ffn_Wg': _L1_ffn_in['Wg'], 'L1_ffn_bg': _L1_ffn_in['bg'], 'L1_ffn_bias': _L1_ffn_in['bias'], 'L1_ffn_W1': _L1_ffn_in['W1'], 'L1_ffn_b1': _L1_ffn_in['b1'], 'L1_ffn_W2': _L1_ffn_in['W2'], 'L1_ffn_b2': _L1_ffn_in['b2'], 'L2_gnn_Wk': _L2_gnn_in['Wk'], 'L2_gnn_bk': _L2_gnn_in['bk'], 'L2_gnn_Wq': _L2_gnn_in['Wq'], 'L2_gnn_bq': _L2_gnn_in['bq'], 'L2_gnn_Wv': _L2_gnn_in['Wv'], 'L2_gnn_bv': _L2_gnn_in['bv'], 'L2_gnn_Wa': _L2_gnn_in['Wa'], 'L2_gnn_ba': _L2_gnn_in['ba'], 'L2_gnn_rel_att': _L2_gnn_in['rel_att'], 'L2_gnn_rel_msg': _L2_gnn_in['rel_msg'], 'L2_gnn_rel_pri': _L2_gnn_in['rel_pri'], 'L2_gnn_skip': _L2_gnn_in['skip'], 'L2_ffn_Wr': _L2_ffn_in['Wr'], 'L2_ffn_br': _L2_ffn_in['br'], 'L2_ffn_W1': _L2_ffn_in['W1'], 'L2_ffn_b1': _L2_ffn_in['b1'], 'L2_ffn_g1': _L2_ffn_in['g1'], 'L2_ffn_be1': _L2_ffn_in['be1'], 'L2_ffn_m1': _L2_ffn_in['m1'], 'L2_ffn_v1': _L2_ffn_in['v1'], 'L2_ffn_W2': _L2_ffn_in['W2'], 'L2_ffn_b2': _L2_ffn_in['b2'], 'L2_ffn_g2': _L2_ffn_in['g2'], 'L2_ffn_be2': _L2_ffn_in['be2'], 'L2_ffn_m2': _L2_ffn_in['m2'], 'L2_ffn_v2': _L2_ffn_in['v2'], 'L2_ffn_Wo': _L2_ffn_in['Wo'], 'L2_ffn_bo': _L2_ffn_in['bo'], 'L3_gnn_W0': _L3_gnn_in['W0'], 'L3_gnn_as0': _L3_gnn_in['as0'], 'L3_gnn_ad0': _L3_gnn_in['ad0'], 'L3_gnn_b0': _L3_gnn_in['b0'], 'L3_gnn_W1': _L3_gnn_in['W1'], 'L3_gnn_as1': _L3_gnn_in['as1'], 'L3_gnn_ad1': _L3_gnn_in['ad1'], 'L3_gnn_b1': _L3_gnn_in['b1'], 'L3_gnn_W2': _L3_gnn_in['W2'], 'L3_gnn_as2': _L3_gnn_in['as2'], 'L3_gnn_ad2': _L3_gnn_in['ad2'], 'L3_gnn_b2': _L3_gnn_in['b2'], 'L3_ffn_W_gat': _L3_ffn_in['W_gat'], 'L3_ffn_att_src': _L3_ffn_in['att_src'], 'L3_ffn_att_dst': _L3_ffn_in['att_dst'], 'L3_ffn_b_gat': _L3_ffn_in['b_gat'], 'L3_ffn_ln_gamma': _L3_ffn_in['ln_gamma'], 'L3_ffn_ln_beta': _L3_ffn_in['ln_beta'], 'L3_ffn_W1': _L3_ffn_in['W1'], 'L3_ffn_b1': _L3_ffn_in['b1'], 'L3_ffn_W2': _L3_ffn_in['W2'], 'L3_ffn_b2': _L3_ffn_in['b2'], 'L3_ffn_edge_index': _L3_ffn_in['edge_index']}

def reference(x, src, dst, edge_type_8, edge_weight, node_type_4, L0_gnn_W, L0_gnn_b, L0_ffn_gate_w, L0_ffn_gate_b, L0_ffn_w1, L0_ffn_b1, L0_ffn_w2, L0_ffn_b2, L0_ffn_gamma, L0_ffn_beta, L1_gnn_W, L1_gnn_b, L1_gnn_W1, L1_gnn_b1, L1_gnn_W2, L1_gnn_b2, L1_ffn_Wg, L1_ffn_bg, L1_ffn_bias, L1_ffn_W1, L1_ffn_b1, L1_ffn_W2, L1_ffn_b2, L2_gnn_Wk, L2_gnn_bk, L2_gnn_Wq, L2_gnn_bq, L2_gnn_Wv, L2_gnn_bv, L2_gnn_Wa, L2_gnn_ba, L2_gnn_rel_att, L2_gnn_rel_msg, L2_gnn_rel_pri, L2_gnn_skip, L2_ffn_Wr, L2_ffn_br, L2_ffn_W1, L2_ffn_b1, L2_ffn_g1, L2_ffn_be1, L2_ffn_m1, L2_ffn_v1, L2_ffn_W2, L2_ffn_b2, L2_ffn_g2, L2_ffn_be2, L2_ffn_m2, L2_ffn_v2, L2_ffn_Wo, L2_ffn_bo, L3_gnn_W0, L3_gnn_as0, L3_gnn_ad0, L3_gnn_b0, L3_gnn_W1, L3_gnn_as1, L3_gnn_ad1, L3_gnn_b1, L3_gnn_W2, L3_gnn_as2, L3_gnn_ad2, L3_gnn_b2, L3_ffn_W_gat, L3_ffn_att_src, L3_ffn_att_dst, L3_ffn_b_gat, L3_ffn_ln_gamma, L3_ffn_ln_beta, L3_ffn_W1, L3_ffn_b1, L3_ffn_W2, L3_ffn_b2, L3_ffn_edge_index):
    import jax
    import jax.numpy as jnp

    def _L0_gnn_ref(x, W, b, src, dst):
        import jax, jax.numpy as jnp
        import numpy as np
        N_NODES = 3125
        N_EDGES = 100000
        IN_FEAT = 256
        OUT_FEAT = 256
        EPS = 1e-12
        N = x.shape[0]
        ones = jnp.ones(src.shape[0], dtype=x.dtype)
        deg_out = jnp.maximum(jax.ops.segment_sum(ones, src, num_segments=N), 1.0)
        deg_in = jnp.maximum(jax.ops.segment_sum(ones, dst, num_segments=N), 1.0)
        h = x * jax.lax.rsqrt(deg_out)[:, None]
        agg = jax.ops.segment_sum(h[src], dst, num_segments=N)
        h = agg * jax.lax.rsqrt(deg_in)[:, None]
        h = h @ W + b
        h = jax.nn.relu(h)
        nrm = jnp.maximum(jnp.linalg.norm(h, axis=1, keepdims=True), EPS)
        return h / nrm

    def _L0_ffn_ref(x, gate_w, gate_b, w1, b1, w2, b2, gamma, beta):
        import jax, jax.numpy as jnp
        import numpy as np
        B, S, H, F, E, K = (8, 128, 256, 512, 16, 2)
        EPS = 1e-05
        gate_logits = x @ gate_w + gate_b
        topk_vals, topk_idx = jax.lax.top_k(gate_logits, K)
        topk_w = jax.nn.softmax(topk_vals, axis=-1)
        h = jax.nn.relu(jnp.einsum('bsh,ehf->bsef', x, w1) + b1)
        expert_out = jnp.einsum('bsef,efh->bseh', h, w2) + b2
        sel = jnp.take_along_axis(expert_out, topk_idx[:, :, :, None], axis=2)
        moe = jnp.sum(topk_w[..., None] * sel, axis=2)
        y = x + moe
        mu = jnp.mean(y, axis=-1, keepdims=True)
        var = jnp.var(y, axis=-1, keepdims=True)
        return (y - mu) / jnp.sqrt(var + EPS) * gamma + beta

    def _L1_gnn_ref(h6_all, edge_index, edge_weight, W, b, W1, b1, W2, b2):
        import jax, jax.numpy as jnp
        import numpy as np
        N_NODES = 3125
        N_EDGES = 50000
        D = 256
        'GCNConv(256->256, weighted, self-loops, symmetric norm) + 2-layer MLP head.'
        N = h6_all.shape[0]
        row, col = (edge_index[0], edge_index[1])
        sl = jnp.arange(N, dtype=edge_index.dtype)
        row_sl = jnp.concatenate([row, sl])
        col_sl = jnp.concatenate([col, sl])
        ew_sl = jnp.concatenate([edge_weight, jnp.ones((N,), dtype=edge_weight.dtype)])
        deg = jax.ops.segment_sum(ew_sl, row_sl, num_segments=N)
        dinv = jnp.where(deg > 0, jax.lax.rsqrt(deg), 0.0)
        norm = dinv[row_sl] * ew_sl * dinv[col_sl]
        xw = h6_all @ W
        msgs = xw[col_sl] * norm[:, None]
        h7 = jax.ops.segment_sum(msgs, row_sl, num_segments=N) + b
        h = jax.nn.relu(h7 @ W1 + b1)
        out = h @ W2 + b2
        return out

    def _L1_ffn_ref(x, Wg, bg, bias, W1, b1, W2, b2):
        import jax, jax.numpy as jnp
        import numpy as np
        D_MODEL = 256
        EXPERT_DIM = 512
        NUM_EXPERTS = 8
        TOP_K = 2
        SEQ_LEN = 64
        BATCH = 2
        x_flat = x.reshape(-1, D_MODEL)
        gate_logits = x_flat @ Wg + bg + bias
        topk_vals, topk_idx = jax.lax.top_k(gate_logits, TOP_K)
        topk_w = jax.nn.softmax(topk_vals, axis=-1)
        combine = (jax.nn.one_hot(topk_idx, NUM_EXPERTS, dtype=x.dtype) * topk_w[..., None]).sum(axis=1)
        h = jax.nn.relu(jnp.einsum('td,edh->teh', x_flat, W1) + b1)
        y = jnp.einsum('teh,ehd->ted', h, W2) + b2
        out = jnp.einsum('ted,te->td', y, combine)
        return out.reshape(x.shape)

    def _L2_gnn_ref(x, node_type, src, dst, etype, Wk, bk, Wq, bq, Wv, bv, Wa, ba, rel_att, rel_msg, rel_pri, skip):
        import jax, jax.numpy as jnp
        import numpy as np
        N, E = (50000, 25000)
        IN_DIM = OUT_DIM = 256
        T, R, H = (4, 8, 8)
        DK = OUT_DIM // H

        def typed_linear(x, node_type, W, b):
            out = jnp.zeros((x.shape[0], W.shape[2]), dtype=x.dtype)
            for t in range(W.shape[0]):
                y = x @ W[t] + b[t]
                out = jnp.where((node_type == t)[:, None], y, out)
            return out
        n = x.shape[0]
        r = rel_att.shape[0]
        h, dk = (rel_att.shape[1], rel_att.shape[2])
        sqrt_dk = jnp.asarray(np.sqrt(dk), x.dtype)
        k = typed_linear(x, node_type, Wk, bk).reshape(n, h, dk)
        q = typed_linear(x, node_type, Wq, bq).reshape(n, h, dk)
        v = typed_linear(x, node_type, Wv, bv).reshape(n, h, dk)
        k_r = jnp.einsum('nhd,rhde->rnhe', k, rel_att)
        v_r = jnp.einsum('nhd,rhde->rnhe', v, rel_msg)
        key_e = k_r[etype, src]
        val_e = v_r[etype, src]
        att = (q[dst] * key_e).sum(-1) * rel_pri[etype] / sqrt_dk
        seg = dst * r + etype
        s = n * r
        m = jax.ops.segment_max(att, seg, num_segments=s)
        ex = jnp.exp(att - m[seg])
        den = jax.ops.segment_sum(ex, seg, num_segments=s)
        alpha = ex / den[seg]
        hmsg = jax.ops.segment_sum(alpha[..., None] * val_e, seg, num_segments=s)
        hmsg = hmsg.reshape(n, r, h * dk)
        cnt = jax.ops.segment_sum(jnp.ones((att.shape[0],), x.dtype), seg, num_segments=s)
        present = (cnt.reshape(n, r) > 0).astype(x.dtype)
        t = hmsg.sum(1) / jnp.maximum(present.sum(1, keepdims=True), 1.0)
        trans = typed_linear(t, node_type, Wa, ba)
        a = jax.nn.sigmoid(skip)[node_type][:, None]
        return trans * a + x * (1.0 - a)

    def _L2_ffn_ref(x, Wr, br, W1, b1, g1, be1, m1, v1, W2, b2, g2, be2, m2, v2, Wo, bo):
        import jax, jax.numpy as jnp
        import numpy as np
        BN_EPS = 0.001

        def _bn(h, g, b, m, v):
            return g * (h - m) * jax.lax.rsqrt(v + BN_EPS) + b
        feat = jnp.mean(x, axis=0)
        w = jax.nn.softmax(feat @ Wr + br, axis=-1)
        h = jnp.einsum('bfd,edh->bfeh', x, W1) + b1
        h = jax.nn.relu(_bn(h, g1, be1, m1, v1))
        h = jnp.einsum('bfeh,ehk->bfek', h, W2) + b2
        h = jax.nn.relu(_bn(h, g2, be2, m2, v2))
        y = jnp.einsum('bfeh,ehd->bfed', h, Wo) + bo
        return jnp.einsum('bfed,fe->bfd', y, w)

    def _L3_gnn_ref(x, edge_index, W0, as0, ad0, b0, W1, as1, ad1, b1, W2, as2, ad2, b2):
        import jax, jax.numpy as jnp
        import numpy as np
        N_NODES = 50000
        N_EDGES = 25000
        NEG_SLOPE = 0.2

        def gat_conv(x, W, att_src, att_dst, bias, src, dst, heads, out_ch, concat):
            n = x.shape[0]
            xh = (x @ W).reshape(n, heads, out_ch)
            a_s = jnp.einsum('nhc,hc->nh', xh, att_src)
            a_d = jnp.einsum('nhc,hc->nh', xh, att_dst)
            e = a_s[src] + a_d[dst]
            e = jnp.where(e > 0, e, NEG_SLOPE * e)
            m = jax.ops.segment_max(e, dst, num_segments=n)
            e = jnp.exp(e - m[dst])
            denom = jax.ops.segment_sum(e, dst, num_segments=n)
            alpha = e / (denom[dst] + 1e-16)
            msg = xh[src] * alpha[:, :, None]
            out = jax.ops.segment_sum(msg, dst, num_segments=n)
            out = out.reshape(n, heads * out_ch) if concat else out.mean(axis=1)
            return out + bias
        loops = jnp.arange(x.shape[0], dtype=edge_index.dtype)
        src = jnp.concatenate([edge_index[0], loops])
        dst = jnp.concatenate([edge_index[1], loops])
        h = jax.nn.elu(gat_conv(x, W0, as0, ad0, b0, src, dst, 4, 64, True))
        h = jax.nn.elu(gat_conv(h, W1, as1, ad1, b1, src, dst, 4, 64, True))
        return gat_conv(h, W2, as2, ad2, b2, src, dst, 1, 256, False)

    def _L3_ffn_ref(x, W_gat, att_src, att_dst, b_gat, ln_gamma, ln_beta, W1, b1, W2, b2, edge_index):
        import jax, jax.numpy as jnp
        import numpy as np
        B, N, D = (16, 128, 256)
        NUM_EXPERTS, TOP_K, HEADS = (4, 2, 4)
        N_EDGES = 32768
        LN_EPS = 1e-05

        def _layernorm(x, g, b):
            mu = x.mean(-1, keepdims=True)
            var = ((x - mu) ** 2).mean(-1, keepdims=True)
            return (x - mu) * jax.lax.rsqrt(var + LN_EPS) * g + b

        def _forward(x, edge_index, W_gat, att_src, att_dst, b_gat, ln_gamma, ln_beta, W1, b1, W2, b2):
            Bc, Nc, Dc = x.shape
            M = Bc * Nc
            x_flat = x.reshape(M, Dc)
            h = (x_flat @ W_gat).reshape(M, HEADS, NUM_EXPERTS)
            loops = jnp.arange(M, dtype=edge_index.dtype)
            src = jnp.concatenate([edge_index[0], loops])
            dst = jnp.concatenate([edge_index[1], loops])
            a_src = (h * att_src).sum(-1)
            a_dst = (h * att_dst).sum(-1)
            e = jax.nn.leaky_relu(a_src[src] + a_dst[dst], negative_slope=0.2)
            e_max = jax.ops.segment_max(e, dst, num_segments=M)
            ee = jnp.exp(e - e_max[dst])
            denom = jax.ops.segment_sum(ee, dst, num_segments=M)
            alpha = ee / (denom[dst] + 1e-16)
            msg = h[src] * alpha[:, :, None]
            agg = jax.ops.segment_sum(msg, dst, num_segments=M).reshape(M, HEADS * NUM_EXPERTS) + b_gat
            scores = _layernorm(agg, ln_gamma, ln_beta).reshape(M, HEADS, NUM_EXPERTS).mean(1)
            scores = scores.reshape(Bc, Nc, NUM_EXPERTS)
            topk_s, topk_i = jax.lax.top_k(scores, TOP_K)
            w = jax.nn.softmax(topk_s, axis=-1)
            out = jnp.zeros_like(x)
            for ei in range(NUM_EXPERTS):
                g = jnp.where(topk_i == ei, w, 0.0).sum(-1)
                hh = jax.nn.gelu(x @ W1[ei] + b1[ei], approximate=False)
                out = out + g[..., None] * (hh @ W2[ei] + b2[ei])
            return out
        return _forward(x, edge_index, W_gat, att_src, att_dst, b_gat, ln_gamma, ln_beta, W1, b1, W2, b2)
    edge_index = jnp.stack([src, dst])
    x = x + _L0_gnn_ref(_layernorm(x, axis=-1), L0_gnn_W, L0_gnn_b, src, dst)
    x = x + _L0_ffn_ref(_layernorm(x, axis=-1)[None], L0_ffn_gate_w, L0_ffn_gate_b, L0_ffn_w1, L0_ffn_b1, L0_ffn_w2, L0_ffn_b2, L0_ffn_gamma, L0_ffn_beta)[0]
    x = x + _L1_gnn_ref(_layernorm(x, axis=-1), edge_index, edge_weight, L1_gnn_W, L1_gnn_b, L1_gnn_W1, L1_gnn_b1, L1_gnn_W2, L1_gnn_b2)
    x = x + _L1_ffn_ref(_layernorm(x, axis=-1)[None], L1_ffn_Wg, L1_ffn_bg, L1_ffn_bias, L1_ffn_W1, L1_ffn_b1, L1_ffn_W2, L1_ffn_b2)[0]
    x = x + _L2_gnn_ref(_layernorm(x, axis=-1), node_type_4, src, dst, edge_type_8, L2_gnn_Wk, L2_gnn_bk, L2_gnn_Wq, L2_gnn_bq, L2_gnn_Wv, L2_gnn_bv, L2_gnn_Wa, L2_gnn_ba, L2_gnn_rel_att, L2_gnn_rel_msg, L2_gnn_rel_pri, L2_gnn_skip)
    x = x + _L2_ffn_ref(_layernorm(x, axis=-1)[None], L2_ffn_Wr, L2_ffn_br, L2_ffn_W1, L2_ffn_b1, L2_ffn_g1, L2_ffn_be1, L2_ffn_m1, L2_ffn_v1, L2_ffn_W2, L2_ffn_b2, L2_ffn_g2, L2_ffn_be2, L2_ffn_m2, L2_ffn_v2, L2_ffn_Wo, L2_ffn_bo)[0]
    x = x + _L3_gnn_ref(_layernorm(x, axis=-1), edge_index, L3_gnn_W0, L3_gnn_as0, L3_gnn_ad0, L3_gnn_b0, L3_gnn_W1, L3_gnn_as1, L3_gnn_ad1, L3_gnn_b1, L3_gnn_W2, L3_gnn_as2, L3_gnn_ad2, L3_gnn_b2)
    x = x + _L3_ffn_ref(_layernorm(x, axis=-1)[None], L3_ffn_W_gat, L3_ffn_att_src, L3_ffn_att_dst, L3_ffn_b_gat, L3_ffn_ln_gamma, L3_ffn_ln_beta, L3_ffn_W1, L3_ffn_b1, L3_ffn_W2, L3_ffn_b2, L3_ffn_edge_index)[0]
    return x

_drawn_inputs = setup_inputs


def setup_inputs(seed=0):
    import zlib

    import numpy as np

    out = dict(_drawn_inputs(seed))
    spreads = {'L0_ffn_gate_b': (0.0, 0.1),
     'L0_ffn_b1': (0.0, 0.452),
     'L0_ffn_b2': (0.0, 0.1),
     'L0_ffn_gamma': (1.0, 0.2),
     'L0_ffn_beta': (0.0, 0.1),
     'L1_gnn_b': (0.0, 0.1),
     'L1_gnn_b1': (0.0, 0.1),
     'L1_gnn_b2': (0.0, 0.1),
     'L1_ffn_bias': (0.0, 0.413),
     'L2_gnn_bk': (0.0, 0.8),
     'L2_gnn_bq': (0.0, 0.8),
     'L2_gnn_bv': (0.0, 0.527),
     'L2_gnn_ba': (0.0, 0.1),
     'L2_gnn_rel_pri': (1.0, 0.6),
     'L2_gnn_skip': (1.0, 0.6),
     'L2_ffn_br': (0.0, 0.55),
     'L2_ffn_b1': (0.0, 0.49),
     'L2_ffn_g1': (1.0, 0.6),
     'L2_ffn_be1': (0.0, 0.527),
     'L2_ffn_m1': (0.0, 0.438),
     'L2_ffn_v1': (1.0, 0.6),
     'L2_ffn_b2': (0.0, 0.407),
     'L2_ffn_g2': (1.0, 0.2),
     'L2_ffn_be2': (0.0, 0.35),
     'L2_ffn_m2': (0.0, 0.352),
     'L2_ffn_v2': (1.0, 0.6),
     'L2_ffn_bo': (0.0, 0.268),
     'L3_gnn_b0': (0.0, 0.273),
     'L3_gnn_b1': (0.0, 0.1),
     'L3_gnn_b2': (0.0, 0.1),
     'L3_ffn_b_gat': (0.0, 0.1),
     'L3_ffn_ln_gamma': (1.0, 0.2),
     'L3_ffn_ln_beta': (0.0, 0.297),
     'L3_ffn_b1': (0.0, 0.354),
     'L3_ffn_b2': (0.0, 0.1)}
    factors = {'L0_gnn_b': 6.946,
     'L1_ffn_bg': 6.39,
     'L1_ffn_b1': 8.0,
     'L1_ffn_b2': 6.191,
     'L3_gnn_as0': 8.0,
     'L3_gnn_ad0': 61.107,
     'L3_gnn_as1': 29.061,
     'L3_gnn_ad1': 64.0,
     'L3_gnn_as2': 47.747,
     'L3_gnn_ad2': 64.0,
     'L3_ffn_att_src': 3.308,
     'L3_ffn_att_dst': 4.751}
    for name, (base, spread) in spreads.items():
        noise = np.random.default_rng([zlib.crc32(name.encode()), seed]).standard_normal(out[name].shape)
        drawn = base * np.exp(spread * noise) if base else spread * noise
        out[name] = jnp.asarray(drawn.astype(out[name].dtype))
    for name, factor in factors.items():
        out[name] = (out[name] * factor).astype(out[name].dtype)
    return out
```

```python
from contextlib import ExitStack

import numpy as np

import concourse.bass as bass
from concourse import mybir

P = 128
N = 3125
D = 256
TILES = (N + P - 1) // P
NP = TILES * P
LAST = N - (TILES - 1) * P
KC = D // P
CHUNK = 512
CHUNKS = [(c, min(CHUNK, NP - c)) for c in range(0, NP, CHUNK)]

F32 = mybir.dt.float32
BF16 = mybir.dt.bfloat16
I32 = mybir.dt.int32
ALU = mybir.AluOpType
ACT = mybir.ActivationFunctionType
AX = mybir.AxisListType.X
LN_EPS = 1e-5


class Chain:

    def __init__(self, eng, sem, base=0):
        self.eng, self.sem, self.n = eng, sem, base

    def __call__(self, instruction):
        instruction.then_inc(self.sem, 1)
        self.n = self.n + 1
        self.eng.wait_ge(self.sem, self.n)

    def mark(self, instruction):
        instruction.then_inc(self.sem, 1)
        self.n = self.n + 1

    def settle(self):
        self.eng.wait_ge(self.sem, self.n)


class Semaphores:

    MOST = 100

    def __init__(self):
        self.held, self.stack, self.kept = [], ExitStack(), ExitStack()

    def take(self, nc, ctx, stage, begins=True):
        if begins and len(self.held) > self.MOST:
            self.clear(nc)

        def sem(name, pool_dma=False):
            if pool_dma:
                return self.kept.enter_context(nc.semaphore(f"{stage}_{name}"))
            self.held.append(self.stack.enter_context(nc.semaphore(f"{stage}_{name}")))
            return self.held[-1]

        return sem

    def clear(self, nc):
        held = sorted(s.num for s in self.held)
        with nc.Block() as block:

            @block.sync
            def _(sp):
                at = 0
                for n in range(1, len(held) + 1):
                    if n == len(held) or held[n] != held[n - 1] + 1:
                        sp.sem_clear(range(held[at], held[n - 1] + 1))
                        at = n
        self.stack.close()
        self.held = []


SEMAPHORES = Semaphores()


class State:

    def __init__(self, nc, ctx, dram):
        self.nc, self.dram = nc, dram
        sb = lambda name, shape, dt=F32: ctx.enter_context(nc.sbuf_tensor(name, shape, dt))
        self.x = sb("residual", [P, TILES, D])
        self.a = sb("nodes_a", [P, TILES, D])
        self.aT = sb("nodes_transposed", [P, KC, NP])
        self.b_flat = sb("nodes_b", [P, TILES * (D + 4)])
        self.b = self.b_flat[:, 0:TILES * D].rearrange("p (t d) -> p t d", d=D)
        self.ident = sb("identity", [P, P])
        self.ones_row = sb("ones_row", [1, CHUNK])
        self.deg_out = sb("out_degree", [P, TILES])
        self.deg_in = sb("in_degree", [P, TILES])
        self.deg_weight = sb("out_weight", [P, TILES])
        self.node_type = sb("node_type", [P, TILES])


def tools(nc, ctx, stage):
    sb = lambda name, shape, dt=F32: ctx.enter_context(nc.sbuf_tensor(f"{stage}_{name}", shape, dt))
    ps = lambda name, shape, dt=F32: ctx.enter_context(nc.psum_tensor(f"{stage}_{name}", shape, dt))
    sem = SEMAPHORES.take(nc, ctx, stage)
    return sb, ps, sem


def load_nodes(nc, st, stage, x):
    with ExitStack() as ctx:
        sb, ps, sem = tools(nc, ctx, stage)
        cleared, loaded, ident_ready = sem("cleared"), sem("loaded"), sem("ident_ready")
        with nc.Block() as block:

            @block.vector
            def _(dve):
                nc.vector.memset(st.x[:, TILES - 1, :], 0.0).then_inc(cleared, 1)
                nc.vector.memset(st.ones_row[:, :], 1.0).then_inc(cleared, 1)

            @block.sync
            def _(sp):
                full = N - LAST
                sp.dma_start(st.x[:, 0:TILES - 1, :], x[0:full, :].rearrange("(t p) f -> p t f", p=P)).then_inc(loaded, 16)
                sp.wait_ge(cleared, 2)
                sp.dma_start(st.x[0:LAST, TILES - 1, :], x[full:N, :]).then_inc(loaded, 16)
                sp.wait_ge(loaded, 32)

            @block.gpsimd
            def _(pool):
                nc.gpsimd.memset(st.ident[:, :], 0.0).then_inc(ident_ready, 1)
                pool.wait_ge(ident_ready, 1)
                nc.gpsimd.affine_select(out=st.ident[:, :], in_=st.ident[:, :], compare_op=ALU.not_equal, fill=1.0,
                                        base=0, pattern=[[-1, P]], channel_multiplier=1).then_inc(ident_ready, 1)
                pool.wait_ge(ident_ready, 2)


def store_nodes(nc, st, stage, out):
    with ExitStack() as ctx:
        sb, ps, sem = tools(nc, ctx, stage)
        stored = sem("stored")
        with nc.Block() as block:

            @block.sync
            def _(sp):
                full = N - LAST
                sp.dma_start(out[0:full, :].rearrange("(t p) f -> p t f", p=P), st.x[:, 0:TILES - 1, :]).then_inc(stored, 16)
                sp.dma_start(out[full:N, :], st.x[0:LAST, TILES - 1, :]).then_inc(stored, 16)
                sp.wait_ge(stored, 32)


def norm_nodes(nc, st, stage, src, dst, transpose, scale=None):
    with ExitStack() as ctx:
        sb, ps, sem = tools(nc, ctx, stage)
        stats = sb("stats", [P, TILES, 6])
        moments = sb("moments", [P, TILES, 2])
        rstd = sb("rstd", [P, TILES])
        factor = sb("factor", [P, TILES])
        turned = ps("turned", [P, 4, 4, P])
        chain, normed, transposed, copied = sem("chain"), sem("normed"), sem("transposed"), sem("copied")
        moments_ready, rooted = sem("moments_ready"), sem("rooted")
        with nc.Block() as block:

            @block.vector
            def _(dve):
                link = Chain(dve, chain)
                for t in range(TILES):
                    link.mark(nc.vector.bn_stats(stats[:, t, :], src[:, t, :]))
                link.settle()
                for t in range(TILES):
                    link.mark(nc.vector.bn_aggr(moments[:, t, :], stats[:, t, :]))
                link.settle()
                nc.vector.tensor_scalar(rstd[:, :], moments[:, :, 1], LN_EPS, None, ALU.add).then_inc(moments_ready, 1)
                if scale is not None:
                    nc.vector.tensor_scalar(factor[:, :], scale[:, :], 1.0, None, ALU.max).then_inc(moments_ready, 1)
                dve.wait_ge(rooted, 2 if scale is not None else 1)
                link(nc.vector.reciprocal(rstd[:, :], rstd[:, :]))
                if scale is not None:
                    link(nc.vector.reciprocal(factor[:, :], factor[:, :]))
                    link(nc.vector.tensor_tensor(rstd[:, :], rstd[:, :], factor[:, :], ALU.mult))
                for t in range(TILES):
                    nc.vector.tensor_scalar(dst[:, t, :], src[:, t, :], moments[:, t, 0:1], rstd[:, t:t + 1],
                                            ALU.subtract, ALU.mult).then_inc(normed, 1)

            if transpose:
                @block.tensor
                def _(pe):
                    for t in range(TILES):
                        pe.wait_ge(normed, t + 1)
                        if t >= 4:
                            pe.wait_ge(copied, t - 3)
                        for c in range(KC):
                            last = nc.tensor.transpose(turned[:, t % 4, c, :], dst[:, t, c * P:(c + 1) * P], st.ident[:, :])
                        last.then_inc(transposed, 1)

            @block.scalar
            def _(act):
                act.wait_ge(moments_ready, 1)
                nc.scalar.activation(rstd[:, :], rstd[:, :], ACT.Sqrt).then_inc(rooted, 1)
                if scale is not None:
                    act.wait_ge(moments_ready, 2)
                    nc.scalar.activation(factor[:, :], factor[:, :], ACT.Sqrt).then_inc(rooted, 1)
                if transpose:
                    for t in range(TILES):
                        act.wait_ge(transposed, t + 1)
                        nc.scalar.copy(st.aT[:, :, t * P:(t + 1) * P], turned[:, t % 4, 0:KC, :]).then_inc(copied, 1)


def transpose_nodes(nc, st, stage, src):
    with ExitStack() as ctx:
        sb, ps, sem = tools(nc, ctx, stage)
        turned = ps("turned", [P, 4, 4, P])
        transposed, copied_by_act, copied_by_dve = sem("transposed"), sem("copied_by_act"), sem("copied_by_dve")
        with nc.Block() as block:

            @block.tensor
            def _(pe):
                for t in range(TILES):
                    if t >= 4:
                        pe.wait_ge((copied_by_act, copied_by_dve)[t % 2], (t - 4) // 2 + 1)
                    for c in range(KC):
                        last = nc.tensor.transpose(turned[:, t % 4, c, :], src[:, t, c * P:(c + 1) * P], st.ident[:, :])
                    last.then_inc(transposed, 1)

            @block.scalar
            def _(act):
                for t in range(0, TILES, 2):
                    act.wait_ge(transposed, t + 1)
                    nc.scalar.copy(st.aT[:, :, t * P:(t + 1) * P], turned[:, t % 4, 0:KC, :]).then_inc(copied_by_act, 1)

            @block.vector
            def _(dve):
                for t in range(1, TILES, 2):
                    dve.wait_ge(transposed, t + 1)
                    nc.vector.tensor_copy(st.aT[:, :, t * P:(t + 1) * P], turned[:, t % 4, 0:KC, :]).then_inc(copied_by_dve, 1)


def linear_nodes(nc, st, stage, weight, bias, width, finish):
    with ExitStack() as ctx:
        sb, ps, sem = tools(nc, ctx, stage)
        w = sb("weight", [P, KC, width])
        b = sb("bias", [1, width]) if bias is not None else None
        acc = ps("acc", [P, 4, CHUNK])
        loaded, chain, multiplied, finished = sem("loaded"), sem("chain"), sem("multiplied"), sem("finished")
        extra = finish.prepare(nc, ctx, stage) if hasattr(finish, "prepare") else None
        with nc.Block() as block:

            @block.sync
            def _(sp):
                sp.dma_start(w[:, :, :], weight.rearrange("(c p) m -> p c m", p=P)).then_inc(loaded, 16)
                if b is not None:
                    sp.dma_start(b[0:1, :], bias.rearrange("(o m) -> o m", o=1)).then_inc(loaded, 16)

            @block.tensor
            def _(pe):
                pe.wait_ge(loaded, 16 if b is None else 32)
                for t in range(TILES):
                    if t >= 4:
                        pe.wait_ge(finished, t - 3)
                    for c in range(KC):
                        last = nc.tensor.matmul(acc[:, t % 4, 0:width], st.aT[:, c, t * P:(t + 1) * P], w[:, c, :],
                                                start=(c == 0), stop=(b is None and c == KC - 1))
                    if b is not None:
                        last = nc.tensor.matmul(acc[:, t % 4, 0:width], st.ones_row[0:1, 0:P], b[0:1, :],
                                                start=False, stop=True)
                    last.then_inc(multiplied, 1)

            @block.vector
            def _(dve):
                link = Chain(dve, chain)
                for t in range(TILES):
                    dve.wait_ge(multiplied, t + 1)
                    finish(nc, link, t, acc[:, t % 4, 0:width], extra).then_inc(finished, 1)


def route_top2(nc, link, v, experts, logits, gates):
    shape = [P, TILES, experts]
    wide = lambda a: a.unsqueeze(2).to_broadcast(shape)
    top1, top2, m, hot1, hot2, work, rank = v
    link(nc.vector.tensor_reduce(top1[:, :], logits[:, :, :], AX, ALU.max))
    source, top = logits, top1
    for hot in (hot1, hot2):
        link(nc.vector.tensor_tensor(work[:, :, :], source[:, :, :], wide(top[:, :]), ALU.is_equal))
        link(nc.vector.tensor_tensor(work[:, :, :], work[:, :, :], rank[:, :, :], ALU.mult))
        link(nc.vector.tensor_reduce(m[:, :], work[:, :, :], AX, ALU.max))
        link(nc.vector.tensor_tensor(hot[:, :, :], work[:, :, :], wide(m[:, :]), ALU.is_equal))
        if hot is hot1:
            link(nc.vector.scalar_tensor_tensor(out=gates[:, :, :], in0=hot1[:, :, :], scalar=-3e38,
                                                in1=logits[:, :, :], op0=ALU.mult, op1=ALU.add))
            link(nc.vector.tensor_reduce(top2[:, :], gates[:, :, :], AX, ALU.max))
            source, top = gates, top2
    link(nc.vector.tensor_tensor(top2[:, :], top2[:, :], top1[:, :], ALU.subtract))


class Experts:

    def __init__(self, experts, hidden, router, router_bias, layers, w_out, b_out, top2, func, norms=None, router_bias2=None):
        self.experts, self.hidden, self.router, self.router_bias = experts, hidden, router, router_bias
        self.layers, self.w_out, self.b_out, self.top2, self.func = layers, w_out, b_out, top2, func
        self.norms, self.router_bias2 = norms, router_bias2


def gate_nodes(nc, st, stage, ex, gates, given=None):
    E = ex.experts
    with ExitStack() as ctx:
        sb, ps, sem = tools(nc, ctx, stage)
        w = sb("router", [P, KC, E])
        b = sb("router_bias", [1, 2, E])
        logits = sb("logits", [P, TILES, E])
        g = sb("g", [P, TILES, E])
        v = [sb(n, [P, TILES]) for n in ("top1", "top2", "m")]
        v += [sb(n, [P, TILES, E]) for n in ("hot1", "hot2", "work", "rank")]
        ranks = sb("ranks", [P, E], I32)
        acc = ps("acc", [P, 512])
        acc3 = acc[:, 0:TILES * E].rearrange("p (t e) -> p t e", e=E)
        loaded, chain, multiplied, ranked, shifted, exped = (
            sem(n) for n in ("loaded", "chain", "multiplied", "ranked", "shifted", "exped"))
        biases = [] if given is not None else [ex.router_bias] + ([ex.router_bias2] if ex.router_bias2 is not None else [])
        with nc.Block() as block:

            @block.sync
            def _(sp):
                if given is not None:
                    return
                sp.dma_start(w[:, :, :], ex.router.rearrange("(c p) m -> p c m", p=P)).then_inc(loaded, 16)
                for k, bias in enumerate(biases):
                    sp.dma_start(b[0:1, k, :], bias.rearrange("(o m) -> o m", o=1)).then_inc(loaded, 16)

            @block.gpsimd
            def _(pool):
                nc.gpsimd.iota(ranks[:, :], pattern=[[-1, E]], base=E, channel_multiplier=0).then_inc(ranked, 1)

            @block.tensor
            def _(pe):
                if given is not None:
                    return
                pe.wait_ge(loaded, 16 * (1 + len(biases)))
                for t in range(TILES):
                    for c in range(KC):
                        nc.tensor.matmul(acc3[:, t, :], st.aT[:, c, t * P:(t + 1) * P], w[:, c, :],
                                         start=(c == 0), stop=False)
                    for k in range(len(biases)):
                        last = nc.tensor.matmul(acc3[:, t, :], st.ones_row[0:1, 0:P], b[0:1, k, :],
                                                start=False, stop=(k == len(biases) - 1))
                last.then_inc(multiplied, 1)

            @block.scalar
            def _(act):
                act.wait_ge(shifted, 1)
                if ex.top2:
                    nc.scalar.activation(v[1][:, :], v[1][:, :], ACT.Exp).then_inc(exped, 1)
                else:
                    nc.scalar.activation(g[:, :, :], g[:, :, :], ACT.Exp).then_inc(exped, 1)

            @block.vector
            def _(dve):
                link = Chain(dve, chain)
                wide = lambda a: a.unsqueeze(2).to_broadcast([P, TILES, E])
                top1, top2, m, hot1, hot2, work, rank = v
                dve.wait_ge(ranked, 1)
                link(nc.vector.tensor_copy(rank[:, :, :], ranks[:, :].unsqueeze(1).to_broadcast([P, TILES, E])))
                if given is None:
                    dve.wait_ge(multiplied, 1)
                link(nc.vector.tensor_copy(logits[:, :, :], acc3 if given is None else given[:, :, :]))
                if ex.top2:
                    route_top2(nc, link, v, E, logits, g)
                    nc.vector.tensor_copy(m[:, :], m[:, :]).then_inc(shifted, 1)
                    dve.wait_ge(exped, 1)
                    link(nc.vector.tensor_scalar(m[:, :], top2[:, :], 1.0, None, ALU.add))
                    link(nc.vector.reciprocal(m[:, :], m[:, :]))
                    link(nc.vector.tensor_tensor(hot2[:, :, :], hot2[:, :, :], wide(top2[:, :]), ALU.mult))
                    link(nc.vector.tensor_tensor(hot1[:, :, :], hot1[:, :, :], hot2[:, :, :], ALU.add))
                    link(nc.vector.tensor_tensor(gates[:, :, :].rearrange("p e t -> p t e"), hot1[:, :, :], wide(m[:, :]), ALU.mult))
                else:
                    link(nc.vector.tensor_reduce(m[:, :], logits[:, :, :], AX, ALU.max))
                    nc.vector.tensor_tensor(g[:, :, :], logits[:, :, :], wide(m[:, :]), ALU.subtract).then_inc(shifted, 1)
                    dve.wait_ge(exped, 1)
                    link(nc.vector.tensor_reduce(m[:, :], g[:, :, :], AX, ALU.add))
                    link(nc.vector.reciprocal(m[:, :], m[:, :]))
                    link(nc.vector.tensor_tensor(gates[:, :, :].rearrange("p e t -> p t e"), g[:, :, :], wide(m[:, :]), ALU.mult))


def mix_experts(nc, st, stage, ex, gates, acc):
    E, H = ex.experts, ex.hidden
    HC = H // P
    L = len(ex.layers)
    with ExitStack() as ctx:
        sb, ps, sem = tools(nc, ctx, stage)
        w_first = sb("w_first", [P, 2, KC, H])
        w_mid = sb("w_mid", [P, 2, HC, H]) if L == 2 else None
        w_last = sb("w_last", [P, 2, HC, D])
        b_hidden = sb("b_hidden", [P, 2, L, HC])
        bn = sb("bn", [P, L, 5, E, HC]) if ex.norms else None
        scale_all = sb("scale_all", [P, L, E, HC]) if ex.norms else None
        shift_all = sb("shift_all", [P, L, E, HC]) if ex.norms else None
        bn_scale = sb("bn_scale", [P, 2, L, HC]) if ex.norms else None
        bn_shift = sb("bn_shift", [P, 2, L, HC]) if ex.norms else None
        b_last = sb("b_last", [E, D])
        gatesT = sb("gates_transposed", [E, NP])
        gate_now = sb("gate_now", [P, 2, TILES])
        hidden = sb("hidden", [P, 2, HC, CHUNK])
        hidden2 = sb("hidden2", [P, 2, HC, CHUNK]) if L == 2 else None
        pre = ps("pre", [P, 4, CHUNK])
        post = ps("post", [P, 4, CHUNK])
        loads = 2 + L + (1 if L == 2 else 0) 
        weights_loaded = [sem(f"weights_loaded{k}") for k in range(2)]
        bias_loaded, pre_ready, pre_used, post_ready, post_used, chain, act_chain, turned, gate_copied, bn_ready = (
            sem(n) for n in ("bias_loaded", "pre_ready", "pre_used", "post_ready", "post_used", "chain",
                             "act_chain", "turned", "gate_copied", "bn_ready"))
        bn_loaded, bn_rooted = sem("bn_loaded"), sem("bn_rooted")
        NC = len(CHUNKS)
        with nc.Block() as block:

            @block.sync
            def _(sp):
                sp.dma_start(b_last[:, :], ex.b_out).then_inc(bias_loaded, 16)
                if ex.norms:
                    for l in range(L):
                        for n, a in enumerate([*ex.norms[l], ex.layers[l][1]]):
                            sp.dma_start(bn[:, l, n, :, :], a.rearrange("e (p j) -> p e j", p=P)).then_inc(bn_loaded, 16)
                with sp.Fori(0, E // 2) as i:
                    for k in range(2):
                        sp.wait_ge(post_ready, (i * 2 + k) * TILES + 1)
                        e = i * 2 + k
                        one = lambda a: a[bass.ds(e, 1)]
                        sp.dma_start(w_first[:, k, :, :], one(ex.layers[0][0]).rearrange("o (c p) h -> p (o c) h", p=P)).then_inc(weights_loaded[k], 16)
                        sp.dma_start(w_last[:, k, :, :], one(ex.w_out).rearrange("o (p j) d -> p (o j) d", p=P)).then_inc(weights_loaded[k], 16)
                        for l in range(L):
                            sp.dma_start(b_hidden[:, k, l, :], one(ex.layers[l][1]).rearrange("o (p j) -> p (o j)", p=P)).then_inc(weights_loaded[k], 16)
                        if L == 2:
                            sp.dma_start(w_mid[:, k, :, :], one(ex.layers[1][0]).rearrange("o (p j) h -> p (o j) h", p=P)).then_inc(weights_loaded[k], 16)

            @block.tensor
            def _(pe):
                for t in range(TILES):
                    if t >= 4:
                        pe.wait_ge(post_used, t - 3)
                    nc.tensor.transpose(post[0:E, t % 4, 0:P], gates[:, :, t], st.ident[:, :]).then_inc(turned, 1)
                pe.wait_ge(bias_loaded, 16)
                pe.wait_ge(post_used, TILES)
                for t in range(TILES):
                    if t >= 4:
                        pe.wait_ge(post_used, TILES + t - 3)
                    nc.tensor.matmul(post[:, t % 4, 0:D], gatesT[:, t * P:(t + 1) * P], b_last[:, :],
                                     start=True, stop=True).then_inc(post_ready, 1)
                pe.wait_ge(post_used, 2 * TILES)
                pre_per, post_per = L * HC * NC, TILES
                with pe.Fori(0, E // 2) as i:
                    for k in range(2):
                        e = i * 2 + k
                        pe.wait_ge(weights_loaded[k], i * 16 * loads + 16 * loads)
                        n_pre = n_post = 0
                        for q, (at, n) in enumerate(CHUNKS):
                            for l in range(L):
                                src = (lambda c: st.aT[:, c, at:at + n]) if l == 0 else (lambda c: hidden[:, q % 2, c, 0:n])
                                w = w_first if l == 0 else w_mid
                                if l == 1:
                                    pe.wait_ge(pre_used, e * pre_per + 4 + n_pre)
                                for j in range(HC):
                                    pe.wait_ge(pre_used, e * pre_per + n_pre + 1)
                                    C = KC if l == 0 else HC
                                    for c in range(C):
                                        last = nc.tensor.matmul(pre[:, n_pre % 4, 0:n], w[:, k, c, j:H:HC], src(c),
                                                                start=(c == 0), stop=(c == C - 1))
                                    last.then_inc(pre_ready, 1)
                                    n_pre += 1
                            pe.wait_ge(pre_used, e * pre_per + 4 + n_pre)
                            top = hidden if L == 1 else hidden2
                            for t in range(at // P, (at + n) // P):
                                pe.wait_ge(post_used, e * post_per + 2 * TILES + (t - 3 if t >= 4 else 0))
                                o = t * P - at
                                for j in range(HC):
                                    last = nc.tensor.matmul(post[:, t % 4, 0:D], top[:, q % 2, j, o:o + P], w_last[:, k, j, :],
                                                            start=(j == 0), stop=(j == HC - 1))
                                last.then_inc(post_ready, 1)

            @block.scalar
            def _(act):
                if ex.norms:
                    act.wait_ge(bn_ready, 1)
                    nc.scalar.activation(scale_all[:, :, :, :], scale_all[:, :, :, :], ACT.Sqrt).then_inc(bn_rooted, 1)
                act.sem_inc(pre_used, 4)
                pre_per = L * HC * NC
                with act.Fori(0, E // 2) as i:
                    for k in range(2):
                        e = i * 2 + k
                        act.wait_ge(weights_loaded[k], i * 16 * loads + 16 * loads)
                        if ex.norms:
                            act.wait_ge(bn_ready, e + 2)
                        n_pre = 0
                        for q, (at, n) in enumerate(CHUNKS):
                            for l in range(L):
                                out = hidden if l == 0 else hidden2
                                done = CHUNKS[q - 2][0] // P + CHUNKS[q - 2][1] // P if q >= 2 else 0
                                act.wait_ge(post_ready, e * TILES + TILES + done)
                                act.wait_ge(pre_used, e * pre_per + 4 + n_pre)
                                for j in range(HC):
                                    act.wait_ge(pre_ready, e * pre_per + n_pre + 1)
                                    if ex.norms:
                                        bias, scale = bn_shift[:, k, l, j:j + 1], bn_scale[:, k, l, j:j + 1]
                                    else:
                                        bias, scale = b_hidden[:, k, l, j:j + 1], 1.0
                                    nc.scalar.activation(out[:, q % 2, j, 0:n], pre[:, n_pre % 4, 0:n], ex.func,
                                                         bias=bias, scale=scale).then_inc(pre_used, 1)
                                    n_pre += 1

            @block.vector
            def _(dve):
                link = Chain(dve, chain)
                for t in range(TILES):
                    dve.wait_ge(turned, t + 1)
                    nc.vector.tensor_copy(gatesT[:, t * P:(t + 1) * P], post[0:E, t % 4, 0:P]).then_inc(post_used, 1)
                for t in range(TILES):
                    dve.wait_ge(post_ready, t + 1)
                    nc.vector.tensor_tensor(acc[:, t, :], acc[:, t, :], post[:, t % 4, 0:D], ALU.add).then_inc(post_used, 1)
                if ex.norms:
                    dve.wait_ge(bn_loaded, 16 * 5 * L)
                    nc.vector.tensor_scalar(scale_all[:, :, :, :], bn[:, :, 3, :, :], 1e-3, None, ALU.add).then_inc(bn_ready, 1)
                    dve.wait_ge(bn_rooted, 1)
                    link(nc.vector.reciprocal(scale_all[:, :, :, :], scale_all[:, :, :, :]))
                    g, be, m, v, b = (bn[:, :, n, :, :] for n in range(5))
                    link(nc.vector.tensor_tensor(scale_all[:, :, :, :], scale_all[:, :, :, :], g, ALU.mult))
                    link(nc.vector.tensor_tensor(shift_all[:, :, :, :], b, m, ALU.subtract))
                    link(nc.vector.tensor_tensor(shift_all[:, :, :, :], shift_all[:, :, :, :], scale_all[:, :, :, :], ALU.mult))
                    link(nc.vector.tensor_tensor(shift_all[:, :, :, :], shift_all[:, :, :, :], be, ALU.add))
                with dve.Fori(0, E // 2) as i:
                    for k in range(2):
                        e = i * 2 + k
                        steps = Chain(dve, gate_copied, e * (3 if ex.norms else 1))
                        dve.wait_ge(post_used, e * TILES + 2 * TILES)
                        if ex.norms:
                            dve.wait_ge(post_ready, e * TILES + TILES)
                            steps(nc.vector.tensor_copy(bn_scale[:, k, :, :], scale_all[:, :, bass.ds(e, 1), :].rearrange("p l o j -> p l (o j)")))
                            steps(nc.vector.tensor_copy(bn_shift[:, k, :, :], shift_all[:, :, bass.ds(e, 1), :].rearrange("p l o j -> p l (o j)")))
                            dve.sem_inc(bn_ready, 1)
                        steps(nc.vector.tensor_copy(gate_now[:, k, :], gates[:, bass.ds(e, 1), :].rearrange("p o t -> p (o t)")))
                        for t in range(TILES):
                            dve.wait_ge(post_ready, e * TILES + TILES + t + 1)
                            nc.vector.scalar_tensor_tensor(out=acc[:, t, :], in0=post[:, t % 4, 0:D],
                                                           scalar=gate_now[:, k, t:t + 1], in1=acc[:, t, :],
                                                           op0=ALU.mult, op1=ALU.add).then_inc(post_used, 1)


def norm_add(nc, st, stage, gamma, beta):
    with ExitStack() as ctx:
        sb, ps, sem = tools(nc, ctx, stage)
        g, b = sb("gamma", [P, D]), sb("beta", [P, D])
        stats, moments, rstd = sb("stats", [P, TILES, 6]), sb("moments", [P, TILES, 2]), sb("rstd", [P, TILES])
        loaded, chain, moments_ready, rooted = sem("loaded"), sem("chain"), sem("moments_ready"), sem("rooted")
        with nc.Block() as block:

            @block.sync
            def _(sp):
                sp.dma_start(g[:, :], gamma.partition_broadcast(P)).then_inc(loaded, 16)
                sp.dma_start(b[:, :], beta.partition_broadcast(P)).then_inc(loaded, 16)

            @block.scalar
            def _(act):
                act.wait_ge(moments_ready, 1)
                nc.scalar.activation(rstd[:, :], rstd[:, :], ACT.Sqrt).then_inc(rooted, 1)

            @block.vector
            def _(dve):
                link = Chain(dve, chain)
                for t in range(TILES):
                    link.mark(nc.vector.bn_stats(stats[:, t, :], st.a[:, t, :]))
                link.settle()
                for t in range(TILES):
                    link.mark(nc.vector.bn_aggr(moments[:, t, :], stats[:, t, :]))
                link.settle()
                nc.vector.tensor_scalar(rstd[:, :], moments[:, :, 1], LN_EPS, None, ALU.add).then_inc(moments_ready, 1)
                dve.wait_ge(rooted, 1)
                link(nc.vector.reciprocal(rstd[:, :], rstd[:, :]))
                dve.wait_ge(loaded, 32)
                for t in range(TILES):
                    link.mark(nc.vector.tensor_scalar(st.a[:, t, :], st.a[:, t, :], moments[:, t, 0:1], rstd[:, t:t + 1], ALU.subtract, ALU.mult))
                link.settle()
                wide = lambda w: w[:, :].unsqueeze(1).to_broadcast([P, TILES, D])
                link(nc.vector.tensor_tensor(st.a[:, :, :], st.a[:, :, :], wide(g), ALU.mult))
                link(nc.vector.tensor_tensor(st.x[:, :, :], st.x[:, :, :], wide(b), ALU.add))
                link(nc.vector.tensor_tensor(st.x[:, :, :], st.x[:, :, :], st.a[:, :, :], ALU.add))



PITCH = NP
SPARE = (NP + 1) * NP + 256
CELLS = (NP + 2) * NP
FAR = -1e30


def edge_columns(edges):
    return (edges + P - 1) // P


def clear_tables(nc, stage, tables):
    with ExitStack() as ctx:
        sb, ps, sem = tools(nc, ctx, stage)
        run = CELLS // P // 10
        zeros = sb("zeros", [P, run])
        cleared, stored = sem("cleared"), sem("stored")
        with nc.Block() as block:

            @block.vector
            def _(dve):
                nc.vector.memset(zeros[:, :], 0.0).then_inc(cleared, 1)

            @block.sync
            def _(sp):
                sp.wait_ge(cleared, 1)
                n = 0
                for table in tables:
                    rows = table.rearrange("(p r) o -> p (r o)", p=P)
                    for k in range(10):
                        sp.dma_start(rows[:, k * run:(k + 1) * run], zeros[:, :]).then_inc(stored, 16)
                        n += 16
                sp.wait_ge(stored, n)


def build_tables(nc, st, stage, src, dst, weight, src2, dst2, count_table, weight_table, count_table2):
    edges, edges2 = src.shape[0], src2.shape[0]
    cols, cols2 = edge_columns(edges), edge_columns(edges2)
    assert cols % 2 == 0 and cols2 % 2 == 0 and cols2 <= cols
    graphs = [(edges, cols, src, dst), (edges2, cols2, src2, dst2)]
    with ExitStack() as ctx:
        sb, ps, sem = tools(nc, ctx, stage)
        raw = [[sb(f"raw{g}{n}", [P, c[1]], I32) for n in ("src", "dst")] for g, c in enumerate(graphs)]
        digit = sb("digit", [P, cols], I32)
        ends = [[sb(f"ends{g}{n}", [P, c[1]]) for n in ("src", "dst")] for g, c in enumerate(graphs)]
        keys = [sb("keys0", [P, 2, cols]), sb("keys1", [P, 1, cols2])]
        low = [sb(f"low{n}", [P, cols]) for n in ("src", "dst")]
        high = [sb(f"high{n}", [P, cols]) for n in ("src", "dst")]
        ew = sb("edge_weight", [P, cols])
        iota_i = sb("iota_i", [P, P], I32)
        iota_f = sb("iota_f", [P, P])
        spare_i = sb("spare_i", [P, 1], I32)
        spare = sb("spare", [P, 1])
        below = sb("below", [P, P])
        zeros = sb("zeros", [P, P])
        keycol = [sb(f"keycol{g}", [P, 2, 2]) for g in range(2)]
        addend = sb("addend", [P, 2, 2])
        same = [sb(f"same{g}", [P, 2, P]) for g in range(2)]
        repeated = [sb(f"repeated{g}", [P, 2, 2]) for g in range(2)]
        junk = sb("junk", [P, P])
        aside = [sb(f"aside{g}", [P, 2, 2]) for g in range(2)]
        cell = [sb(f"cell{g}", [P, 2, 2], I32) for g in range(2)]
        merged = [sb(f"merged{g}", [P, 2, 2]) for g in range(2)]
        hot_src = sb("hot_src", [P, 2, P])
        hot_dst = sb("hot_dst", [P, 2, P])
        hot_high = sb("hot_high", [P, 2, 3, TILES])
        keyrow = [ps(f"keyrow{g}", [P, 512]) for g in range(2)]
        sums = [ps(f"sums{g}", [P, 512]) for g in range(2)]
        hist_src = ps("hist_src", [P, 512])
        hist_dst = ps("hist_dst", [P, 512])
        loaded, chain, consts, iotas = sem("loaded"), sem("chain"), sem("consts"), sem("iotas")
        col_ready = [sem(f"col_ready{g}") for g in range(2)]
        row_ready = [sem(f"row_ready{g}") for g in range(2)]
        same_ready = [sem(f"same_ready{g}") for g in range(2)]
        sum_ready = [sem(f"sum_ready{g}") for g in range(2)]
        cell_ready = [sem(f"cell_ready{g}") for g in range(2)]
        merged_ready = [sem(f"merged_ready{g}") for g in range(2)]
        rep = [sem(f"repeats{g}") for g in range(2)]
        hots, weight_ready, hist_done = sem("hots"), sem("weight_ready"), sem("hist_done")
        tables = [[count_table, weight_table], [count_table2]]
        added = [[sem(f"added{g}{n}", pool_dma=True) for n in range(len(tables[g]))] for g in range(2)]
        tick = sem("tick")

        def loops(eng, body, between=None):
            half, half2 = cols // 2, cols2 // 2
            with eng.Fori(0, half2) as i:
                for k in range(2):
                    body(i * 2 + k, k, (0, 1))
            if half > half2:
                if between:
                    between()
                with eng.Fori(half2, half) as i:
                    for k in range(2):
                        body(i * 2 + k, k, (0,))

        with nc.Block() as block:

            @block.sync
            def _(sp):
                sp.wait_ge(consts, 6)
                for g, (count, c, *arrays) in enumerate(graphs):
                    full = count // c
                    for n, a in enumerate(arrays):
                        sp.dma_start(raw[g][n][0:full, :], a[0:full * c].rearrange("(p c) -> p c", c=c)).then_inc(loaded, 16)
                        if count > full * c:
                            rest = count - full * c
                            sp.dma_start(raw[g][n][full:full + 1, 0:rest], a[full * c:count].rearrange("(o c) -> o c", o=1)).then_inc(loaded, 16)
                full, rest = edges // cols, edges % cols
                sp.dma_start(ew[0:full, :], weight[0:full * cols].rearrange("(p c) -> p c", c=cols)).then_inc(loaded, 16)
                sp.dma_start(ew[full:full + 1, 0:rest], weight[full * cols:edges].rearrange("(o c) -> o c", o=1)).then_inc(loaded, 16)

            @block.gpsimd
            def _(pool):
                nc.gpsimd.iota(iota_i[:, :], pattern=[[1, P]], base=0, channel_multiplier=0).then_inc(iotas, 1)
                nc.gpsimd.iota(spare_i[:, :], pattern=[[0, 1]], base=SPARE, channel_multiplier=1).then_inc(iotas, 1)
                nc.gpsimd.memset(below[:, :], 1.0).then_inc(tick, 1)
                pool.wait_ge(tick, 1)
                nc.gpsimd.affine_select(out=below[:, :], in_=below[:, :], compare_op=ALU.is_gt, fill=0.0, base=0,
                                        pattern=[[-1, P]], channel_multiplier=1).then_inc(iotas, 1)
                pool.wait_ge(iotas, 3)
                pool.wait_ge(consts, 6)
                for g in range(2):
                    for n, table in enumerate(tables[g]):
                        for k in range(2):
                            if k:
                                pool.wait_ge(added[g][n], 16)
                            pool.indirect_dma_start(out=table, out_offset=bass.IndirectOffsetOnAxis(ap=spare_i[:, 0:1], axis=0),
                                                    in_=zeros[:, 0:1], in_offset=None, compute_op=ALU.add).then_inc(added[g][n], 16)

                def body(c, k, which):
                    for g in which:
                        pool.wait_ge(cell_ready[g], c + 1)
                        pool.wait_ge(merged_ready[g], c + 2)
                        for n, table in enumerate(tables[g]):
                            pool.wait_ge(added[g][n], c * 16 + 32)
                            pool.sem_inc(tick, 1)
                            pool.indirect_dma_start(out=table, out_offset=bass.IndirectOffsetOnAxis(ap=cell[g][:, k, n:n + 1], axis=0),
                                                    in_=merged[g][:, k, n:n + 1], in_offset=None, compute_op=ALU.add).then_inc(added[g][n], 16)

                loops(pool, body)
                for g in range(2):
                    for s in added[g]:
                        pool.wait_ge(s, 32 + 16 * graphs[g][1])

            @block.tensor
            def _(pe):
                pe.wait_ge(consts, 6)
                nc.tensor.matmul(hist_src[:, 0:2 * TILES], zeros[:, :], zeros[:, 0:2 * TILES], start=True, stop=False, skip_group_check=True).then_inc(hist_done, 1)
                nc.tensor.matmul(hist_dst[:, 0:TILES], zeros[:, :], zeros[:, 0:TILES], start=True, stop=False, skip_group_check=True).then_inc(hist_done, 1)

                def body(c, k, which):
                    for g in which:
                        pe.wait_ge(col_ready[g], c + 1)
                        pe.wait_ge(same_ready[g], c + 1)
                        nc.tensor.transpose(keyrow[g][:, 0:P], keycol[g][:, k, 0:1].to_broadcast([P, P]), st.ident[:, :]).then_inc(row_ready[g], 1)
                    for g in which:
                        pe.wait_ge(same_ready[g], c + 2)
                        if g == 0:
                            pe.wait_ge(weight_ready, c + 1)
                        pe.wait_ge(merged_ready[g], c + 1)
                        nc.tensor.matmul(sums[g][:, 0:2], same[g][:, k, :], addend[:, k, :], start=True, stop=True).then_inc(sum_ready[g], 1)
                    pe.wait_ge(hots, c * 5 + 5)
                    nc.tensor.matmul(hist_src[:, 0:2 * TILES], hot_src[:, k, :], hot_high[:, k, 0:2, :].rearrange("p a b -> p (a b)"),
                                     start=False, stop=False, skip_group_check=True)
                    nc.tensor.matmul(hist_dst[:, 0:TILES], hot_dst[:, k, :], hot_high[:, k, 2, :],
                                     start=False, stop=False, skip_group_check=True).then_inc(hist_done, 1)

                loops(pe, body)
                nc.tensor.matmul(hist_src[:, 0:2 * TILES], zeros[:, :], zeros[:, 0:2 * TILES], start=False, stop=True, skip_group_check=True)
                nc.tensor.matmul(hist_dst[:, 0:TILES], zeros[:, :], zeros[:, 0:TILES], start=False, stop=True, skip_group_check=True).then_inc(hist_done, 1)

            @block.scalar
            def _(act):
                for g in range(2):
                    act.sem_inc(merged_ready[g], 1)

                def body(c, k, which):
                    for g in which:
                        act.wait_ge(sum_ready[g], c + 1)
                        for s in added[g]:
                            act.wait_ge(s, c * 16 + 16)
                        nc.scalar.copy(merged[g][:, k, :], sums[g][:, 0:2]).then_inc(merged_ready[g], 1)

                loops(act, body)

            @block.vector
            def _(dve):
                link = Chain(dve, chain)
                nc.vector.memset(zeros[:, :], 0.0).then_inc(consts, 1)
                nc.vector.memset(ew[:, :], 0.0).then_inc(consts, 1)
                for g in range(2):
                    for n in range(2):
                        nc.vector.memset(raw[g][n][:, :], NP).then_inc(consts, 1)
                dve.wait_ge(iotas, 3)
                link.mark(nc.vector.memset(addend[:, :, :], 1.0))
                link.mark(nc.vector.tensor_copy(iota_f[:, :], iota_i[:, :]))
                link.mark(nc.vector.tensor_copy(spare[:, :], spare_i[:, :]))
                dve.wait_ge(loaded, 16 * (4 + 2 + 2 + (2 if edges2 % cols2 else 0)))
                for g in range(2):
                    for n in range(2):
                        link.mark(nc.vector.tensor_copy(ends[g][n][:, :], raw[g][n][:, :]))
                link.settle()
                for n in range(2):
                    link(nc.vector.tensor_single_scalar(digit[:, :], raw[0][n][:, :], P - 1, op=ALU.bitwise_and))
                    link(nc.vector.tensor_copy(low[n][:, :], digit[:, :]))
                    link(nc.vector.tensor_single_scalar(digit[:, :], raw[0][n][:, :], 7, op=ALU.logical_shift_right))
                    link(nc.vector.tensor_copy(high[n][:, :], digit[:, :]))
                for g, n in ((0, 0), (0, 1), (1, 0)):
                    link(nc.vector.scalar_tensor_tensor(out=keys[g][:, n, :], in0=ends[g][n][:, :], scalar=float(PITCH),
                                                        in1=ends[g][1 - n][:, :], op0=ALU.mult, op1=ALU.add))

                def body(c, k, which):
                    for g in which:
                        w = len(tables[g])
                        for s in added[g]:
                            dve.wait_ge(s, c * 16 + 16)
                        nc.vector.tensor_copy(keycol[g][:, k, 0:w], keys[g][:, :, bass.ds(c, 1)].rearrange("p n o -> p (n o)")).then_inc(col_ready[g], 1)
                    if 0 in which:
                        nc.vector.tensor_copy(addend[:, k, 1:2], ew[:, bass.ds(c, 1)]).then_inc(weight_ready, 1)
                    dve.wait_ge(hist_done, c + 1)
                    col = lambda a: a[:, bass.ds(c, 1)]
                    nc.vector.tensor_scalar(hot_src[:, k, :], iota_f[:, :], col(low[0]), None, ALU.is_equal).then_inc(hots, 1)
                    nc.vector.tensor_scalar(hot_dst[:, k, :], iota_f[:, :], col(low[1]), None, ALU.is_equal).then_inc(hots, 1)
                    nc.vector.tensor_scalar(hot_high[:, k, 0, :], iota_f[:, 0:TILES], col(high[0]), None, ALU.is_equal).then_inc(hots, 1)
                    nc.vector.tensor_scalar(hot_high[:, k, 1, :], iota_f[:, 0:TILES], col(high[0]), col(ew), ALU.is_equal, ALU.mult).then_inc(hots, 1)
                    nc.vector.tensor_scalar(hot_high[:, k, 2, :], iota_f[:, 0:TILES], col(high[1]), None, ALU.is_equal).then_inc(hots, 1)
                    for g in which:
                        w = len(tables[g])
                        dve.wait_ge(row_ready[g], c + 1)
                        nc.vector.tensor_scalar(same[g][:, k, :], keyrow[g][:, 0:P], keycol[g][:, k, 0:1], None, ALU.is_equal).then_inc(same_ready[g], 1)
                        dve.wait_ge(same_ready[g], c + 2)
                        nc.vector.tensor_tensor_reduce(junk[:, :], same[g][:, k, :], below[:, :], 1.0, 0.0, ALU.mult, ALU.add,
                                                       repeated[g][:, k, 0:1]).then_inc(rep[g], 1)
                        nc.vector.tensor_scalar(aside[g][:, k, 0:w], keycol[g][:, k, 0:w], -1.0, spare[:, 0:1], ALU.mult, ALU.add).then_inc(rep[g], 1)
                        dve.wait_ge(rep[g], c * 3 + 2)
                        nc.vector.tensor_scalar(repeated[g][:, k, 1:2], repeated[g][:, k, 0:1], 0.0, None, ALU.is_gt).then_inc(rep[g], 1)
                        dve.wait_ge(rep[g], c * 3 + 3)
                        nc.vector.scalar_tensor_tensor(out=cell[g][:, k, 0:w], in0=aside[g][:, k, 0:w], scalar=repeated[g][:, k, 1:2],
                                                       in1=keycol[g][:, k, 0:w], op0=ALU.mult, op1=ALU.add).then_inc(cell_ready[g], 1)

                def second_graph_done():
                    dve.wait_ge(added[1][0], 32 + 16 * cols2)

                for g in range(2):
                    dve.sem_inc(same_ready[g], 1)
                loops(dve, body, second_graph_done)
                dve.wait_ge(hist_done, cols + 3)
                nc.vector.tensor_copy(st.deg_out[:, :], hist_src[:, 0:TILES]).then_inc(chain, 1)
                nc.vector.tensor_copy(st.deg_weight[:, :], hist_src[:, TILES:2 * TILES]).then_inc(chain, 1)
                nc.vector.tensor_copy(st.deg_in[:, :], hist_dst[:, 0:TILES]).then_inc(chain, 1)


def build_masks(nc, st, stage, table, mask):
    view = table[0:NP * NP, :].rearrange("(c p d) o -> p c (d o)", p=P, d=NP)
    with ExitStack() as ctx:
        sb, ps, sem = tools(nc, ctx, stage)
        block_in = sb("block_in", [P, 3, TILES, P])
        block_out = sb("block_out", [P, 2, NP], BF16)
        off_diagonal = sb("off_diagonal", [P, P], BF16)
        turned = ps("turned", [P, 4, 512])
        loaded = [sem(f"loaded{k}") for k in range(3)]
        stored = [sem(f"stored{k}") for k in range(2)]
        transposed, compared, diagonal, const = sem("transposed"), sem("compared"), sem("diagonal"), sem("const")
        groups = [(c, min(4, TILES - c)) for c in range(0, TILES, 4)]
        G = len(groups)
        with nc.Block() as block:

            @block.sync
            def _(sp):
                for t in range(TILES):
                    if t >= 3:
                        sp.wait_ge(transposed, (t - 2) * G)
                    sp.dma_start(block_in[:, t % 3, :, :], view[:, :, t * P:(t + 1) * P]).then_inc(loaded[t % 3], 16)
                    if t >= 1:
                        sp.wait_ge(diagonal, t)
                        sp.dma_start(mask[(t - 1) * P:t * P, :], block_out[:, (t - 1) % 2, :]).then_inc(stored[(t - 1) % 2], 16)
                sp.wait_ge(diagonal, TILES)
                sp.dma_start(mask[(TILES - 1) * P:NP, :], block_out[:, (TILES - 1) % 2, :]).then_inc(stored[(TILES - 1) % 2], 16)
                sp.wait_ge(stored[0], 16 * ((TILES + 1) // 2))
                sp.wait_ge(stored[1], 16 * (TILES // 2))

            @block.tensor
            def _(pe):
                n = 0
                for t in range(TILES):
                    pe.wait_ge(loaded[t % 3], 16 * (t // 3 + 1))
                    for c, w in groups:
                        if n >= 4:
                            pe.wait_ge(compared, n - 3)
                        for j in range(w):
                            last = nc.tensor.transpose(turned[:, n % 4, j * P:(j + 1) * P], block_in[:, t % 3, c + j, :], st.ident[:, :])
                        last.then_inc(transposed, 1)
                        n += 1

            @block.vector
            def _(dve):
                nc.vector.tensor_scalar(off_diagonal[:, :], st.ident[:, :], -1.0, 1.0, ALU.mult, ALU.add).then_inc(const, 1)
                dve.wait_ge(const, 1)
                n = 0
                for t in range(TILES):
                    if t >= 2:
                        dve.wait_ge(stored[t % 2], 16 * (t // 2))
                    for c, w in groups:
                        dve.wait_ge(transposed, n + 1)
                        nc.vector.tensor_scalar(block_out[:, t % 2, c * P:(c + w) * P], turned[:, n % 4, 0:w * P], 0.0, FAR,
                                                ALU.is_equal, ALU.mult).then_inc(compared, 1)
                        n += 1
                    dve.wait_ge(compared, n)
                    own = block_out[:, t % 2, t * P:(t + 1) * P]
                    nc.vector.tensor_tensor(own, own, off_diagonal[:, :], ALU.mult).then_inc(diagonal, 1)




def degree_factors(nc, st, stage):
    with ExitStack() as ctx:
        sb, ps, sem = tools(nc, ctx, stage)
        positive = sb("positive", [P, TILES])
        chain, floored, rooted = sem("chain"), sem("floored"), sem("rooted")
        with nc.Block() as block:

            @block.vector
            def _(dve):
                link = Chain(dve, chain)
                link(nc.vector.tensor_scalar(st.deg_weight[:, :], st.deg_weight[:, :], 1.0, None, ALU.add))
                link(nc.vector.tensor_scalar(positive[:, :], st.deg_weight[:, :], 0.0, None, ALU.is_gt))
                nc.vector.tensor_scalar(st.deg_weight[:, :], st.deg_weight[:, :], 1e-30, None, ALU.max).then_inc(floored, 1)
                nc.vector.tensor_scalar(st.deg_in[:, :], st.deg_in[:, :], 1.0, None, ALU.max).then_inc(floored, 1)
                dve.wait_ge(rooted, 2)
                link.mark(nc.vector.reciprocal(st.deg_in[:, :], st.deg_in[:, :]))
                link(nc.vector.reciprocal(st.deg_weight[:, :], st.deg_weight[:, :]))
                link(nc.vector.tensor_tensor(st.deg_weight[:, :], st.deg_weight[:, :], positive[:, :], ALU.mult))

            @block.scalar
            def _(act):
                act.wait_ge(floored, 2)
                for a in (st.deg_in, st.deg_weight):
                    nc.scalar.activation(a[:, :], a[:, :], ACT.Sqrt).then_inc(rooted, 1)


def aggregate(nc, st, stage, table, src, finish):
    view = table[0:NP * NP, :].rearrange("(c p d) o -> p c (d o)", p=P, d=NP)
    with ExitStack() as ctx:
        sb, ps, sem = tools(nc, ctx, stage)
        block_in = sb("block_in", [P, 3, TILES, P])
        acc = ps("acc", [P, 2, 512])
        loaded = [sem(f"loaded{k}") for k in range(3)]
        multiplied, finished, chain = sem("multiplied"), sem("finished"), sem("chain")
        extra = finish.prepare(nc, ctx, stage) if hasattr(finish, "prepare") else None
        with nc.Block() as block:

            @block.sync
            def _(sp):
                if extra is not None:
                    finish.load(sp, extra)
                for t in range(TILES):
                    if t >= 3:
                        sp.wait_ge(multiplied, t - 2)
                    sp.dma_start(block_in[:, t % 3, :, :], view[:, :, t * P:(t + 1) * P]).then_inc(loaded[t % 3], 16)

            @block.tensor
            def _(pe):
                for t in range(TILES):
                    pe.wait_ge(loaded[t % 3], 16 * (t // 3 + 1))
                    if t >= 2:
                        pe.wait_ge(finished, t - 1)
                    for c in range(TILES):
                        last = nc.tensor.matmul(acc[:, t % 2, 0:D], block_in[:, t % 3, c, :], src[:, c, :],
                                                start=(c == 0), stop=(c == TILES - 1))
                    last.then_inc(multiplied, 1)

            @block.vector
            def _(dve):
                link = Chain(dve, chain)
                if extra is not None:
                    finish.wait(dve, extra)
                for t in range(TILES):
                    dve.wait_ge(multiplied, t + 1)
                    finish(nc, link, t, acc[:, t % 2, 0:D], extra).then_inc(finished, 1)


def scaled_into(dst, factor):
    def finish(nc, link, t, psum, extra):
        return nc.vector.tensor_scalar(dst[:, t, :], psum, factor[:, t:t + 1], None, ALU.mult)
    return finish


def relu_into(dst):
    def finish(nc, link, t, psum, extra):
        return nc.vector.tensor_scalar(dst[:, t, :], psum, 0.0, None, ALU.max)
    return finish


def copied_into(dst):
    def finish(nc, link, t, psum, extra):
        return nc.vector.tensor_copy(dst[:, t, :], psum)
    return finish


def added_to(dst):
    def finish(nc, link, t, psum, extra):
        return nc.vector.tensor_tensor(dst[:, t, :], dst[:, t, :], psum, ALU.add)
    return finish


class WeightedSum:

    def __init__(self, dst, own, factor, bias):
        self.dst, self.own, self.factor, self.bias = dst, own, factor, bias

    def prepare(self, nc, ctx, stage):
        return (ctx.enter_context(nc.sbuf_tensor(f"{stage}_bias_rows", [P, D], F32)),
                SEMAPHORES.take(nc, ctx, stage, begins=False)("bias_loaded"))

    def load(self, sp, extra):
        sp.dma_start(extra[0][:, :], self.bias.partition_broadcast(P)).then_inc(extra[1], 16)

    def wait(self, dve, extra):
        dve.wait_ge(extra[1], 16)

    def __call__(self, nc, link, t, psum, extra):
        out = self.dst[:, t, :]
        link(nc.vector.tensor_tensor(out, psum, self.own[:, t, :], ALU.add))
        return nc.vector.scalar_tensor_tensor(out=out, in0=out, scalar=self.factor[:, t:t + 1], in1=extra[0][:, :],
                                              op0=ALU.mult, op1=ALU.add)


def add_unit_rows(nc, st, stage, src):
    with ExitStack() as ctx:
        sb, ps, sem = tools(nc, ctx, stage)
        squares = sb("squares", [P, TILES, D])
        length = sb("length", [P, TILES])
        chain, summed, rooted = sem("chain"), sem("summed"), sem("rooted")
        with nc.Block() as block:

            @block.vector
            def _(dve):
                link = Chain(dve, chain)
                link(nc.vector.tensor_tensor(squares[:, :, :], src[:, :, :], src[:, :, :], ALU.mult))
                nc.vector.tensor_reduce(length[:, :], squares[:, :, :], AX, ALU.add).then_inc(summed, 1)
                dve.wait_ge(rooted, 1)
                link(nc.vector.tensor_scalar(length[:, :], length[:, :], 1e-12, None, ALU.max))
                link(nc.vector.reciprocal(length[:, :], length[:, :]))
                for t in range(TILES):
                    link.mark(nc.vector.scalar_tensor_tensor(out=st.x[:, t, :], in0=src[:, t, :], scalar=length[:, t:t + 1],
                                                             in1=st.x[:, t, :], op0=ALU.mult, op1=ALU.add))

            @block.scalar
            def _(act):
                act.wait_ge(summed, 1)
                nc.scalar.activation(length[:, :], length[:, :], ACT.Sqrt).then_inc(rooted, 1)


def layer0_gnn(nc, st, d, count_table):
    norm_nodes(nc, st, "l0_norm", st.x, st.a, False, scale=st.deg_out)
    aggregate(nc, st, "l0_sum", count_table, st.a, scaled_into(st.b, st.deg_in))
    transpose_nodes(nc, st, "l0_turn", st.b)
    linear_nodes(nc, st, "l0_linear", d["L0_gnn_W"], d["L0_gnn_b"], D, relu_into(st.b))
    add_unit_rows(nc, st, "l0_unit", st.b)


def layer1_gnn(nc, st, d, weight_table):
    norm_nodes(nc, st, "l1_norm", st.x, st.a, True)
    linear_nodes(nc, st, "l1_linear", d["L1_gnn_W"], None, D, scaled_into(st.b, st.deg_weight))
    aggregate(nc, st, "l1_sum", weight_table, st.b, WeightedSum(st.a, st.b, st.deg_weight, d["L1_gnn_b"]))
    transpose_nodes(nc, st, "l1_turn1", st.a)
    linear_nodes(nc, st, "l1_head1", d["L1_gnn_W1"], d["L1_gnn_b1"], D, relu_into(st.b))
    transpose_nodes(nc, st, "l1_turn2", st.b)
    linear_nodes(nc, st, "l1_head2", d["L1_gnn_W2"], d["L1_gnn_b2"], D, added_to(st.x))



SLOPE = 0.2


class Attention:

    def __init__(self, st, heads, width):
        self.heads, self.width = heads, width
        self.cols = heads * (width + 1)
        self.values = st.b_flat[:, 0:TILES * self.cols].rearrange("p (t h w) -> p t h w", h=heads, w=width + 1)
        flat = st.b_flat[:, 0:TILES * self.cols].rearrange("p (t c) -> p t c", c=self.cols)
        self.flat = flat
        self.groups = []
        for h in range(heads):
            for o in range(0, width + 1, P):
                self.groups.append((h, h * (width + 1) + o, min(P, width + 1 - o)))


def attention_values(nc, st, stage, att, weight, att_src, att_dst, scores):
    H, W = att.heads, att.width
    HW = H * W
    with ExitStack() as ctx:
        sb, ps, sem = tools(nc, ctx, stage)
        w = sb("weight", [P, KC, HW + 2 * H])
        vectors = sb("vectors", [P, 2, HW])
        work = sb("work", [P, KC, HW])
        acc = ps("acc", [P, 4, CHUNK])
        loaded, chain, folded, multiplied, finished = (sem(n) for n in ("loaded", "chain", "folded", "multiplied", "finished"))
        with nc.Block() as block:

            @block.sync
            def _(sp):
                sp.dma_start(w[:, :, 0:HW], weight.rearrange("(c p) m -> p c m", p=P)).then_inc(loaded, 16)
                for n, a in enumerate((att_src, att_dst)):
                    sp.dma_start(vectors[:, n, :], a.rearrange("h w -> (h w)").partition_broadcast(P)).then_inc(loaded, 16)

            @block.tensor
            def _(pe):
                pe.wait_ge(folded, 1)
                for t in range(TILES):
                    if t >= 4:
                        pe.wait_ge(finished, 2 * (t - 3))
                    for c in range(KC):
                        last = nc.tensor.matmul(acc[:, t % 4, 0:HW + 2 * H], st.aT[:, c, t * P:(t + 1) * P], w[:, c, :],
                                                start=(c == 0), stop=(c == KC - 1))
                    last.then_inc(multiplied, 1)

            @block.vector
            def _(dve):
                link = Chain(dve, chain)
                dve.wait_ge(loaded, 48)
                for n in range(2):
                    link(nc.vector.tensor_tensor(work[:, :, :], w[:, :, 0:HW], vectors[:, n, :].unsqueeze(1).to_broadcast([P, KC, HW]), ALU.mult))
                    for c in range(KC):
                        link(nc.vector.tensor_reduce(w[:, c, HW + n * H:HW + (n + 1) * H],
                                                     work[:, c, :].rearrange("p (h w) -> p h w", h=H), AX, ALU.add))
                nc.vector.memset(att.values[:, :, :, W], 1.0).then_inc(folded, 1)
                for t in range(TILES):
                    dve.wait_ge(multiplied, t + 1)
                    nc.vector.tensor_copy(att.values[:, t, :, 0:W], acc[:, t % 4, 0:HW].rearrange("p (h w) -> p h w", h=H)).then_inc(finished, 1)
                    nc.vector.tensor_copy(scores[:, t, :, :], acc[:, t % 4, HW:HW + 2 * H].rearrange("p (n h) -> p n h", n=2)).then_inc(finished, 1)


def attention_maxima(nc, st, stage, att, mask, scores, shifts):
    H = att.heads
    with ExitStack() as ctx:
        sb, ps, sem = tools(nc, ctx, stage)
        more = sb("rows", [P, 2, NP]) if H > 2 else None
        row = [st.aT[:, h, :] if h < 2 else more[:, h - 2, :] for h in range(H)]
        mask_in = sb("mask_in", [P, 3, NP], BF16)
        junk = sb("junk", [P, NP], BF16)
        top = sb("top", [P, TILES, H])
        turned = ps("turned", [P, 4, 512])
        loaded = [sem(f"loaded{k}") for k in range(3)]
        chain, transposed, copied, reduced = (sem(n) for n in ("chain", "transposed", "copied", "reduced"))
        with nc.Block() as block:

            @block.sync
            def _(sp):
                for t in range(TILES):
                    if t >= 3:
                        sp.wait_ge(reduced, (t - 2) * H)
                    sp.dma_start(mask_in[:, t % 3, :], mask[t * P:(t + 1) * P, :]).then_inc(loaded[t % 3], 16)

            @block.tensor
            def _(pe):
                n = 0
                for h in range(H):
                    for at, w in CHUNKS:
                        if n >= 4:
                            pe.wait_ge(copied, n - 3)
                        for j in range(w // P):
                            last = nc.tensor.transpose(turned[:, n % 4, j * P:(j + 1) * P],
                                                       scores[:, at // P + j, 0, h:h + 1].to_broadcast([P, P]), st.ident[:, :])
                        last.then_inc(transposed, 1)
                        n += 1

            @block.scalar
            def _(act):
                n = 0
                for h in range(H):
                    for at, w in CHUNKS:
                        act.wait_ge(transposed, n + 1)
                        nc.scalar.copy(row[h][:, at:at + w], turned[:, n % 4, 0:w]).then_inc(copied, 1)
                        n += 1

            @block.vector
            def _(dve):
                link = Chain(dve, chain)
                dve.wait_ge(copied, H * len(CHUNKS))
                n = 0
                for t in range(TILES):
                    dve.wait_ge(loaded[t % 3], 16 * (t // 3 + 1))
                    for h in range(H):
                        if n >= 1:
                            dve.wait_ge(reduced, n)
                        nc.vector.tensor_tensor_reduce(junk[:, :], row[h], mask_in[:, t % 3, :], 1.0, -3e38, ALU.add, ALU.max,
                                                       top[:, t, h:h + 1]).then_inc(reduced, 1)
                        n += 1
                dve.wait_ge(reduced, n)
                src, dst = scores[:, :, 0, :], scores[:, :, 1, :]
                link(nc.vector.tensor_tensor(top[:, :, :], top[:, :, :], dst, ALU.add))
                link(nc.vector.scalar_tensor_tensor(out=top[:, :, :], in0=top[:, :, :], scalar=SLOPE, in1=top[:, :, :], op0=ALU.mult, op1=ALU.max))
                link(nc.vector.tensor_tensor(shifts[:, :, 0, :], dst, top[:, :, :], ALU.subtract))
                link(nc.vector.scalar_tensor_tensor(out=shifts[:, :, 1, :], in0=dst, scalar=SLOPE, in1=top[:, :, :], op0=ALU.mult, op1=ALU.subtract))
                link(nc.vector.tensor_scalar(dst, src, SLOPE, None, ALU.mult))


def attention_sums(nc, st, stage, att, table, scores, shifts, finish):
    H, G = att.heads, len(att.groups)
    view = table[0:NP * NP, :].rearrange("(r d) o -> r (d o)", d=NP)
    with ExitStack() as ctx:
        sb, ps, sem = tools(nc, ctx, stage)
        rows = sb("rows", [P, 2, H, CHUNK])
        count_in = sb("count_in", [P, 4, CHUNK])
        e = sb("e", [P, 2, 2, H, CHUNK])
        p = st.aT[:, :, :].rearrange("p c n -> p (c n)")[:, 0:2 * H * CHUNK].rearrange("p (s h n) -> p s h n", s=2, h=H)
        outT = sb("outT", [P, G, CHUNK])
        acc = ps("acc", [P, 4, 512])
        turned = ps("turned", [P, 2, 512])
        final = ps("final", [P, 2, 512])
        loaded = [sem(f"loaded{k}") for k in range(4)]
        chain, transposed, copied, exped, weighed, summed, drained, final_ready, finished = (
            sem(n) for n in ("chain", "transposed", "copied", "exped", "weighed", "summed", "drained", "final_ready", "finished"))
        used = sem("used")
        extra = finish.prepare(nc, ctx, stage) if hasattr(finish, "prepare") else None
        with nc.Block() as block:

            @block.sync
            def _(sp):
                if extra is not None:
                    finish.load(sp, extra)
                n = 0
                for at, w in CHUNKS:
                    for c in range(TILES):
                        if n >= 4:
                            sp.wait_ge(weighed, n - 3)
                        sp.dma_start(count_in[:, n % 4, 0:w], view[c * P:(c + 1) * P, at:at + w]).then_inc(loaded[n % 4], 16)
                        n += 1

            @block.tensor
            def _(pe):
                n = r = f = 0

                def turn_chunk(f, at, w):
                    for t in range(at // P, (at + w) // P):
                        if f >= 2:
                            pe.wait_ge(finished, f - 1)
                        for g, (h, col, m) in enumerate(att.groups):
                            last = nc.tensor.transpose(final[:, f % 2, col:col + m], outT[0:m, g, t * P - at:(t + 1) * P - at], st.ident[0:m, 0:m])
                        last.then_inc(final_ready, 1)
                        f += 1
                    return f

                for q, (at, w) in enumerate(CHUNKS):
                    for k in range(2):
                        for h in range(H):
                            if r >= 2:
                                pe.wait_ge(copied, r - 1)
                            for j in range(w // P):
                                last = nc.tensor.transpose(turned[:, r % 2, j * P:(j + 1) * P],
                                                           shifts[:, at // P + j, k, h:h + 1].to_broadcast([P, P]), st.ident[:, :])
                            last.then_inc(transposed, 1)
                            r += 1
                    for c in range(TILES):
                        pe.wait_ge(weighed, n + 1)
                        if c == 0 and q > 0:
                            pe.wait_ge(drained, q * G)
                        for g, (h, col, m) in enumerate(att.groups):
                            last = nc.tensor.matmul(acc[0:m, g, 0:w], att.flat[:, c, col:col + m], p[:, n % 2, h, 0:w],
                                                    start=(c == 0), stop=(c == TILES - 1))
                        last.then_inc(summed, 1)
                        n += 1
                        if c == 1 and q:
                            f = turn_chunk(f, *CHUNKS[q - 1])
                pe.wait_ge(drained, len(CHUNKS) * G)
                turn_chunk(f, *CHUNKS[-1])

            @block.scalar
            def _(act):
                n = r = f = 0
                for q, (at, w) in enumerate(CHUNKS):
                    if q:
                        act.wait_ge(exped, n)
                    for k in range(2):
                        for h in range(H):
                            act.wait_ge(transposed, r + 1)
                            nc.scalar.copy(rows[:, k, h, 0:w], turned[:, r % 2, 0:w]).then_inc(copied, 1)
                            r += 1
                    act.wait_ge(copied, r)
                    for c in range(TILES):
                        if n >= 2:
                            act.wait_ge(weighed, n - 1)
                        for k in range(2):
                            for h in range(H):
                                last = nc.scalar.activation(e[:, n % 2, k, h, 0:w], rows[:, k, h, 0:w], ACT.Exp,
                                                            bias=scores[:, c, k, h:h + 1])
                        last.then_inc(exped, 1)
                        n += 1
                    act.wait_ge(summed, n)
                    if q:
                        act.wait_ge(final_ready, at // P)
                    for g, (h, col, m) in enumerate(att.groups):
                        nc.scalar.copy(outT[0:m, g, 0:w], acc[0:m, g, 0:w]).then_inc(drained, 1)

            @block.vector
            def _(dve):
                link = Chain(dve, chain)
                if extra is not None:
                    finish.wait(dve, extra)
                n = f = 0

                def finish_chunk(f, at, w):
                    for t in range(at // P, (at + w) // P):
                        dve.wait_ge(final_ready, f + 1)
                        finish(nc, link, t, final[:, f % 2, 0:att.cols].rearrange("p (h w) -> p h w", h=H), extra).then_inc(finished, 1)
                        f += 1
                    return f

                for q, (at, w) in enumerate(CHUNKS):
                    for c in range(TILES):
                        dve.wait_ge(loaded[n % 4], 16 * (n // 4 + 1))
                        if at <= c * P < at + w:
                            own = count_in[:, n % 4, c * P - at:(c + 1) * P - at]
                            link(nc.vector.tensor_tensor(own, own, st.ident[:, :], ALU.add))
                        dve.wait_ge(exped, n + 1)
                        if n >= 2:
                            dve.wait_ge(summed, n - 1)
                        link(nc.vector.tensor_tensor(e[:, n % 2, 0, :, 0:w], e[:, n % 2, 0, :, 0:w], e[:, n % 2, 1, :, 0:w], ALU.max))
                        nc.vector.scalar_tensor_tensor(out=p[:, n % 2, :, 0:w], in0=e[:, n % 2, 0, :, 0:w], scalar=1.0,
                                                       in1=count_in[:, n % 4, 0:w].unsqueeze(1).to_broadcast([P, H, w]),
                                                       op0=ALU.min, op1=ALU.mult).then_inc(weighed, 1)
                        n += 1
                        if c == 1 and q:
                            f = finish_chunk(f, *CHUNKS[q - 1])
                finish_chunk(f, *CHUNKS[-1])


class Averaged:

    def __init__(self, att, target, bias, add=False):
        self.att, self.target, self.bias, self.add = att, target, bias, add

    def prepare(self, nc, ctx, stage):
        width = self.att.heads * self.att.width
        return (ctx.enter_context(nc.sbuf_tensor(f"{stage}_bias_rows", [P, width], F32)),
                SEMAPHORES.take(nc, ctx, stage, begins=False)("bias_loaded"),
                ctx.enter_context(nc.sbuf_tensor(f"{stage}_inverse", [P, self.att.heads], F32)),
                ctx.enter_context(nc.sbuf_tensor(f"{stage}_average", [P, width], F32)))

    def load(self, sp, extra):
        sp.dma_start(extra[0][:, :], self.bias.partition_broadcast(P)).then_inc(extra[1], 16)

    def wait(self, dve, extra):
        dve.wait_ge(extra[1], 16)

    def __call__(self, nc, link, t, psum, extra):
        H, W = self.att.heads, self.att.width
        bias, _, inverse, average = extra
        out = self.target[:, t, :]
        link(nc.vector.tensor_scalar(inverse[:, :], psum[:, :, W], 1e-16, None, ALU.add))
        link(nc.vector.reciprocal(inverse[:, :], inverse[:, :]))
        link(nc.vector.tensor_tensor(average[:, :].rearrange("p (h w) -> p h w", h=H), psum[:, :, 0:W],
                                     inverse[:, :].unsqueeze(2).to_broadcast([P, H, W]), ALU.mult))
        if self.add:
            link(nc.vector.tensor_tensor(out, out, bias[:, :], ALU.add))
            last = nc.vector.tensor_tensor(out, out, average[:, :], ALU.add)
        else:
            last = nc.vector.tensor_tensor(out, average[:, :], bias[:, :], ALU.add)
        return last


def elu_nodes(nc, st, stage):
    with ExitStack() as ctx:
        sb, ps, sem = tools(nc, ctx, stage)
        chain, clipped, exped = sem("chain"), sem("clipped"), sem("exped")
        with nc.Block() as block:

            @block.vector
            def _(dve):
                link = Chain(dve, chain)
                for t in range(0, TILES, 5):
                    nc.vector.tensor_scalar(st.b[:, t:t + 5, :], st.a[:, t:t + 5, :], 0.0, None, ALU.min).then_inc(clipped, 1)
                for n, t in enumerate(range(0, TILES, 5)):
                    dve.wait_ge(exped, n + 1)
                    a = st.a[:, t:t + 5, :].rearrange("p t d -> p (t d)")
                    b = st.b[:, t:t + 5, :].rearrange("p t d -> p (t d)")
                    link(nc.vector.scalar_tensor_tensor(out=a, in0=a, scalar=0.0, in1=b, op0=ALU.max, op1=ALU.add))
                    link(nc.vector.tensor_scalar(a, a, -1.0, None, ALU.add))

            @block.scalar
            def _(act):
                for n, t in enumerate(range(0, TILES, 5)):
                    act.wait_ge(clipped, n + 1)
                    nc.scalar.activation(st.b[:, t:t + 5, :], st.b[:, t:t + 5, :], ACT.Exp).then_inc(exped, 1)


def attend(nc, st, stage, att, table, mask, weight, att_src, att_dst, finish):
    with ExitStack() as ctx:
        sb, ps, sem = tools(nc, ctx, stage)
        scores = sb("scores", [P, TILES, 2, att.heads])
        shifts = sb("shifts", [P, TILES, 2, att.heads])
        attention_values(nc, st, stage + "v", att, weight, att_src, att_dst, scores)
        attention_maxima(nc, st, stage + "m", att, mask, scores, shifts)
        attention_sums(nc, st, stage + "s", att, table, scores, shifts, finish)


def layer3_gnn(nc, st, d, table, mask):
    norm_nodes(nc, st, "l3_norm", st.x, st.a, True)
    for n in range(2):
        att = Attention(st, 4, D // 4)
        attend(nc, st, f"l3_{n}", att, table, mask, d[f"L3_gnn_W{n}"], d[f"L3_gnn_as{n}"], d[f"L3_gnn_ad{n}"],
               Averaged(att, st.a, d[f"L3_gnn_b{n}"]))
        elu_nodes(nc, st, f"l3_{n}elu")
        transpose_nodes(nc, st, f"l3_{n}turn", st.a)
    att = Attention(st, 1, D)
    attend(nc, st, "l3_2", att, table, mask, d["L3_gnn_W2"], d["L3_gnn_as2"], d["L3_gnn_ad2"],
           Averaged(att, st.x, d["L3_gnn_b2"], add=True))



TYPES, RELATIONS, HEADS = 4, 8, 8
HEAD = D // HEADS
SEGMENTS = NP * RELATIONS
SUMS = D + HEADS
AHEAD = 2


def typed_linear(nc, st, stage, type_masks, weight, bias, dst):
    with ExitStack() as ctx:
        sb, ps, sem = tools(nc, ctx, stage)
        w = sb("weight", [P, TYPES, KC, D])
        b = sb("bias", [1, TYPES, D])
        acc = ps("acc", [P, 2, TYPES, 512])
        loaded, chain, multiplied, finished = sem("loaded"), sem("chain"), sem("multiplied"), sem("finished")
        with nc.Block() as block:

            @block.sync
            def _(sp):
                for k in range(TYPES):
                    sp.dma_start(w[:, k, :, :], weight[k].rearrange("(c p) m -> p c m", p=P)).then_inc(loaded, 16)
                    sp.dma_start(b[0:1, k, :], bias[k:k + 1, :]).then_inc(loaded, 16)

            @block.tensor
            def _(pe):
                pe.wait_ge(loaded, 32 * TYPES)
                for t in range(TILES):
                    if t >= 2:
                        pe.wait_ge(finished, t - 1)
                    for k in range(TYPES):
                        for c in range(KC):
                            nc.tensor.matmul(acc[:, t % 2, k, 0:D], st.aT[:, c, t * P:(t + 1) * P], w[:, k, c, :],
                                             start=(c == 0), stop=False)
                        nc.tensor.matmul(acc[:, t % 2, k, 0:D], st.ones_row[0:1, 0:P], b[0:1, k, :],
                                         start=False, stop=True).then_inc(multiplied, 1)

            @block.vector
            def _(dve):
                link = Chain(dve, chain)
                for t in range(TILES):
                    for k in range(TYPES):
                        dve.wait_ge(multiplied, t * TYPES + k + 1)
                        mask = type_masks[:, k, t:t + 1]
                        if k == 0:
                            last = nc.vector.tensor_scalar(dst[:, t, :], acc[:, t % 2, k, 0:D], mask, None, ALU.mult)
                        else:
                            last = nc.vector.scalar_tensor_tensor(out=dst[:, t, :], in0=acc[:, t % 2, k, 0:D], scalar=mask,
                                                                  in1=dst[:, t, :], op0=ALU.mult, op1=ALU.add)
                        if k < TYPES - 1:
                            link(last)
                        else:
                            last.then_inc(finished, 1)


def load_types(nc, st, stage, node_type, skip, type_masks, keep):
    with ExitStack() as ctx:
        sb, ps, sem = tools(nc, ctx, stage)
        kinds = sb("kinds", [P, TILES], I32)
        kinds_f = sb("kinds_f", [P, TILES])
        gate = sb("gate", [P, TYPES])
        cleared, loaded, chain, gated = sem("cleared"), sem("loaded"), sem("chain"), sem("gated")
        with nc.Block() as block:

            @block.sync
            def _(sp):
                sp.wait_ge(cleared, 1)
                full = N - LAST
                with nc.allow_non_contiguous_dma("types by tile"):
                    sp.dma_start(kinds[:, 0:TILES - 1], node_type[0:full].rearrange("(t p) -> p t", p=P)).then_inc(loaded, 16)
                    sp.dma_start(kinds[0:LAST, TILES - 1:TILES], node_type[full:N].rearrange("(p o) -> p o", o=1)).then_inc(loaded, 16)
                sp.dma_start(gate[:, :], skip.partition_broadcast(P)).then_inc(loaded, 16)

            @block.scalar
            def _(act):
                act.wait_ge(loaded, 48)
                nc.scalar.activation(gate[:, :], gate[:, :], ACT.Sigmoid).then_inc(gated, 1)

            @block.vector
            def _(dve):
                link = Chain(dve, chain)
                nc.vector.memset(kinds[:, :], 0).then_inc(cleared, 1)
                dve.wait_ge(loaded, 48)
                link(nc.vector.tensor_copy(kinds_f[:, :], kinds[:, :]))
                for k in range(TYPES):
                    link(nc.vector.tensor_scalar(type_masks[:, k, :], kinds_f[:, :], float(k), None, ALU.is_equal))
                dve.wait_ge(gated, 1)
                link(nc.vector.tensor_scalar(keep[:, :], type_masks[:, 0, :], gate[:, 0:1], None, ALU.mult))
                for k in range(1, TYPES):
                    link(nc.vector.scalar_tensor_tensor(out=keep[:, :], in0=type_masks[:, k, :], scalar=gate[:, k:k + 1],
                                                        in1=keep[:, :], op0=ALU.mult, op1=ALU.add))


def store_rows(nc, st, stage, src, table):
    with ExitStack() as ctx:
        sb, ps, sem = tools(nc, ctx, stage)
        stored = sem("stored")
        with nc.Block() as block:

            @block.sync
            def _(sp):
                sp.dma_start(table.rearrange("(t p) f -> p t f", p=P), src[:, :, :]).then_inc(stored, 16)
                sp.wait_ge(stored, 16)


def relate_rows(nc, st, stage, relation, priority, table):
    with ExitStack() as ctx:
        sb, ps, sem = tools(nc, ctx, stage)
        blocks = sb("blocks", [P, KC, RELATIONS, P])
        pri = sb("pri", [P, RELATIONS, HEADS])
        rows = sb("rows", [P, 2, RELATIONS, D])
        acc = ps("acc", [P, 2, 4, 512])
        cleared, loaded, ready, chain, multiplied = (sem(n) for n in ("cleared", "loaded", "ready", "chain", "multiplied"))
        stored = [sem(f"stored{k}") for k in range(2)]
        copied = [sem("copied_by_act"), sem("copied_by_dve")]
        PER = P // HEAD
        with nc.Block() as block:

            @block.sync
            def _(sp):
                sp.wait_ge(cleared, 1)
                for h in range(HEADS):
                    c, o = h // PER, h % PER * HEAD
                    sp.dma_start(blocks[o:o + HEAD, c, :, o:o + HEAD], relation[:, h, :, :].rearrange("r d e -> d r e")).then_inc(loaded, 16)
                if priority is not None:
                    sp.dma_start(pri[:, :, :], priority.rearrange("r h -> (r h)").partition_broadcast(P).rearrange("p (r h) -> p r h", h=HEADS)).then_inc(loaded, 16)
                out = table[0:SEGMENTS, :].rearrange("(t p r) f -> t p r f", p=P, r=RELATIONS)
                for t in range(TILES):
                    for s in copied:
                        sp.wait_ge(s, 2 * (t + 1))
                    sp.dma_start(out[t], rows[:, t % 2, :, :]).then_inc(stored[t % 2], 16)
                for k in range(2):
                    sp.wait_ge(stored[k], 16 * ((TILES + 1 - k) // 2))

            @block.tensor
            def _(pe):
                pe.wait_ge(ready, 1)
                for t in range(TILES):
                    if t >= 2:
                        for s in copied:
                            pe.wait_ge(s, 2 * (t - 1))
                    for c in range(KC):
                        for half in range(2):
                            nc.tensor.matmul(acc[:, t % 2, c * 2 + half, :], st.aT[:, c, t * P:(t + 1) * P],
                                             blocks[:, c, half * 4:half * 4 + 4, :].rearrange("p r e -> p (r e)"),
                                             start=True, stop=True).then_inc(multiplied, 1)

            def copy_half(eng, op, mine, t, c):
                for half in range(2):
                    eng.wait_ge(multiplied, t * 4 + c * 2 + half + 1)
                    op(rows[:, t % 2, half * 4:half * 4 + 4, c * P:(c + 1) * P],
                       acc[:, t % 2, c * 2 + half, :].rearrange("p (r e) -> p r e", e=P)).then_inc(mine, 1)

            @block.scalar
            def _(act):
                for t in range(TILES):
                    if t >= 2:
                        act.wait_ge(stored[t % 2], 16 * (t // 2))
                    copy_half(act, nc.scalar.copy, copied[0], t, 0)

            @block.vector
            def _(dve):
                link = Chain(dve, chain)
                nc.vector.memset(blocks[:, :, :, :], 0.0).then_inc(cleared, 1)
                dve.wait_ge(loaded, 16 * (HEADS + (priority is not None)))
                if priority is not None:
                    link(nc.vector.tensor_scalar(pri[:, :, :], pri[:, :, :], float(HEAD) ** -0.5, None, ALU.mult))
                    for c in range(KC):
                        own = blocks[:, c, :, :].rearrange("p r (h e) -> p r h e", e=HEAD)
                        link(nc.vector.tensor_tensor(own, own, pri[:, :, c * PER:(c + 1) * PER].unsqueeze(3).to_broadcast([P, RELATIONS, PER, HEAD]), ALU.mult))
                dve.sem_inc(ready, 1)
                for t in range(TILES):
                    if t >= 2:
                        dve.wait_ge(stored[t % 2], 16 * (t // 2))
                    copy_half(dve, nc.vector.tensor_copy, copied[1], t, 1)


def fill_table(nc, stage, table, value, parts):
    rows = table.rearrange("(p r) f -> p (r f)", p=P)
    run = rows.shape[1] // parts
    assert run * parts == rows.shape[1]
    with ExitStack() as ctx:
        sb, ps, sem = tools(nc, ctx, stage)
        fill = sb("fill", [P, run])
        cleared, stored = sem("cleared"), sem("stored")
        with nc.Block() as block:

            @block.vector
            def _(dve):
                nc.vector.memset(fill[:, :], value).then_inc(cleared, 1)

            @block.sync
            def _(sp):
                sp.wait_ge(cleared, 1)
                for k in range(parts):
                    sp.dma_start(rows[:, k * run:(k + 1) * run], fill[:, :]).then_inc(stored, 16)
                sp.wait_ge(stored, 16 * parts)


def edge_lists(nc, st, stage, src, dst, kind, lists):
    src_rows, segment, segment_f, dst_i = lists
    edges = src.shape[0]
    cols = edge_columns(edges)
    full, rest = edges // cols, edges % cols
    with ExitStack() as ctx:
        sb, ps, sem = tools(nc, ctx, stage)
        raw = [sb(n, [P, cols + AHEAD], I32) for n in ("src_raw", "dst_raw", "kind_raw")]
        value = [sb(n, [P, cols + AHEAD]) for n in ("src_value", "dst_value", "kind_value")]
        cleared, loaded, chain = sem("cleared"), sem("loaded"), sem("chain")
        with nc.Block() as block:

            @block.sync
            def _(sp):
                sp.wait_ge(cleared, 3)
                for a, r in zip((src, dst, kind), raw):
                    sp.dma_start(r[0:full, 0:cols], a[0:full * cols].rearrange("(p c) -> p c", c=cols)).then_inc(loaded, 16)
                    if rest:
                        sp.dma_start(r[full:full + 1, 0:rest], a[full * cols:edges].rearrange("(o c) -> o c", o=1)).then_inc(loaded, 16)

            @block.vector
            def _(dve):
                link = Chain(dve, chain)
                for r, fill in zip(raw, (N, N, 0)):
                    nc.vector.memset(r[:, :], fill).then_inc(cleared, 1)
                dve.wait_ge(loaded, 16 * 3 * (2 if rest else 1))
                for v, r in zip(value, raw):
                    link.mark(nc.vector.tensor_copy(v[:, :], r[:, :]))
                link.mark(nc.vector.tensor_copy(dst_i[:, :], raw[1][:, :]))
                link.settle()
                for v, out in ((value[0], src_rows), (value[1], segment), (value[1], segment_f)):
                    link.mark(nc.vector.scalar_tensor_tensor(out=out[:, :], in0=v[:, :], scalar=float(RELATIONS), in1=value[2][:, :],
                                                             op0=ALU.mult, op1=ALU.add))


def segment_maxima(nc, st, stage, lists, cells, scores, q_table, k_table, max_table):
    src_rows, segment, segment_f, dst_i = lists
    cols = segment.shape[1] - AHEAD
    with ExitStack() as ctx:
        sb, ps, sem = tools(nc, ctx, stage)
        spare_i = sb("spare_i", [P, 1], I32)
        spare = sb("spare", [P, 1])
        below = sb("below", [P, P])
        index = sb("index", [P, 2, 3], I32)
        key = sb("key", [P, 2, 1])
        k_in = sb("k_in", [P, 2, D])
        q_in = sb("q_in", [P, 2, D])
        product = sb("product", [P, 2, D])
        score = sb("score", [P, 2, HEADS])
        same = sb("same", [P, 2, P])
        junk = sb("junk", [P, P])
        repeated = sb("repeated", [P, 2, 2])
        aside = sb("aside", [P, 2, 1])
        cell = sb("cell", [P, 2, 1], I32)
        masked = sb("masked", [P, HEADS, P])
        local = sb("local", [P, 2, HEADS])
        old = sb("old", [P, 2, HEADS])
        new = sb("new", [P, 2, HEADS])
        keyrow = ps("keyrow", [P, 512])
        spread = ps("spread", [P, 2, 4, P])
        tick, consts, chain = sem("tick"), sem("consts"), sem("chain")
        gathered = [sem(f"gathered{k}", pool_dma=True) for k in range(2)]
        indexed, scored, row_ready, compared, spread_ready, spread_used, local_ready, new_ready, steps = (
            sem(n) for n in ("indexed", "scored", "row_ready", "compared", "spread_ready", "spread_used", "local_ready",
                             "new_ready", "steps"))
        old_ready, written = sem("old_ready", pool_dma=True), sem("written", pool_dma=True)
        with nc.Block() as block:

            @block.gpsimd
            def _(pool):
                nc.gpsimd.iota(spare_i[:, :], pattern=[[0, 1]], base=SEGMENTS, channel_multiplier=1).then_inc(tick, 1)
                nc.gpsimd.memset(below[:, :], 1.0).then_inc(tick, 1)
                nc.gpsimd.memset(new[:, 0, :], FAR).then_inc(tick, 1)
                pool.wait_ge(tick, 3)
                nc.gpsimd.affine_select(out=below[:, :], in_=below[:, :], compare_op=ALU.is_gt, fill=0.0, base=0,
                                        pattern=[[-1, P]], channel_multiplier=1).then_inc(consts, 1)
                pool.indirect_dma_start(out=max_table, out_offset=bass.IndirectOffsetOnAxis(ap=spare_i[:, 0:1], axis=0),
                                        in_=new[:, 0, :], in_offset=None).then_inc(written, 16)

                def gather_ends(c, k):
                    pool.wait_ge(indexed, c + 1)
                    pool.sem_inc(tick, 1)
                    pool.indirect_dma_start(out=k_in[:, k, :], out_offset=None, in_=k_table,
                                            in_offset=bass.IndirectOffsetOnAxis(ap=index[:, k, 0:1], axis=0)).then_inc(gathered[k], 16)
                    pool.indirect_dma_start(out=q_in[:, k, :], out_offset=None, in_=q_table,
                                            in_offset=bass.IndirectOffsetOnAxis(ap=index[:, k, 1:2], axis=0)).then_inc(gathered[k], 16)

                gather_ends(0, 0)
                with pool.Fori(0, cols // 2) as i:
                    for k in range(2):
                        c = i * 2 + k
                        pool.wait_ge(written, c * 16 + 16)
                        pool.sem_inc(tick, 1)
                        pool.indirect_dma_start(out=old[:, k, :], out_offset=None, in_=max_table,
                                                in_offset=bass.IndirectOffsetOnAxis(ap=index[:, k, 2:3], axis=0)).then_inc(old_ready, 16)
                        gather_ends(c + 1, 1 - k)
                        pool.wait_ge(new_ready, c + 1)
                        pool.sem_inc(tick, 1)
                        pool.indirect_dma_start(out=max_table, out_offset=bass.IndirectOffsetOnAxis(ap=cell[:, k, 0:1], axis=0),
                                                in_=new[:, k, :], in_offset=None).then_inc(written, 16)
                pool.wait_ge(gathered[0], 16 * (cols + 2))
                pool.wait_ge(written, 16 + 16 * cols)

            @block.tensor
            def _(pe):
                with pe.Fori(0, cols // 2) as i:
                    for k in range(2):
                        c = i * 2 + k
                        pe.wait_ge(indexed, c + 1)
                        pe.wait_ge(compared, c + 1)
                        nc.tensor.transpose(keyrow[:, 0:P], key[:, k, 0:1].to_broadcast([P, P]), st.ident[:, :]).then_inc(row_ready, 1)
                        pe.wait_ge(scored, c + 1)
                        pe.wait_ge(spread_used, c * 2 + 2)
                        for h in range(HEADS):
                            last = nc.tensor.transpose(spread[:, h // 4, h % 4, :], score[:, k, h:h + 1].to_broadcast([P, P]), st.ident[:, :])
                        last.then_inc(spread_ready, 1)

            @block.vector
            def _(dve):
                PER = 12
                dve.wait_ge(tick, 3)
                link = Chain(dve, chain)
                link(nc.vector.tensor_copy(spare[:, :], spare_i[:, :]))
                dve.wait_ge(consts, 1)
                dve.wait_ge(written, 16)
                dve.sem_inc(compared, 1)
                dve.sem_inc(spread_used, 2)

                def fetch_lists(c, k, before):
                    col = lambda a: a[:, bass.ds(c, 1)]
                    nc.vector.tensor_copy(key[:, k, :], col(segment_f)).then_inc(steps, 1)
                    nc.vector.tensor_copy(index[:, k, 0:1], col(src_rows)).then_inc(steps, 1)
                    nc.vector.tensor_copy(index[:, k, 1:2], col(dst_i)).then_inc(steps, 1)
                    nc.vector.tensor_copy(index[:, k, 2:3], col(segment)).then_inc(steps, 1)
                    dve.wait_ge(steps, before + 4)
                    dve.sem_inc(indexed, 1)

                fetch_lists(0, 0, 0)
                with dve.Fori(0, cols // 2) as i:
                    for k in range(2):
                        c = i * 2 + k
                        fetch_lists(c + 1, 1 - k, c * PER + 4)
                        link = Chain(dve, steps, c * PER + 8)
                        dve.wait_ge(row_ready, c + 1)
                        nc.vector.tensor_scalar(same[:, k, :], keyrow[:, 0:P], key[:, k, 0:1], None, ALU.is_equal).then_inc(compared, 1)
                        dve.wait_ge(compared, c + 2)
                        link.mark(nc.vector.tensor_tensor_reduce(junk[:, :], same[:, k, :], below[:, :], 1.0, 0.0, ALU.mult, ALU.add,
                                                                 repeated[:, k, 0:1]))
                        link(nc.vector.tensor_scalar(aside[:, k, :], key[:, k, :], -1.0, spare[:, 0:1], ALU.mult, ALU.add))
                        link(nc.vector.tensor_scalar(repeated[:, k, 1:2], repeated[:, k, 0:1], 0.0, None, ALU.is_gt))
                        link(nc.vector.scalar_tensor_tensor(out=cell[:, k, :], in0=aside[:, k, :], scalar=repeated[:, k, 1:2],
                                                            in1=key[:, k, :], op0=ALU.mult, op1=ALU.add))
                        link.mark(nc.vector.tensor_scalar(same[:, k, :], same[:, k, :], -1.0, -FAR, ALU.add, ALU.mult))
                        dve.wait_ge(gathered[k], i * 32 + 32)
                        link(nc.vector.tensor_tensor(product[:, k, :], q_in[:, k, :], k_in[:, k, :], ALU.mult))
                        nc.vector.tensor_reduce(score[:, k, :], product[:, k, :].rearrange("p (h e) -> p h e", e=HEAD), AX, ALU.add).then_inc(scored, 1)
                        dve.wait_ge(scored, c + 1)
                        link.mark(nc.vector.tensor_copy(scores[:, bass.ds(c, 1), :].rearrange("p o h -> p (o h)"), score[:, k, :]))
                        link.mark(nc.vector.tensor_copy(cells[:, bass.ds(c, 1)], cell[:, k, :]))
                        dve.wait_ge(spread_ready, c + 1)
                        for half in range(2):
                            nc.vector.tensor_tensor(masked[:, half * 4:half * 4 + 4, :], spread[:, half, :, :],
                                                    same[:, k, :].unsqueeze(1).to_broadcast([P, 4, P]), ALU.add).then_inc(spread_used, 1)
                        dve.wait_ge(spread_used, c * 2 + 4)
                        nc.vector.tensor_reduce(local[:, k, :], masked[:, :, :], AX, ALU.max).then_inc(local_ready, 1)
                        dve.wait_ge(local_ready, c + 1)
                        dve.wait_ge(old_ready, c * 16 + 16)
                        dve.wait_ge(written, c * 16 + 16)
                        nc.vector.tensor_tensor(new[:, k, :], local[:, k, :], old[:, k, :], ALU.max).then_inc(new_ready, 1)


def segment_sums(nc, st, stage, lists, cells, scores, v_table, max_table, sum_table):
    src_rows, segment, segment_f, dst_i = lists
    cols = segment.shape[1] - AHEAD
    with ExitStack() as ctx:
        sb, ps, sem = tools(nc, ctx, stage)
        spare_i = sb("spare_i", [P, 1], I32)
        zeros = sb("zeros", [P, SUMS])
        index = sb("index", [P, 4, 2], I32)
        cell = sb("cell", [P, 4, 1], I32)
        key = sb("key", [P, 4, 1])
        v_in = sb("v_in", [P, 4, D])
        top = sb("top", [P, 4, HEADS])
        same = sb("same", [P, 4, P])
        term = sb("term", [P, 4, SUMS])
        merged = sb("merged", [P, 4, SUMS])
        keyrow = ps("keyrow", [P, 512])
        sums = ps("sums", [P, 2, 512])
        tick, consts, chain, steps = sem("tick"), sem("consts"), sem("chain"), sem("steps")
        gathered = [sem(f"gathered{k}", pool_dma=True) for k in range(4)]
        indexed, row_ready, compared, shifted, exped, term_ready, sum_ready, merged_ready = (
            sem(n) for n in ("indexed", "row_ready", "compared", "shifted", "exped", "term_ready", "sum_ready", "merged_ready"))
        added = sem("added", pool_dma=True)
        with nc.Block() as block:

            @block.gpsimd
            def _(pool):
                nc.gpsimd.iota(spare_i[:, :], pattern=[[0, 1]], base=SEGMENTS, channel_multiplier=1).then_inc(consts, 1)
                nc.gpsimd.memset(zeros[:, :], 0.0).then_inc(consts, 1)
                pool.wait_ge(consts, 2)
                for n in range(2):
                    if n:
                        pool.wait_ge(added, 16)
                    pool.indirect_dma_start(out=sum_table, out_offset=bass.IndirectOffsetOnAxis(ap=spare_i[:, 0:1], axis=0),
                                            in_=zeros[:, :], in_offset=None, compute_op=ALU.add).then_inc(added, 16)

                def gather(c, k):
                    pool.wait_ge(indexed, c + 1)
                    pool.sem_inc(tick, 1)
                    pool.indirect_dma_start(out=v_in[:, k, :], out_offset=None, in_=v_table,
                                            in_offset=bass.IndirectOffsetOnAxis(ap=index[:, k, 0:1], axis=0)).then_inc(gathered[k], 16)
                    pool.indirect_dma_start(out=top[:, k, :], out_offset=None, in_=max_table,
                                            in_offset=bass.IndirectOffsetOnAxis(ap=index[:, k, 1:2], axis=0)).then_inc(gathered[k], 16)

                gather(0, 0)
                gather(1, 1)
                with pool.Fori(0, cols // 4) as i:
                    for pair in (0, 2):
                        for k in (pair, pair + 1):
                            gather(i * 4 + k + 2, (k + 2) % 4)
                        for k in (pair, pair + 1):
                            c = i * 4 + k
                            pool.wait_ge(merged_ready, c + 3)
                            pool.wait_ge(added, c * 16 + 32)
                            pool.sem_inc(tick, 1)
                            pool.indirect_dma_start(out=sum_table, out_offset=bass.IndirectOffsetOnAxis(ap=cell[:, k, 0:1], axis=0),
                                                    in_=merged[:, k, :], in_offset=None, compute_op=ALU.add).then_inc(added, 16)
                pool.wait_ge(added, 32 + 16 * cols)
                for k in range(4):
                    pool.wait_ge(gathered[k], 32 * (cols // 4 + (k < 2)))

            @block.tensor
            def _(pe):
                with pe.Fori(0, cols // 4) as i:
                    for pair in (0, 2):
                        for k in (pair, pair + 1):
                            c = i * 4 + k
                            pe.wait_ge(indexed, c + 1)
                            pe.wait_ge(compared, c + 1)
                            nc.tensor.transpose(keyrow[:, 0:P], key[:, k, 0:1].to_broadcast([P, P]), st.ident[:, :]).then_inc(row_ready, 1)
                        for k in (pair, pair + 1):
                            c = i * 4 + k
                            pe.wait_ge(term_ready, c + 2)
                            pe.wait_ge(merged_ready, c + 1)
                            nc.tensor.matmul(sums[:, k % 2, 0:SUMS], same[:, k, :], term[:, k, :], start=True, stop=True).then_inc(sum_ready, 1)

            @block.scalar
            def _(act):
                act.sem_inc(merged_ready, 2)
                with act.Fori(0, cols // 4) as i:
                    for pair in (0, 2):
                        for k in (pair, pair + 1):
                            act.wait_ge(shifted, i * 4 + k + 1)
                            nc.scalar.activation(term[:, k, D:SUMS], top[:, k, :], ACT.Exp).then_inc(exped, 1)
                        for k in (pair, pair + 1):
                            c = i * 4 + k
                            act.wait_ge(sum_ready, c + 1)
                            act.wait_ge(added, c * 16 + 16)
                            nc.scalar.copy(merged[:, k, :], sums[:, k % 2, 0:SUMS]).then_inc(merged_ready, 1)

            @block.vector
            def _(dve):
                PER = 4
                dve.sem_inc(compared, 1)
                dve.sem_inc(term_ready, 1)
                col = lambda a, c: a[:, bass.ds(c, 1)]

                def fetch_lists(c, k, before):
                    nc.vector.tensor_copy(key[:, k, :], col(segment_f, c)).then_inc(steps, 1)
                    nc.vector.tensor_copy(index[:, k, 0:1], col(src_rows, c)).then_inc(steps, 1)
                    nc.vector.tensor_copy(index[:, k, 1:2], col(segment, c)).then_inc(steps, 1)
                    dve.wait_ge(steps, before + 3)
                    dve.sem_inc(indexed, 1)

                fetch_lists(0, 0, 0)
                fetch_lists(1, 1, 3)
                with dve.Fori(0, cols // 4) as i:
                    for pair in (0, 2):
                        dve.wait_ge(term_ready, i * 4 + pair + 1)
                        for n in range(2):
                            k = pair + n
                            fetch_lists(i * 4 + k + 2, (k + 2) % 4, (i * 4 + pair) * PER + 6 + 3 * n)
                        for n in range(2):
                            k = pair + n
                            c = i * 4 + k
                            dve.wait_ge(added, c * 16 + 16)
                            nc.vector.tensor_copy(cell[:, k, :], col(cells, c)).then_inc(steps, 1)
                            dve.wait_ge(row_ready, c + 1)
                            nc.vector.tensor_scalar(same[:, k, :], keyrow[:, 0:P], key[:, k, 0:1], None, ALU.is_equal).then_inc(compared, 1)
                        for n in range(2):
                            k = pair + n
                            dve.wait_ge(gathered[k], i * 32 + 32)
                            nc.vector.tensor_tensor(top[:, k, :], scores[:, bass.ds(i * 4 + k, 1), :].rearrange("p o h -> p (o h)"), top[:, k, :],
                                                    ALU.subtract).then_inc(shifted, 1)
                        for n in range(2):
                            k = pair + n
                            dve.wait_ge(exped, i * 4 + k + 1)
                            nc.vector.tensor_tensor(term[:, k, 0:D].rearrange("p (h e) -> p h e", e=HEAD), v_in[:, k, :].rearrange("p (h e) -> p h e", e=HEAD),
                                                    term[:, k, D:SUMS].unsqueeze(2).to_broadcast([P, HEADS, HEAD]), ALU.mult).then_inc(term_ready, 1)


def average_segments(nc, st, stage, sum_table, dst):
    view = sum_table[0:SEGMENTS, :].rearrange("(t p r) f -> t p r f", p=P, r=RELATIONS)
    with ExitStack() as ctx:
        sb, ps, sem = tools(nc, ctx, stage)
        s = sb("sums_in", [P, 2, RELATIONS, SUMS])
        inverse = sb("inverse", [P, RELATIONS, HEADS])
        present = sb("present", [P, RELATIONS])
        count = sb("count", [P, 1])
        loaded = [sem(f"loaded{k}") for k in range(2)]
        chain, used = sem("chain"), sem("used")
        with nc.Block() as block:

            @block.sync
            def _(sp):
                for t in range(TILES):
                    if t >= 2:
                        sp.wait_ge(used, t - 1)
                    sp.dma_start(s[:, t % 2, :, :], view[t]).then_inc(loaded[t % 2], 16)

            @block.vector
            def _(dve):
                link = Chain(dve, chain)
                for t in range(TILES):
                    dve.wait_ge(loaded[t % 2], 16 * (t // 2 + 1))
                    weights = s[:, t % 2, :, D:SUMS]
                    link.mark(nc.vector.tensor_scalar(present[:, :], weights[:, :, 0], 0.0, None, ALU.is_gt))
                    link(nc.vector.tensor_scalar(inverse[:, :, :], weights, 1e-30, None, ALU.max))
                    link.mark(nc.vector.tensor_reduce(count[:, :], present[:, :], AX, ALU.add))
                    link(nc.vector.reciprocal(inverse[:, :, :], inverse[:, :, :]))
                    link(nc.vector.tensor_scalar(count[:, :], count[:, :], 1.0, None, ALU.max))
                    link(nc.vector.reciprocal(count[:, :], count[:, :]))
                    own = s[:, t % 2, :, 0:D].rearrange("p r (h e) -> p r h e", e=HEAD)
                    link(nc.vector.tensor_tensor(own, own, inverse[:, :, :].unsqueeze(3).to_broadcast([P, RELATIONS, HEADS, HEAD]), ALU.mult))
                    nc.vector.tensor_reduce(dst[:, t, :], s[:, t % 2, :, 0:D].rearrange("p r f -> p f r"), AX, ALU.add).then_inc(used, 1)
                    dve.wait_ge(used, t + 1)
                    link(nc.vector.tensor_scalar(dst[:, t, :], dst[:, t, :], count[:, 0:1], None, ALU.mult))


def blend_nodes(nc, st, stage, trans, keep):
    with ExitStack() as ctx:
        sb, ps, sem = tools(nc, ctx, stage)
        rest = sb("rest", [P, TILES])
        chain = sem("chain")
        with nc.Block() as block:

            @block.vector
            def _(dve):
                link = Chain(dve, chain)
                link(nc.vector.tensor_scalar(rest[:, :], keep[:, :], -1.0, 1.0, ALU.mult, ALU.add))
                for t in range(TILES):
                    link.mark(nc.vector.scalar_tensor_tensor(out=st.x[:, t, :], in0=trans[:, t, :], scalar=keep[:, t:t + 1],
                                                             in1=st.x[:, t, :], op0=ALU.mult, op1=ALU.add))
                link.settle()
                for t in range(TILES):
                    link.mark(nc.vector.scalar_tensor_tensor(out=st.x[:, t, :], in0=st.a[:, t, :], scalar=rest[:, t:t + 1],
                                                             in1=st.x[:, t, :], op0=ALU.mult, op1=ALU.add))


def layer2_gnn(nc, st, d):
    dram = lambda name, rows, cols: nc.dram_tensor(name, (rows, cols), F32, kind="Internal").ap()
    q_table = dram("query_rows", NP, D)
    k_table = dram("key_rows", SEGMENTS, D)
    v_table = dram("value_rows", SEGMENTS, D)
    max_table = dram("segment_maxima", SEGMENTS + P, HEADS)
    sum_table = dram("segment_sums", SEGMENTS + P, SUMS)
    cols = edge_columns(d["src"].shape[0])
    norm_nodes(nc, st, "l2_norm", st.x, st.a, True)
    fill_table(nc, "l2_max_fill", max_table, FAR, 1)
    fill_table(nc, "l2_sum_fill", sum_table, 0.0, 6)
    with ExitStack() as ctx:
        sb, ps, sem = tools(nc, ctx, "l2")
        type_masks, keep = sb("type_masks", [P, TYPES, TILES]), sb("keep", [P, TILES])
        load_types(nc, st, "l2_types", d["node_type_4"], d["L2_gnn_skip"], type_masks, keep)
        with ExitStack() as values:
            v = values.enter_context(nc.sbuf_tensor("l2_values", [P, TILES, D], F32))
            typed_linear(nc, st, "l2_query", type_masks, d["L2_gnn_Wq"], d["L2_gnn_bq"], st.b)
            store_rows(nc, st, "l2_query_rows", st.b, q_table)
            typed_linear(nc, st, "l2_value", type_masks, d["L2_gnn_Wv"], d["L2_gnn_bv"], v)
            typed_linear(nc, st, "l2_key", type_masks, d["L2_gnn_Wk"], d["L2_gnn_bk"], st.b)
            transpose_nodes(nc, st, "l2_turn_key", st.b)
            relate_rows(nc, st, "l2_relate_key", d["L2_gnn_rel_att"], d["L2_gnn_rel_pri"], k_table)
            transpose_nodes(nc, st, "l2_turn_value", v)
            relate_rows(nc, st, "l2_relate_value", d["L2_gnn_rel_msg"], None, v_table)
        with ExitStack() as edges:
            own = lambda name, shape, dt=F32: edges.enter_context(nc.sbuf_tensor(f"l2_{name}", shape, dt))
            wide = [P, cols + AHEAD]
            lists = (own("src_rows", wide, I32), own("segment", wide, I32), own("segment_f", wide), own("dst", wide, I32))
            cells, scores = own("cells", [P, cols], I32), own("scores", [P, cols, HEADS])
            edge_lists(nc, st, "l2_lists", d["src"], d["dst"], d["edge_type_8"], lists)
            segment_maxima(nc, st, "l2_maxima", lists, cells, scores, q_table, k_table, max_table)
            segment_sums(nc, st, "l2_sums", lists, cells, scores, v_table, max_table, sum_table)
        average_segments(nc, st, "l2_average", sum_table, st.b)
        transpose_nodes(nc, st, "l2_turn_average", st.b)
        typed_linear(nc, st, "l2_out", type_masks, d["L2_gnn_Wa"], d["L2_gnn_ba"], st.b)
        blend_nodes(nc, st, "l2_blend", st.b, keep)


def score_experts(nc, st, stage, agg, gamma, beta, scores, heads, experts):
    W = heads * experts
    with ExitStack() as ctx:
        sb, ps, sem = tools(nc, ctx, stage)
        g, b = sb("gamma", [P, W]), sb("beta", [P, W])
        mean, rstd = sb("mean", [P, TILES]), sb("rstd", [P, TILES])
        square = sb("square", [P, TILES, W])
        loaded, chain, floored, rooted = sem("loaded"), sem("chain"), sem("floored"), sem("rooted")
        with nc.Block() as block:

            @block.sync
            def _(sp):
                sp.dma_start(g[:, :], gamma.partition_broadcast(P)).then_inc(loaded, 16)
                sp.dma_start(b[:, :], beta.partition_broadcast(P)).then_inc(loaded, 16)

            @block.scalar
            def _(act):
                act.wait_ge(floored, 1)
                nc.scalar.activation(rstd[:, :], rstd[:, :], ACT.Sqrt).then_inc(rooted, 1)

            @block.vector
            def _(dve):
                link = Chain(dve, chain)
                by_node = lambda a: a[:, :].unsqueeze(2).to_broadcast([P, TILES, W])
                by_column = lambda a: a[:, :].unsqueeze(1).to_broadcast([P, TILES, W])
                v = agg[:, :, :]
                link(nc.vector.tensor_reduce(mean[:, :], v, AX, ALU.add))
                link(nc.vector.tensor_scalar(mean[:, :], mean[:, :], 1.0 / W, None, ALU.mult))
                link(nc.vector.tensor_tensor(v, v, by_node(mean), ALU.subtract))
                link(nc.vector.tensor_tensor(square[:, :, :], v, v, ALU.mult))
                link(nc.vector.tensor_reduce(rstd[:, :], square[:, :, :], AX, ALU.add))
                nc.vector.tensor_scalar(rstd[:, :], rstd[:, :], 1.0 / W, LN_EPS, ALU.mult, ALU.add).then_inc(floored, 1)
                dve.wait_ge(rooted, 1)
                link(nc.vector.reciprocal(rstd[:, :], rstd[:, :]))
                link(nc.vector.tensor_tensor(v, v, by_node(rstd), ALU.mult))
                dve.wait_ge(loaded, 32)
                link(nc.vector.tensor_tensor(v, v, by_column(g), ALU.mult))
                link(nc.vector.tensor_tensor(v, v, by_column(b), ALU.add))
                link(nc.vector.tensor_reduce(scores[:, :, :], agg[:, :, :].rearrange("p t (h e) -> p t e h", h=heads), AX, ALU.add))
                link(nc.vector.tensor_scalar(scores[:, :, :], scores[:, :, :], 1.0 / heads, None, ALU.mult))


def mixture(nc, st, stage, ex, acc, given=None):
    with ExitStack() as ctx:
        gates = ctx.enter_context(nc.sbuf_tensor(f"{stage}_gates", [P, ex.experts, TILES], F32))
        gate_nodes(nc, st, stage + "_gate", ex, gates, given)
        mix_experts(nc, st, stage + "_mix", ex, gates, acc)


def layer0_ffn(nc, st, d):
    ex = Experts(16, 512, d["L0_ffn_gate_w"], d["L0_ffn_gate_b"], [(d["L0_ffn_w1"], d["L0_ffn_b1"])],
                 d["L0_ffn_w2"], d["L0_ffn_b2"], True, ACT.Relu)
    norm_nodes(nc, st, "f0_norm", st.x, st.a, True)
    mixture(nc, st, "f0", ex, st.a)
    norm_add(nc, st, "f0_add", d["L0_ffn_gamma"], d["L0_ffn_beta"])


def layer1_ffn(nc, st, d):
    ex = Experts(8, 512, d["L1_ffn_Wg"], d["L1_ffn_bg"], [(d["L1_ffn_W1"], d["L1_ffn_b1"])],
                 d["L1_ffn_W2"], d["L1_ffn_b2"], True, ACT.Relu, router_bias2=d["L1_ffn_bias"])
    norm_nodes(nc, st, "f1_norm", st.x, st.a, True)
    mixture(nc, st, "f1", ex, st.x)


def layer2_ffn(nc, st, d):
    norms = [[d[f"L2_ffn_{a}{l}"] for a in ("g", "be", "m", "v")] for l in (1, 2)]
    ex = Experts(8, 256, d["L2_ffn_Wr"], d["L2_ffn_br"],
                 [(d["L2_ffn_W1"], d["L2_ffn_b1"]), (d["L2_ffn_W2"], d["L2_ffn_b2"])],
                 d["L2_ffn_Wo"], d["L2_ffn_bo"], False, ACT.Relu, norms=norms)
    norm_nodes(nc, st, "f2_norm", st.x, st.a, True)
    mixture(nc, st, "f2", ex, st.x)


def layer3_ffn(nc, st, d, table, mask):
    heads, experts = d["L3_ffn_att_src"].shape
    ex = Experts(experts, 512, None, None, [(d["L3_ffn_W1"], d["L3_ffn_b1"])],
                 d["L3_ffn_W2"], d["L3_ffn_b2"], True, ACT.Gelu)
    norm_nodes(nc, st, "f3_norm", st.x, st.a, True)
    att = Attention(st, heads, experts)
    with ExitStack() as ctx:
        sb, ps, sem = tools(nc, ctx, "f3")
        agg, scores = sb("agg", [P, TILES, heads * experts]), sb("expert_scores", [P, TILES, experts])
        attend(nc, st, "f3a", att, table, mask, d["L3_ffn_W_gat"], d["L3_ffn_att_src"], d["L3_ffn_att_dst"],
               Averaged(att, agg, d["L3_ffn_b_gat"]))
        score_experts(nc, st, "f3_scores", agg, d["L3_ffn_ln_gamma"], d["L3_ffn_ln_beta"], scores, heads, experts)
        transpose_nodes(nc, st, "f3_turn", st.a)
        mixture(nc, st, "f3", ex, st.x, given=scores)


def network(nc, d, out):
    SEMAPHORES.__init__()
    with ExitStack() as ctx:
        dram = lambda name, shape, dt=F32: nc.dram_tensor(name, shape, dt, kind="Internal").ap()
        count_table, weight_table, count_table2 = (dram(n, (CELLS, 1)) for n in ("edge_counts", "edge_weights", "edge_counts2"))
        mask, mask2 = dram("edge_mask", (NP, NP), BF16), dram("edge_mask2", (NP, NP), BF16)
        st = State(nc, ctx, d)
        load_nodes(nc, st, "load", d["x"])
        clear_tables(nc, "clear", [count_table, weight_table, count_table2])
        pairs = d["L3_ffn_edge_index"]
        build_tables(nc, st, "build", d["src"], d["dst"], d["edge_weight"], pairs[0, :], pairs[1, :],
                     count_table, weight_table, count_table2)
        build_masks(nc, st, "mask", count_table, mask)
        build_masks(nc, st, "mask2", count_table2, mask2)
        degree_factors(nc, st, "factors")
        layer0_gnn(nc, st, d, count_table)
        layer0_ffn(nc, st, d)
        layer1_gnn(nc, st, d, weight_table)
        layer1_ffn(nc, st, d)
        layer2_gnn(nc, st, d)
        layer2_ffn(nc, st, d)
        layer3_gnn(nc, st, d, count_table, mask)
        layer3_ffn(nc, st, d, count_table2, mask2)
        store_nodes(nc, st, "store", out)
        SEMAPHORES.clear(nc)




def kernel(**inputs):
    import numpy as _np
    import concourse.bacc as _bacc
    from concourse import mybir as _mybir
    from concourse.bass_utils import run_bass_kernel_spmd as _run

    nc = _bacc.Bacc("TRN2", target_bir_lowering=False, num_devices=1)
    arrays, d = {}, {}
    for name, value in inputs.items():
        a = _np.ascontiguousarray(value)
        arrays[f"in_{name}"] = a
        d[name] = nc.dram_tensor(f"in_{name}", a.shape, _mybir.dt.from_np(a.dtype), kind="ExternalInput").ap()
    out = nc.dram_tensor("out_nodes", inputs["x"].shape, _mybir.dt.float32, kind="ExternalOutput").ap()
    network(nc, d, out)
    r = _run(nc, [arrays], core_ids=[0])
    return r.results[0]["out_nodes"]
```

```python
from contextlib import ExitStack

import numpy as np

import concourse.bass as bass
from concourse import mybir

P = 128
N = 3125
D = 256
TILES = (N + P - 1) // P
NP = TILES * P
LAST = N - (TILES - 1) * P
KC = D // P
CHUNK = 512
CHUNKS = [(c, min(CHUNK, NP - c)) for c in range(0, NP, CHUNK)]

F32 = mybir.dt.float32
BF16 = mybir.dt.bfloat16
I32 = mybir.dt.int32
ALU = mybir.AluOpType
ACT = mybir.ActivationFunctionType
AX = mybir.AxisListType.X
LN_EPS = 1e-5


class Chain:

    def __init__(self, eng, sem, base=0):
        self.eng, self.sem, self.n = eng, sem, base

    def __call__(self, instruction):
        instruction.then_inc(self.sem, 1)
        self.n = self.n + 1
        self.eng.wait_ge(self.sem, self.n)

    def mark(self, instruction):
        instruction.then_inc(self.sem, 1)
        self.n = self.n + 1

    def settle(self):
        self.eng.wait_ge(self.sem, self.n)


class Semaphores:

    MOST = 100

    def __init__(self):
        self.held, self.stack, self.kept = [], ExitStack(), ExitStack()

    def take(self, nc, ctx, stage, begins=True):
        if begins and len(self.held) > self.MOST:
            self.clear(nc)

        def sem(name, pool_dma=False):
            if pool_dma:
                return self.kept.enter_context(nc.semaphore(f"{stage}_{name}"))
            self.held.append(self.stack.enter_context(nc.semaphore(f"{stage}_{name}")))
            return self.held[-1]

        return sem

    def clear(self, nc):
        held = sorted(s.num for s in self.held)
        with nc.Block() as block:

            @block.sync
            def _(sp):
                at = 0
                for n in range(1, len(held) + 1):
                    if n == len(held) or held[n] != held[n - 1] + 1:
                        sp.sem_clear(range(held[at], held[n - 1] + 1))
                        at = n
        self.stack.close()
        self.held = []


SEMAPHORES = Semaphores()


class State:

    def __init__(self, nc, ctx, dram):
        self.nc, self.dram = nc, dram
        sb = lambda name, shape, dt=F32: ctx.enter_context(nc.sbuf_tensor(name, shape, dt))
        self.x = sb("residual", [P, TILES, D])
        self.a = sb("nodes_a", [P, TILES, D])
        self.aT = sb("nodes_transposed", [P, KC, NP])
        self.b_flat = sb("nodes_b", [P, TILES * (D + 4)])
        self.b = self.b_flat[:, 0:TILES * D].rearrange("p (t d) -> p t d", d=D)
        self.ident = sb("identity", [P, P])
        self.ones_row = sb("ones_row", [1, CHUNK])
        self.deg_out = sb("out_degree", [P, TILES])
        self.deg_in = sb("in_degree", [P, TILES])
        self.deg_weight = sb("out_weight", [P, TILES])
        self.node_type = sb("node_type", [P, TILES])


def tools(nc, ctx, stage):
    sb = lambda name, shape, dt=F32: ctx.enter_context(nc.sbuf_tensor(f"{stage}_{name}", shape, dt))
    ps = lambda name, shape, dt=F32: ctx.enter_context(nc.psum_tensor(f"{stage}_{name}", shape, dt))
    sem = SEMAPHORES.take(nc, ctx, stage)
    return sb, ps, sem


def load_nodes(nc, st, stage, x):
    with ExitStack() as ctx:
        sb, ps, sem = tools(nc, ctx, stage)
        cleared, loaded, ident_ready = sem("cleared"), sem("loaded"), sem("ident_ready")
        with nc.Block() as block:

            @block.vector
            def _(dve):
                nc.vector.memset(st.x[:, TILES - 1, :], 0.0).then_inc(cleared, 1)
                nc.vector.memset(st.ones_row[:, :], 1.0).then_inc(cleared, 1)

            @block.sync
            def _(sp):
                full = N - LAST
                sp.dma_start(st.x[:, 0:TILES - 1, :], x[0:full, :].rearrange("(t p) f -> p t f", p=P)).then_inc(loaded, 16)
                sp.wait_ge(cleared, 2)
                sp.dma_start(st.x[0:LAST, TILES - 1, :], x[full:N, :]).then_inc(loaded, 16)
                sp.wait_ge(loaded, 32)

            @block.gpsimd
            def _(pool):
                nc.gpsimd.memset(st.ident[:, :], 0.0).then_inc(ident_ready, 1)
                pool.wait_ge(ident_ready, 1)
                nc.gpsimd.affine_select(out=st.ident[:, :], in_=st.ident[:, :], compare_op=ALU.not_equal, fill=1.0,
                                        base=0, pattern=[[-1, P]], channel_multiplier=1).then_inc(ident_ready, 1)
                pool.wait_ge(ident_ready, 2)


def store_nodes(nc, st, stage, out):
    with ExitStack() as ctx:
        sb, ps, sem = tools(nc, ctx, stage)
        stored = sem("stored")
        with nc.Block() as block:

            @block.sync
            def _(sp):
                full = N - LAST
                sp.dma_start(out[0:full, :].rearrange("(t p) f -> p t f", p=P), st.x[:, 0:TILES - 1, :]).then_inc(stored, 16)
                sp.dma_start(out[full:N, :], st.x[0:LAST, TILES - 1, :]).then_inc(stored, 16)
                sp.wait_ge(stored, 32)


def norm_nodes(nc, st, stage, src, dst, transpose, scale=None):
    with ExitStack() as ctx:
        sb, ps, sem = tools(nc, ctx, stage)
        stats = sb("stats", [P, TILES, 6])
        moments = sb("moments", [P, TILES, 2])
        rstd = sb("rstd", [P, TILES])
        factor = sb("factor", [P, TILES])
        turned = ps("turned", [P, 4, 4, P])
        chain, normed, transposed, copied = sem("chain"), sem("normed"), sem("transposed"), sem("copied")
        moments_ready, rooted = sem("moments_ready"), sem("rooted")
        with nc.Block() as block:

            @block.vector
            def _(dve):
                link = Chain(dve, chain)
                for t in range(TILES):
                    link.mark(nc.vector.bn_stats(stats[:, t, :], src[:, t, :]))
                link.settle()
                for t in range(TILES):
                    link.mark(nc.vector.bn_aggr(moments[:, t, :], stats[:, t, :]))
                link.settle()
                nc.vector.tensor_scalar(rstd[:, :], moments[:, :, 1], LN_EPS, None, ALU.add).then_inc(moments_ready, 1)
                if scale is not None:
                    nc.vector.tensor_scalar(factor[:, :], scale[:, :], 1.0, None, ALU.max).then_inc(moments_ready, 1)
                dve.wait_ge(rooted, 2 if scale is not None else 1)
                link(nc.vector.reciprocal(rstd[:, :], rstd[:, :]))
                if scale is not None:
                    link(nc.vector.reciprocal(factor[:, :], factor[:, :]))
                    link(nc.vector.tensor_tensor(rstd[:, :], rstd[:, :], factor[:, :], ALU.mult))
                for t in range(TILES):
                    nc.vector.tensor_scalar(dst[:, t, :], src[:, t, :], moments[:, t, 0:1], rstd[:, t:t + 1],
                                            ALU.subtract, ALU.mult).then_inc(normed, 1)

            if transpose:
                @block.tensor
                def _(pe):
                    for t in range(TILES):
                        pe.wait_ge(normed, t + 1)
                        if t >= 4:
                            pe.wait_ge(copied, t - 3)
                        for c in range(KC):
                            last = nc.tensor.transpose(turned[:, t % 4, c, :], dst[:, t, c * P:(c + 1) * P], st.ident[:, :])
                        last.then_inc(transposed, 1)

            @block.scalar
            def _(act):
                act.wait_ge(moments_ready, 1)
                nc.scalar.activation(rstd[:, :], rstd[:, :], ACT.Sqrt).then_inc(rooted, 1)
                if scale is not None:
                    act.wait_ge(moments_ready, 2)
                    nc.scalar.activation(factor[:, :], factor[:, :], ACT.Sqrt).then_inc(rooted, 1)
                if transpose:
                    for t in range(TILES):
                        act.wait_ge(transposed, t + 1)
                        nc.scalar.copy(st.aT[:, :, t * P:(t + 1) * P], turned[:, t % 4, 0:KC, :]).then_inc(copied, 1)


def transpose_nodes(nc, st, stage, src):
    with ExitStack() as ctx:
        sb, ps, sem = tools(nc, ctx, stage)
        turned = ps("turned", [P, 4, 4, P])
        transposed, copied_by_act, copied_by_dve = sem("transposed"), sem("copied_by_act"), sem("copied_by_dve")
        with nc.Block() as block:

            @block.tensor
            def _(pe):
                for t in range(TILES):
                    if t >= 4:
                        pe.wait_ge((copied_by_act, copied_by_dve)[t % 2], (t - 4) // 2 + 1)
                    for c in range(KC):
                        last = nc.tensor.transpose(turned[:, t % 4, c, :], src[:, t, c * P:(c + 1) * P], st.ident[:, :])
                    last.then_inc(transposed, 1)

            @block.scalar
            def _(act):
                for t in range(0, TILES, 2):
                    act.wait_ge(transposed, t + 1)
                    nc.scalar.copy(st.aT[:, :, t * P:(t + 1) * P], turned[:, t % 4, 0:KC, :]).then_inc(copied_by_act, 1)

            @block.vector
            def _(dve):
                for t in range(1, TILES, 2):
                    dve.wait_ge(transposed, t + 1)
                    nc.vector.tensor_copy(st.aT[:, :, t * P:(t + 1) * P], turned[:, t % 4, 0:KC, :]).then_inc(copied_by_dve, 1)


def linear_nodes(nc, st, stage, weight, bias, width, finish):
    with ExitStack() as ctx:
        sb, ps, sem = tools(nc, ctx, stage)
        w = sb("weight", [P, KC, width])
        b = sb("bias", [1, width]) if bias is not None else None
        acc = ps("acc", [P, 4, CHUNK])
        loaded, chain, multiplied, finished = sem("loaded"), sem("chain"), sem("multiplied"), sem("finished")
        extra = finish.prepare(nc, ctx, stage) if hasattr(finish, "prepare") else None
        with nc.Block() as block:

            @block.sync
            def _(sp):
                sp.dma_start(w[:, :, :], weight.rearrange("(c p) m -> p c m", p=P)).then_inc(loaded, 16)
                if b is not None:
                    sp.dma_start(b[0:1, :], bias.rearrange("(o m) -> o m", o=1)).then_inc(loaded, 16)

            @block.tensor
            def _(pe):
                pe.wait_ge(loaded, 16 if b is None else 32)
                for t in range(TILES):
                    if t >= 4:
                        pe.wait_ge(finished, t - 3)
                    for c in range(KC):
                        last = nc.tensor.matmul(acc[:, t % 4, 0:width], st.aT[:, c, t * P:(t + 1) * P], w[:, c, :],
                                                start=(c == 0), stop=(b is None and c == KC - 1))
                    if b is not None:
                        last = nc.tensor.matmul(acc[:, t % 4, 0:width], st.ones_row[0:1, 0:P], b[0:1, :],
                                                start=False, stop=True)
                    last.then_inc(multiplied, 1)

            @block.vector
            def _(dve):
                link = Chain(dve, chain)
                for t in range(TILES):
                    dve.wait_ge(multiplied, t + 1)
                    finish(nc, link, t, acc[:, t % 4, 0:width], extra).then_inc(finished, 1)


def route_top2(nc, link, v, experts, logits, gates):
    shape = [P, TILES, experts]
    wide = lambda a: a.unsqueeze(2).to_broadcast(shape)
    top1, top2, m, hot1, hot2, work, rank = v
    link(nc.vector.tensor_reduce(top1[:, :], logits[:, :, :], AX, ALU.max))
    source, top = logits, top1
    for hot in (hot1, hot2):
        link(nc.vector.tensor_tensor(work[:, :, :], source[:, :, :], wide(top[:, :]), ALU.is_equal))
        link(nc.vector.tensor_tensor(work[:, :, :], work[:, :, :], rank[:, :, :], ALU.mult))
        link(nc.vector.tensor_reduce(m[:, :], work[:, :, :], AX, ALU.max))
        link(nc.vector.tensor_tensor(hot[:, :, :], work[:, :, :], wide(m[:, :]), ALU.is_equal))
        if hot is hot1:
            link(nc.vector.scalar_tensor_tensor(out=gates[:, :, :], in0=hot1[:, :, :], scalar=-3e38,
                                                in1=logits[:, :, :], op0=ALU.mult, op1=ALU.add))
            link(nc.vector.tensor_reduce(top2[:, :], gates[:, :, :], AX, ALU.max))
            source, top = gates, top2
    link(nc.vector.tensor_tensor(top2[:, :], top2[:, :], top1[:, :], ALU.subtract))


class Experts:

    def __init__(self, experts, hidden, router, router_bias, layers, w_out, b_out, top2, func, norms=None, router_bias2=None):
        self.experts, self.hidden, self.router, self.router_bias = experts, hidden, router, router_bias
        self.layers, self.w_out, self.b_out, self.top2, self.func = layers, w_out, b_out, top2, func
        self.norms, self.router_bias2 = norms, router_bias2


def gate_nodes(nc, st, stage, ex, gates, given=None):
    E = ex.experts
    with ExitStack() as ctx:
        sb, ps, sem = tools(nc, ctx, stage)
        w = sb("router", [P, KC, E])
        b = sb("router_bias", [1, 2, E])
        logits = sb("logits", [P, TILES, E])
        g = sb("g", [P, TILES, E])
        v = [sb(n, [P, TILES]) for n in ("top1", "top2", "m")]
        v += [sb(n, [P, TILES, E]) for n in ("hot1", "hot2", "work", "rank")]
        ranks = sb("ranks", [P, E], I32)
        acc = ps("acc", [P, 512])
        acc3 = acc[:, 0:TILES * E].rearrange("p (t e) -> p t e", e=E)
        loaded, chain, multiplied, ranked, shifted, exped = (
            sem(n) for n in ("loaded", "chain", "multiplied", "ranked", "shifted", "exped"))
        biases = [] if given is not None else [ex.router_bias] + ([ex.router_bias2] if ex.router_bias2 is not None else [])
        with nc.Block() as block:

            @block.sync
            def _(sp):
                if given is not None:
                    return
                sp.dma_start(w[:, :, :], ex.router.rearrange("(c p) m -> p c m", p=P)).then_inc(loaded, 16)
                for k, bias in enumerate(biases):
                    sp.dma_start(b[0:1, k, :], bias.rearrange("(o m) -> o m", o=1)).then_inc(loaded, 16)

            @block.gpsimd
            def _(pool):
                nc.gpsimd.iota(ranks[:, :], pattern=[[-1, E]], base=E, channel_multiplier=0).then_inc(ranked, 1)

            @block.tensor
            def _(pe):
                if given is not None:
                    return
                pe.wait_ge(loaded, 16 * (1 + len(biases)))
                for t in range(TILES):
                    for c in range(KC):
                        nc.tensor.matmul(acc3[:, t, :], st.aT[:, c, t * P:(t + 1) * P], w[:, c, :],
                                         start=(c == 0), stop=False)
                    for k in range(len(biases)):
                        last = nc.tensor.matmul(acc3[:, t, :], st.ones_row[0:1, 0:P], b[0:1, k, :],
                                                start=False, stop=(k == len(biases) - 1))
                last.then_inc(multiplied, 1)

            @block.scalar
            def _(act):
                act.wait_ge(shifted, 1)
                if ex.top2:
                    nc.scalar.activation(v[1][:, :], v[1][:, :], ACT.Exp).then_inc(exped, 1)
                else:
                    nc.scalar.activation(g[:, :, :], g[:, :, :], ACT.Exp).then_inc(exped, 1)

            @block.vector
            def _(dve):
                link = Chain(dve, chain)
                wide = lambda a: a.unsqueeze(2).to_broadcast([P, TILES, E])
                top1, top2, m, hot1, hot2, work, rank = v
                dve.wait_ge(ranked, 1)
                link(nc.vector.tensor_copy(rank[:, :, :], ranks[:, :].unsqueeze(1).to_broadcast([P, TILES, E])))
                if given is None:
                    dve.wait_ge(multiplied, 1)
                link(nc.vector.tensor_copy(logits[:, :, :], acc3 if given is None else given[:, :, :]))
                if ex.top2:
                    route_top2(nc, link, v, E, logits, g)
                    nc.vector.tensor_copy(m[:, :], m[:, :]).then_inc(shifted, 1)
                    link.mark(nc.vector.tensor_copy(gates.hot[:, 0, :, :], hot1[:, :, :]))
                    link.mark(nc.vector.tensor_copy(gates.hot[:, 1, :, :], hot2[:, :, :]))
                    dve.wait_ge(exped, 1)
                    link(nc.vector.tensor_scalar(m[:, :], top2[:, :], 1.0, None, ALU.add))
                    link(nc.vector.reciprocal(gates.gate[:, 0, :], m[:, :]))
                    link(nc.vector.tensor_tensor(gates.gate[:, 1, :], gates.gate[:, 0, :], top2[:, :], ALU.mult))
                else:
                    link(nc.vector.tensor_reduce(m[:, :], logits[:, :, :], AX, ALU.max))
                    nc.vector.tensor_tensor(g[:, :, :], logits[:, :, :], wide(m[:, :]), ALU.subtract).then_inc(shifted, 1)
                    dve.wait_ge(exped, 1)
                    link(nc.vector.tensor_reduce(m[:, :], g[:, :, :], AX, ALU.add))
                    link(nc.vector.reciprocal(m[:, :], m[:, :]))
                    link(nc.vector.tensor_tensor(gates[:, :, :].rearrange("p e t -> p t e"), g[:, :, :], wide(m[:, :]), ALU.mult))


def mix_experts(nc, st, stage, ex, gates, acc):
    E, H = ex.experts, ex.hidden
    HC = H // P
    L = len(ex.layers)
    with ExitStack() as ctx:
        sb, ps, sem = tools(nc, ctx, stage)
        w_first = sb("w_first", [P, 2, KC, H])
        w_mid = sb("w_mid", [P, 2, HC, H]) if L == 2 else None
        w_last = sb("w_last", [P, 2, HC, D])
        b_hidden = sb("b_hidden", [P, 2, L, HC])
        bn = sb("bn", [P, L, 5, E, HC]) if ex.norms else None
        scale_all = sb("scale_all", [P, L, E, HC]) if ex.norms else None
        shift_all = sb("shift_all", [P, L, E, HC]) if ex.norms else None
        bn_scale = sb("bn_scale", [P, 2, L, HC]) if ex.norms else None
        bn_shift = sb("bn_shift", [P, 2, L, HC]) if ex.norms else None
        b_last = sb("b_last", [E, D])
        gatesT = sb("gates_transposed", [E, NP])
        gate_now = sb("gate_now", [P, 2, TILES])
        hidden = [sb(f"hidden{l}", [P, 2, HC, CHUNK]) for l in range(L)]
        pre = ps("pre", [P, 4, CHUNK])
        post = ps("post", [P, 4, CHUNK])
        loads = 2 + L + (1 if L == 2 else 0) 
        weights_loaded = [sem(f"weights_loaded{k}") for k in range(2)]
        bias_loaded, pre_ready, pre_used, post_ready, post_used, chain, act_chain, turned, gate_copied, bn_ready = (
            sem(n) for n in ("bias_loaded", "pre_ready", "pre_used", "post_ready", "post_used", "chain",
                             "act_chain", "turned", "gate_copied", "bn_ready"))
        bn_loaded, bn_rooted = sem("bn_loaded"), sem("bn_rooted")
        NC = len(CHUNKS)
        steps = [(l, s - l) for s in range(NC + L) for l in range(L + 1) if 0 <= s - l < NC]
        place, placed = {}, 0
        for l, q in steps:
            if l < L:
                place[l, q] = placed
                placed += HC
        with nc.Block() as block:

            @block.sync
            def _(sp):
                sp.dma_start(b_last[:, :], ex.b_out).then_inc(bias_loaded, 16)
                if ex.norms:
                    for l in range(L):
                        for n, a in enumerate([*ex.norms[l], ex.layers[l][1]]):
                            sp.dma_start(bn[:, l, n, :, :], a.rearrange("e (p j) -> p e j", p=P)).then_inc(bn_loaded, 16)
                with sp.Fori(0, E // 2) as i:
                    for k in range(2):
                        sp.wait_ge(post_ready, (i * 2 + k) * TILES + 1)
                        e = i * 2 + k
                        one = lambda a: a[bass.ds(e, 1)]
                        sp.dma_start(w_first[:, k, :, :], one(ex.layers[0][0]).rearrange("o (c p) h -> p (o c) h", p=P)).then_inc(weights_loaded[k], 16)
                        sp.dma_start(w_last[:, k, :, :], one(ex.w_out).rearrange("o (p j) d -> p (o j) d", p=P)).then_inc(weights_loaded[k], 16)
                        for l in range(L):
                            sp.dma_start(b_hidden[:, k, l, :], one(ex.layers[l][1]).rearrange("o (p j) -> p (o j)", p=P)).then_inc(weights_loaded[k], 16)
                        if L == 2:
                            sp.dma_start(w_mid[:, k, :, :], one(ex.layers[1][0]).rearrange("o (p j) h -> p (o j) h", p=P)).then_inc(weights_loaded[k], 16)

            @block.tensor
            def _(pe):
                for t in range(TILES):
                    if t >= 4:
                        pe.wait_ge(post_used, t - 3)
                    nc.tensor.transpose(post[0:E, t % 4, 0:P], gates[:, :, t], st.ident[:, :]).then_inc(turned, 1)
                pe.wait_ge(bias_loaded, 16)
                pe.wait_ge(post_used, TILES)
                for t in range(TILES):
                    if t >= 4:
                        pe.wait_ge(post_used, TILES + t - 3)
                    nc.tensor.matmul(post[:, t % 4, 0:D], gatesT[:, t * P:(t + 1) * P], b_last[:, :],
                                     start=True, stop=True).then_inc(post_ready, 1)
                pe.wait_ge(post_used, 2 * TILES)
                pre_per, post_per = L * HC * NC, TILES
                with pe.Fori(0, E // 2) as i:
                    for k in range(2):
                        e = i * 2 + k
                        pe.wait_ge(weights_loaded[k], i * 16 * loads + 16 * loads)
                        for l, q in steps:
                            at, n = CHUNKS[q]
                            if l == L:
                                pe.wait_ge(pre_used, e * pre_per + 4 + place[L - 1, q] + HC)
                                for t in range(at // P, (at + n) // P):
                                    pe.wait_ge(post_used, e * post_per + 2 * TILES + (t - 3 if t >= 4 else 0))
                                    o = t * P - at
                                    for j in range(HC):
                                        last = nc.tensor.matmul(post[:, t % 4, 0:D], hidden[L - 1][:, q % 2, j, o:o + P], w_last[:, k, j, :],
                                                                start=(j == 0), stop=(j == HC - 1))
                                    last.then_inc(post_ready, 1)
                                continue
                            src = (lambda c: st.aT[:, c, at:at + n]) if l == 0 else (lambda c: hidden[l - 1][:, q % 2, c, 0:n])
                            w = w_first if l == 0 else w_mid
                            if l:
                                pe.wait_ge(pre_used, e * pre_per + 4 + place[l - 1, q] + HC)
                            for j in range(HC):
                                n_pre = place[l, q] + j
                                pe.wait_ge(pre_used, e * pre_per + n_pre + 1)
                                C = KC if l == 0 else HC
                                for c in range(C):
                                    last = nc.tensor.matmul(pre[:, n_pre % 4, 0:n], w[:, k, c, j:H:HC], src(c),
                                                            start=(c == 0), stop=(c == C - 1))
                                last.then_inc(pre_ready, 1)

            @block.scalar
            def _(act):
                if ex.norms:
                    act.wait_ge(bn_ready, 1)
                    nc.scalar.activation(scale_all[:, :, :, :], scale_all[:, :, :, :], ACT.Sqrt).then_inc(bn_rooted, 1)
                act.sem_inc(pre_used, 4)
                pre_per = L * HC * NC
                with act.Fori(0, E // 2) as i:
                    for k in range(2):
                        e = i * 2 + k
                        act.wait_ge(weights_loaded[k], i * 16 * loads + 16 * loads)
                        if ex.norms:
                            act.wait_ge(bn_ready, e + 2)
                        for l, q in steps:
                            if l == L:
                                continue
                            n = CHUNKS[q][1]
                            act.wait_ge(pre_used, e * pre_per + 4 + place[l, q])
                            for j in range(HC):
                                n_pre = place[l, q] + j
                                act.wait_ge(pre_ready, e * pre_per + n_pre + 1)
                                if ex.norms:
                                    bias, scale = bn_shift[:, k, l, j:j + 1], bn_scale[:, k, l, j:j + 1]
                                else:
                                    bias, scale = b_hidden[:, k, l, j:j + 1], 1.0
                                nc.scalar.activation(hidden[l][:, q % 2, j, 0:n], pre[:, n_pre % 4, 0:n], ex.func,
                                                     bias=bias, scale=scale).then_inc(pre_used, 1)

            @block.vector
            def _(dve):
                link = Chain(dve, chain)
                for t in range(TILES):
                    dve.wait_ge(turned, t + 1)
                    nc.vector.tensor_copy(gatesT[:, t * P:(t + 1) * P], post[0:E, t % 4, 0:P]).then_inc(post_used, 1)
                for t in range(TILES):
                    dve.wait_ge(post_ready, t + 1)
                    nc.vector.tensor_tensor(acc[:, t, :], acc[:, t, :], post[:, t % 4, 0:D], ALU.add).then_inc(post_used, 1)
                if ex.norms:
                    dve.wait_ge(bn_loaded, 16 * 5 * L)
                    nc.vector.tensor_scalar(scale_all[:, :, :, :], bn[:, :, 3, :, :], 1e-3, None, ALU.add).then_inc(bn_ready, 1)
                    dve.wait_ge(bn_rooted, 1)
                    link(nc.vector.reciprocal(scale_all[:, :, :, :], scale_all[:, :, :, :]))
                    g, be, m, v, b = (bn[:, :, n, :, :] for n in range(5))
                    link(nc.vector.tensor_tensor(scale_all[:, :, :, :], scale_all[:, :, :, :], g, ALU.mult))
                    link(nc.vector.tensor_tensor(shift_all[:, :, :, :], b, m, ALU.subtract))
                    link(nc.vector.tensor_tensor(shift_all[:, :, :, :], shift_all[:, :, :, :], scale_all[:, :, :, :], ALU.mult))
                    link(nc.vector.tensor_tensor(shift_all[:, :, :, :], shift_all[:, :, :, :], be, ALU.add))
                with dve.Fori(0, E // 2) as i:
                    for k in range(2):
                        e = i * 2 + k
                        copies = Chain(dve, gate_copied, e * (3 if ex.norms else 1))
                        dve.wait_ge(post_used, e * TILES + 2 * TILES)
                        if ex.norms:
                            dve.wait_ge(post_ready, e * TILES + TILES)
                            copies(nc.vector.tensor_copy(bn_scale[:, k, :, :], scale_all[:, :, bass.ds(e, 1), :].rearrange("p l o j -> p l (o j)")))
                            copies(nc.vector.tensor_copy(bn_shift[:, k, :, :], shift_all[:, :, bass.ds(e, 1), :].rearrange("p l o j -> p l (o j)")))
                            dve.sem_inc(bn_ready, 1)
                        copies(nc.vector.tensor_copy(gate_now[:, k, :], gates[:, bass.ds(e, 1), :].rearrange("p o t -> p (o t)")))
                        for t in range(TILES):
                            dve.wait_ge(post_ready, e * TILES + TILES + t + 1)
                            nc.vector.scalar_tensor_tensor(out=acc[:, t, :], in0=post[:, t % 4, 0:D],
                                                           scalar=gate_now[:, k, t:t + 1], in1=acc[:, t, :],
                                                           op0=ALU.mult, op1=ALU.add).then_inc(post_used, 1)


def norm_add(nc, st, stage, gamma, beta):
    with ExitStack() as ctx:
        sb, ps, sem = tools(nc, ctx, stage)
        g, b = sb("gamma", [P, D]), sb("beta", [P, D])
        stats, moments, rstd = sb("stats", [P, TILES, 6]), sb("moments", [P, TILES, 2]), sb("rstd", [P, TILES])
        loaded, chain, moments_ready, rooted = sem("loaded"), sem("chain"), sem("moments_ready"), sem("rooted")
        with nc.Block() as block:

            @block.sync
            def _(sp):
                sp.dma_start(g[:, :], gamma.partition_broadcast(P)).then_inc(loaded, 16)
                sp.dma_start(b[:, :], beta.partition_broadcast(P)).then_inc(loaded, 16)

            @block.scalar
            def _(act):
                act.wait_ge(moments_ready, 1)
                nc.scalar.activation(rstd[:, :], rstd[:, :], ACT.Sqrt).then_inc(rooted, 1)

            @block.vector
            def _(dve):
                link = Chain(dve, chain)
                for t in range(TILES):
                    link.mark(nc.vector.bn_stats(stats[:, t, :], st.a[:, t, :]))
                link.settle()
                for t in range(TILES):
                    link.mark(nc.vector.bn_aggr(moments[:, t, :], stats[:, t, :]))
                link.settle()
                nc.vector.tensor_scalar(rstd[:, :], moments[:, :, 1], LN_EPS, None, ALU.add).then_inc(moments_ready, 1)
                dve.wait_ge(rooted, 1)
                link(nc.vector.reciprocal(rstd[:, :], rstd[:, :]))
                dve.wait_ge(loaded, 32)
                for t in range(TILES):
                    link.mark(nc.vector.tensor_scalar(st.a[:, t, :], st.a[:, t, :], moments[:, t, 0:1], rstd[:, t:t + 1], ALU.subtract, ALU.mult))
                link.settle()
                wide = lambda w: w[:, :].unsqueeze(1).to_broadcast([P, TILES, D])
                link(nc.vector.tensor_tensor(st.a[:, :, :], st.a[:, :, :], wide(g), ALU.mult))
                link(nc.vector.tensor_tensor(st.x[:, :, :], st.x[:, :, :], wide(b), ALU.add))
                link(nc.vector.tensor_tensor(st.x[:, :, :], st.x[:, :, :], st.a[:, :, :], ALU.add))



PITCH = NP
SPARE = (NP + 1) * NP + 256
CELLS = (NP + 2) * NP
FAR = -1e30


def edge_columns(edges):
    return (edges + P - 1) // P


def build_tables(nc, st, stage, src, dst, weight, src2, dst2, count_table, weight_table, count_table2,
                 zero_tables, far_tables):
    edges, edges2 = src.shape[0], src2.shape[0]
    cols, cols2 = edge_columns(edges), edge_columns(edges2)
    RING = 4
    assert cols % RING == 0 and cols2 % RING == 0 and cols2 <= cols
    graphs = [(edges, cols, src, dst), (edges2, cols2, src2, dst2)]
    with ExitStack() as ctx:
        sb, ps, sem = tools(nc, ctx, stage)
        raw = [[sb(f"raw{g}{n}", [P, c[1]], I32) for n in ("src", "dst")] for g, c in enumerate(graphs)]
        digit = sb("digit", [P, cols], I32)
        ends = [[sb(f"ends{g}{n}", [P, c[1]]) for n in ("src", "dst")] for g, c in enumerate(graphs)]
        keys = [sb("keys0", [P, 2, cols]), sb("keys1", [P, 1, cols2])]
        low = [sb(f"low{n}", [P, cols]) for n in ("src", "dst")]
        high = [sb(f"high{n}", [P, cols]) for n in ("src", "dst")]
        ew = sb("edge_weight", [P, cols])
        iota_i = sb("iota_i", [P, P], I32)
        iota_f = sb("iota_f", [P, P])
        spare_i = sb("spare_i", [P, 1], I32)
        spare = sb("spare", [P, 1])
        below = sb("below", [P, P])
        zeros = sb("zeros", [P, P])
        keycol = [sb(f"keycol{g}", [P, RING, 2]) for g in range(2)]
        addend = sb("addend", [P, RING, 2])
        same = [sb(f"same{g}", [P, RING, P]) for g in range(2)]
        repeated = [sb(f"repeated{g}", [P, RING, 2]) for g in range(2)]
        junk = sb("junk", [P, P])
        aside = [sb(f"aside{g}", [P, RING, 2]) for g in range(2)]
        cell = [sb(f"cell{g}", [P, RING, 2], I32) for g in range(2)]
        merged = [sb(f"merged{g}", [P, RING, 2]) for g in range(2)]
        hot_src = sb("hot_src", [P, RING, P])
        hot_dst = sb("hot_dst", [P, RING, P])
        hot_high = sb("hot_high", [P, RING, 3, TILES])
        zero_run, far_run = sb("zero_run", [P, 8192]), sb("far_run", [P, 2048])
        filled, runs_ready = sem("filled"), sem("runs_ready")
        keyrow = [ps(f"keyrow{g}", [P, 512]) for g in range(2)]
        sums = [ps(f"sums{g}", [P, 512]) for g in range(2)]
        hist_src = ps("hist_src", [P, 512])
        hist_dst = ps("hist_dst", [P, 512])
        loaded, chain, consts, iotas = sem("loaded"), sem("chain"), sem("consts"), sem("iotas")
        col_ready = [sem(f"col_ready{g}") for g in range(2)]
        row_ready = [sem(f"row_ready{g}") for g in range(2)]
        same_ready = [sem(f"same_ready{g}") for g in range(2)]
        sum_ready = [sem(f"sum_ready{g}") for g in range(2)]
        cell_ready = [sem(f"cell_ready{g}") for g in range(2)]
        merged_ready = [sem(f"merged_ready{g}") for g in range(2)]
        rep = [sem(f"repeats{g}") for g in range(2)]
        hots, weight_ready, hist_done = sem("hots"), sem("weight_ready"), sem("hist_done")
        tables = [[count_table, weight_table], [count_table2]]
        added = [[sem(f"added{g}{n}", pool_dma=True) for n in range(len(tables[g]))] for g in range(2)]
        tick = sem("tick")

        def loops(eng, body, between=None):
            rounds, rounds2 = cols // RING, cols2 // RING
            with eng.Fori(0, rounds2) as i:
                for k in range(RING):
                    body(i * RING + k, k, (0, 1))
            if rounds > rounds2:
                if between:
                    between()
                with eng.Fori(rounds2, rounds) as i:
                    for k in range(RING):
                        body(i * RING + k, k, (0,))

        with nc.Block() as block:

            @block.sync
            def _(sp):
                sp.wait_ge(consts, 6)
                for g, (count, c, *arrays) in enumerate(graphs):
                    full = count // c
                    for n, a in enumerate(arrays):
                        sp.dma_start(raw[g][n][0:full, :], a[0:full * c].rearrange("(p c) -> p c", c=c)).then_inc(loaded, 16)
                        if count > full * c:
                            rest = count - full * c
                            sp.dma_start(raw[g][n][full:full + 1, 0:rest], a[full * c:count].rearrange("(o c) -> o c", o=1)).then_inc(loaded, 16)
                full, rest = edges // cols, edges % cols
                sp.dma_start(ew[0:full, :], weight[0:full * cols].rearrange("(p c) -> p c", c=cols)).then_inc(loaded, 16)
                sp.dma_start(ew[full:full + 1, 0:rest], weight[full * cols:edges].rearrange("(o c) -> o c", o=1)).then_inc(loaded, 16)
                sp.wait_ge(runs_ready, 2)
                sent = 0
                for run, some in ((zero_run, zero_tables), (far_run, far_tables)):
                    for table in some:
                        cells = table.rearrange("(p r) f -> p (r f)", p=P)
                        for at in range(0, cells.shape[1], run.shape[1]):
                            n = min(run.shape[1], cells.shape[1] - at)
                            sp.dma_start(cells[:, at:at + n], run[:, 0:n]).then_inc(filled, 16)
                            sent += 1
                sp.wait_ge(filled, 16 * sent)

            @block.gpsimd
            def _(pool):
                nc.gpsimd.iota(iota_i[:, :], pattern=[[1, P]], base=0, channel_multiplier=0).then_inc(iotas, 1)
                nc.gpsimd.iota(spare_i[:, :], pattern=[[0, 1]], base=SPARE, channel_multiplier=1).then_inc(iotas, 1)
                nc.gpsimd.memset(below[:, :], 1.0).then_inc(tick, 1)
                pool.wait_ge(tick, 1)
                nc.gpsimd.affine_select(out=below[:, :], in_=below[:, :], compare_op=ALU.is_gt, fill=0.0, base=0,
                                        pattern=[[-1, P]], channel_multiplier=1).then_inc(iotas, 1)
                pool.wait_ge(iotas, 3)
                pool.wait_ge(consts, 6)
                for g in range(2):
                    for n, table in enumerate(tables[g]):
                        for k in range(RING):
                            if k:
                                pool.wait_ge(added[g][n], 16 * k)
                            pool.indirect_dma_start(out=table, out_offset=bass.IndirectOffsetOnAxis(ap=spare_i[:, 0:1], axis=0),
                                                    in_=zeros[:, 0:1], in_offset=None, compute_op=ALU.add).then_inc(added[g][n], 16)

                def body(c, k, which):
                    for g in which:
                        pool.wait_ge(cell_ready[g], c + 1)
                        pool.wait_ge(merged_ready[g], c + 2)
                        for n, table in enumerate(tables[g]):
                            pool.wait_ge(added[g][n], c * 16 + 16 * RING)
                            pool.sem_inc(tick, 1)
                            pool.indirect_dma_start(out=table, out_offset=bass.IndirectOffsetOnAxis(ap=cell[g][:, k, n:n + 1], axis=0),
                                                    in_=merged[g][:, k, n:n + 1], in_offset=None, compute_op=ALU.add).then_inc(added[g][n], 16)

                loops(pool, body)
                for g in range(2):
                    for s in added[g]:
                        pool.wait_ge(s, 16 * RING + 16 * graphs[g][1])

            @block.tensor
            def _(pe):
                pe.wait_ge(consts, 6)
                nc.tensor.matmul(hist_src[:, 0:2 * TILES], zeros[:, :], zeros[:, 0:2 * TILES], start=True, stop=False, skip_group_check=True).then_inc(hist_done, 1)
                nc.tensor.matmul(hist_dst[:, 0:TILES], zeros[:, :], zeros[:, 0:TILES], start=True, stop=False, skip_group_check=True).then_inc(hist_done, 1)

                def body(c, k, which):
                    for g in which:
                        pe.wait_ge(col_ready[g], c + 1)
                        pe.wait_ge(same_ready[g], c + 1)
                        nc.tensor.transpose(keyrow[g][:, 0:P], keycol[g][:, k, 0:1].to_broadcast([P, P]), st.ident[:, :]).then_inc(row_ready[g], 1)
                    for g in which:
                        pe.wait_ge(same_ready[g], c + 2)
                        if g == 0:
                            pe.wait_ge(weight_ready, c + 1)
                        pe.wait_ge(merged_ready[g], c + 1)
                        nc.tensor.matmul(sums[g][:, 0:2], same[g][:, k, :], addend[:, k, :], start=True, stop=True).then_inc(sum_ready[g], 1)
                    pe.wait_ge(hots, c * 5 + 5)
                    nc.tensor.matmul(hist_src[:, 0:2 * TILES], hot_src[:, k, :], hot_high[:, k, 0:2, :].rearrange("p a b -> p (a b)"),
                                     start=False, stop=False, skip_group_check=True)
                    nc.tensor.matmul(hist_dst[:, 0:TILES], hot_dst[:, k, :], hot_high[:, k, 2, :],
                                     start=False, stop=False, skip_group_check=True).then_inc(hist_done, 1)

                loops(pe, body)
                nc.tensor.matmul(hist_src[:, 0:2 * TILES], zeros[:, :], zeros[:, 0:2 * TILES], start=False, stop=True, skip_group_check=True)
                nc.tensor.matmul(hist_dst[:, 0:TILES], zeros[:, :], zeros[:, 0:TILES], start=False, stop=True, skip_group_check=True).then_inc(hist_done, 1)

            @block.scalar
            def _(act):
                for g in range(2):
                    act.sem_inc(merged_ready[g], 1)

                def body(c, k, which):
                    for g in which:
                        act.wait_ge(sum_ready[g], c + 1)
                        for s in added[g]:
                            act.wait_ge(s, c * 16 + 16)
                        nc.scalar.copy(merged[g][:, k, :], sums[g][:, 0:2]).then_inc(merged_ready[g], 1)

                loops(act, body)

            @block.vector
            def _(dve):
                link = Chain(dve, chain)
                nc.vector.memset(zeros[:, :], 0.0).then_inc(consts, 1)
                nc.vector.memset(ew[:, :], 0.0).then_inc(consts, 1)
                for g in range(2):
                    for n in range(2):
                        nc.vector.memset(raw[g][n][:, :], NP).then_inc(consts, 1)
                nc.vector.memset(zero_run[:, :], 0.0).then_inc(runs_ready, 1)
                nc.vector.memset(far_run[:, :], FAR).then_inc(runs_ready, 1)
                dve.wait_ge(iotas, 3)
                link.mark(nc.vector.memset(addend[:, :, :], 1.0))
                link.mark(nc.vector.tensor_copy(iota_f[:, :], iota_i[:, :]))
                link.mark(nc.vector.tensor_copy(spare[:, :], spare_i[:, :]))
                dve.wait_ge(loaded, 16 * (4 + 2 + 2 + (2 if edges2 % cols2 else 0)))
                for g in range(2):
                    for n in range(2):
                        link.mark(nc.vector.tensor_copy(ends[g][n][:, :], raw[g][n][:, :]))
                link.settle()
                for n in range(2):
                    link(nc.vector.tensor_single_scalar(digit[:, :], raw[0][n][:, :], P - 1, op=ALU.bitwise_and))
                    link(nc.vector.tensor_copy(low[n][:, :], digit[:, :]))
                    link(nc.vector.tensor_single_scalar(digit[:, :], raw[0][n][:, :], 7, op=ALU.logical_shift_right))
                    link(nc.vector.tensor_copy(high[n][:, :], digit[:, :]))
                for g, n in ((0, 0), (0, 1), (1, 0)):
                    link(nc.vector.scalar_tensor_tensor(out=keys[g][:, n, :], in0=ends[g][n][:, :], scalar=float(PITCH),
                                                        in1=ends[g][1 - n][:, :], op0=ALU.mult, op1=ALU.add))

                def body(c, k, which):
                    for g in which:
                        w = len(tables[g])
                        for s in added[g]:
                            dve.wait_ge(s, c * 16 + 16)
                        nc.vector.tensor_copy(keycol[g][:, k, 0:w], keys[g][:, :, bass.ds(c, 1)].rearrange("p n o -> p (n o)")).then_inc(col_ready[g], 1)
                    if 0 in which:
                        nc.vector.tensor_copy(addend[:, k, 1:2], ew[:, bass.ds(c, 1)]).then_inc(weight_ready, 1)
                    dve.wait_ge(hist_done, c + 1)
                    col = lambda a: a[:, bass.ds(c, 1)]
                    nc.vector.tensor_scalar(hot_src[:, k, :], iota_f[:, :], col(low[0]), None, ALU.is_equal).then_inc(hots, 1)
                    nc.vector.tensor_scalar(hot_dst[:, k, :], iota_f[:, :], col(low[1]), None, ALU.is_equal).then_inc(hots, 1)
                    nc.vector.tensor_scalar(hot_high[:, k, 0, :], iota_f[:, 0:TILES], col(high[0]), None, ALU.is_equal).then_inc(hots, 1)
                    nc.vector.tensor_scalar(hot_high[:, k, 1, :], iota_f[:, 0:TILES], col(high[0]), col(ew), ALU.is_equal, ALU.mult).then_inc(hots, 1)
                    nc.vector.tensor_scalar(hot_high[:, k, 2, :], iota_f[:, 0:TILES], col(high[1]), None, ALU.is_equal).then_inc(hots, 1)
                    for g in which:
                        w = len(tables[g])
                        dve.wait_ge(row_ready[g], c + 1)
                        nc.vector.tensor_scalar(same[g][:, k, :], keyrow[g][:, 0:P], keycol[g][:, k, 0:1], None, ALU.is_equal).then_inc(same_ready[g], 1)
                        dve.wait_ge(same_ready[g], c + 2)
                        nc.vector.tensor_tensor_reduce(junk[:, :], same[g][:, k, :], below[:, :], 1.0, 0.0, ALU.mult, ALU.add,
                                                       repeated[g][:, k, 0:1]).then_inc(rep[g], 1)
                        nc.vector.tensor_scalar(aside[g][:, k, 0:w], keycol[g][:, k, 0:w], -1.0, spare[:, 0:1], ALU.mult, ALU.add).then_inc(rep[g], 1)
                        dve.wait_ge(rep[g], c * 3 + 2)
                        nc.vector.tensor_scalar(repeated[g][:, k, 1:2], repeated[g][:, k, 0:1], 0.0, None, ALU.is_gt).then_inc(rep[g], 1)
                        dve.wait_ge(rep[g], c * 3 + 3)
                        nc.vector.scalar_tensor_tensor(out=cell[g][:, k, 0:w], in0=aside[g][:, k, 0:w], scalar=repeated[g][:, k, 1:2],
                                                       in1=keycol[g][:, k, 0:w], op0=ALU.mult, op1=ALU.add).then_inc(cell_ready[g], 1)

                def second_graph_done():
                    dve.wait_ge(added[1][0], 16 * RING + 16 * cols2)

                for g in range(2):
                    dve.sem_inc(same_ready[g], 1)
                loops(dve, body, second_graph_done)
                dve.wait_ge(hist_done, cols + 3)
                nc.vector.tensor_copy(st.deg_out[:, :], hist_src[:, 0:TILES]).then_inc(chain, 1)
                nc.vector.tensor_copy(st.deg_weight[:, :], hist_src[:, TILES:2 * TILES]).then_inc(chain, 1)
                nc.vector.tensor_copy(st.deg_in[:, :], hist_dst[:, 0:TILES]).then_inc(chain, 1)




def degree_factors(nc, st, stage):
    with ExitStack() as ctx:
        sb, ps, sem = tools(nc, ctx, stage)
        positive = sb("positive", [P, TILES])
        chain, floored, rooted = sem("chain"), sem("floored"), sem("rooted")
        with nc.Block() as block:

            @block.vector
            def _(dve):
                link = Chain(dve, chain)
                link(nc.vector.tensor_scalar(st.deg_weight[:, :], st.deg_weight[:, :], 1.0, None, ALU.add))
                link(nc.vector.tensor_scalar(positive[:, :], st.deg_weight[:, :], 0.0, None, ALU.is_gt))
                nc.vector.tensor_scalar(st.deg_weight[:, :], st.deg_weight[:, :], 1e-30, None, ALU.max).then_inc(floored, 1)
                nc.vector.tensor_scalar(st.deg_in[:, :], st.deg_in[:, :], 1.0, None, ALU.max).then_inc(floored, 1)
                dve.wait_ge(rooted, 2)
                link.mark(nc.vector.reciprocal(st.deg_in[:, :], st.deg_in[:, :]))
                link(nc.vector.reciprocal(st.deg_weight[:, :], st.deg_weight[:, :]))
                link(nc.vector.tensor_tensor(st.deg_weight[:, :], st.deg_weight[:, :], positive[:, :], ALU.mult))

            @block.scalar
            def _(act):
                act.wait_ge(floored, 2)
                for a in (st.deg_in, st.deg_weight):
                    nc.scalar.activation(a[:, :], a[:, :], ACT.Sqrt).then_inc(rooted, 1)


def aggregate(nc, st, stage, table, src, finish, clear, masked_table, mask):
    by_block = lambda t: t[0:NP * NP, :].rearrange("(c p d) o -> p c (d o)", p=P, d=NP)
    view = by_block(table)
    groups = [(c, min(4, TILES - c)) for c in range(0, TILES, 4)]
    apart = masked_table is not table
    G = len(groups)
    with ExitStack() as ctx:
        sb, ps, sem = tools(nc, ctx, stage)
        block_in = sb("block_in", [P, 3, TILES, P])
        acc = ps("acc", [P, 2, 512])
        cells = clear.rearrange("(p r) f -> p (r f)", p=P)
        RUN = -(-cells.shape[1] // TILES)
        zeros = sb("zeros", [P, RUN])
        zeros_ready, cleared = sem("zeros_ready"), sem("cleared")
        loaded = [sem(f"loaded{k}") for k in range(3)]
        multiplied, finished, chain = sem("multiplied"), sem("finished"), sem("chain")
        masked_in = sb("masked_in", [P, 2, TILES, P]) if apart else block_in
        SLOTS = 2 if apart else 3
        masked_loaded = [sem(f"masked_loaded{k}") for k in range(2)] if apart else loaded
        block_out = sb("block_out", [P, 2, NP], BF16)
        off_diagonal = sb("off_diagonal", [P, P], BF16)
        turned = ps("turned", [P, 4, 512])
        stored = [sem(f"stored{k}") for k in range(2)]
        transposed, compared, diagonal, const = (sem(n) for n in ("transposed", "compared", "diagonal", "const"))
        extra = finish.prepare(nc, ctx, stage) if hasattr(finish, "prepare") else None
        with nc.Block() as block:

            @block.sync
            def _(sp):
                if extra is not None:
                    finish.load(sp, extra)

                def store_mask(t):
                    sp.wait_ge(diagonal, t + 1)
                    sp.dma_start(mask[t * P:(t + 1) * P, :], block_out[:, t % 2, :]).then_inc(stored[t % 2], 16)

                sp.wait_ge(zeros_ready, 1)
                for t in range(TILES):
                    if apart:
                        if t >= 2:
                            sp.wait_ge(transposed, (t - 1) * G)
                        sp.dma_start(masked_in[:, t % 2, :, :], by_block(masked_table)[:, :, t * P:(t + 1) * P]).then_inc(masked_loaded[t % 2], 16)
                    if t >= 3:
                        sp.wait_ge(multiplied, t - 2)
                    sp.dma_start(block_in[:, t % 3, :, :], view[:, :, t * P:(t + 1) * P]).then_inc(loaded[t % 3], 16)
                    part = cells[:, t * RUN:min((t + 1) * RUN, cells.shape[1])]
                    sp.dma_start(part, zeros[:, 0:part.shape[1]]).then_inc(cleared, 16)
                    if t >= 2:
                        store_mask(t - 2)
                sp.wait_ge(cleared, 16 * TILES)
                for t in range(TILES - 2, TILES):
                    store_mask(t)
                for k in range(2):
                    sp.wait_ge(stored[k], 16 * ((TILES + 1 - k) // 2))

            @block.tensor
            def _(pe):
                n = 0
                for t in range(TILES):
                    pe.wait_ge(masked_loaded[t % SLOTS], 16 * (t // SLOTS + 1))
                    for c, w in groups:
                        if n >= 4:
                            pe.wait_ge(compared, n - 3)
                        for j in range(w):
                            last = nc.tensor.transpose(turned[:, n % 4, j * P:(j + 1) * P], masked_in[:, t % SLOTS, c + j, :], st.ident[:, :])
                        last.then_inc(transposed, 1)
                        n += 1
                    if apart:
                        pe.wait_ge(loaded[t % 3], 16 * (t // 3 + 1))
                    if t >= 2:
                        pe.wait_ge(finished, t - 1)
                    for c in range(TILES):
                        last = nc.tensor.matmul(acc[:, t % 2, 0:D], block_in[:, t % 3, c, :], src[:, c, :],
                                                start=(c == 0), stop=(c == TILES - 1))
                    last.then_inc(multiplied, 1)

            @block.vector
            def _(dve):
                link = Chain(dve, chain)
                nc.vector.memset(zeros[:, :], 0.0).then_inc(zeros_ready, 1)
                if extra is not None:
                    finish.wait(dve, extra)
                nc.vector.tensor_scalar(off_diagonal[:, :], st.ident[:, :], -1.0, 1.0, ALU.mult, ALU.add).then_inc(const, 1)
                dve.wait_ge(const, 1)
                n = 0
                for t in range(TILES):
                    if t >= 2:
                        dve.wait_ge(stored[t % 2], 16 * (t // 2))
                    for c, w in groups:
                        dve.wait_ge(transposed, n + 1)
                        nc.vector.tensor_scalar(block_out[:, t % 2, c * P:(c + w) * P], turned[:, n % 4, 0:w * P], 0.0, FAR,
                                                ALU.is_equal, ALU.mult).then_inc(compared, 1)
                        n += 1
                    dve.wait_ge(compared, n)
                    own = block_out[:, t % 2, t * P:(t + 1) * P]
                    nc.vector.tensor_tensor(own, own, off_diagonal[:, :], ALU.mult).then_inc(diagonal, 1)
                    dve.wait_ge(multiplied, t + 1)
                    finish(nc, link, t, acc[:, t % 2, 0:D], extra).then_inc(finished, 1)


def scaled_into(dst, factor):
    def finish(nc, link, t, psum, extra):
        return nc.vector.tensor_scalar(dst[:, t, :], psum, factor[:, t:t + 1], None, ALU.mult)
    return finish


def relu_into(dst):
    def finish(nc, link, t, psum, extra):
        return nc.vector.tensor_scalar(dst[:, t, :], psum, 0.0, None, ALU.max)
    return finish


def copied_into(dst):
    def finish(nc, link, t, psum, extra):
        return nc.vector.tensor_copy(dst[:, t, :], psum)
    return finish


def added_to(dst):
    def finish(nc, link, t, psum, extra):
        return nc.vector.tensor_tensor(dst[:, t, :], dst[:, t, :], psum, ALU.add)
    return finish


class WeightedSum:

    def __init__(self, dst, own, factor, bias):
        self.dst, self.own, self.factor, self.bias = dst, own, factor, bias

    def prepare(self, nc, ctx, stage):
        return (ctx.enter_context(nc.sbuf_tensor(f"{stage}_bias_rows", [P, D], F32)),
                SEMAPHORES.take(nc, ctx, stage, begins=False)("bias_loaded"))

    def load(self, sp, extra):
        sp.dma_start(extra[0][:, :], self.bias.partition_broadcast(P)).then_inc(extra[1], 16)

    def wait(self, dve, extra):
        dve.wait_ge(extra[1], 16)

    def __call__(self, nc, link, t, psum, extra):
        out = self.dst[:, t, :]
        link(nc.vector.tensor_tensor(out, psum, self.own[:, t, :], ALU.add))
        return nc.vector.scalar_tensor_tensor(out=out, in0=out, scalar=self.factor[:, t:t + 1], in1=extra[0][:, :],
                                              op0=ALU.mult, op1=ALU.add)


def add_unit_rows(nc, st, stage, src):
    with ExitStack() as ctx:
        sb, ps, sem = tools(nc, ctx, stage)
        squares = sb("squares", [P, TILES, D])
        length = sb("length", [P, TILES])
        chain, summed, rooted = sem("chain"), sem("summed"), sem("rooted")
        with nc.Block() as block:

            @block.vector
            def _(dve):
                link = Chain(dve, chain)
                link(nc.vector.tensor_tensor(squares[:, :, :], src[:, :, :], src[:, :, :], ALU.mult))
                nc.vector.tensor_reduce(length[:, :], squares[:, :, :], AX, ALU.add).then_inc(summed, 1)
                dve.wait_ge(rooted, 1)
                link(nc.vector.tensor_scalar(length[:, :], length[:, :], 1e-12, None, ALU.max))
                link(nc.vector.reciprocal(length[:, :], length[:, :]))
                for t in range(TILES):
                    link.mark(nc.vector.scalar_tensor_tensor(out=st.x[:, t, :], in0=src[:, t, :], scalar=length[:, t:t + 1],
                                                             in1=st.x[:, t, :], op0=ALU.mult, op1=ALU.add))

            @block.scalar
            def _(act):
                act.wait_ge(summed, 1)
                nc.scalar.activation(length[:, :], length[:, :], ACT.Sqrt).then_inc(rooted, 1)


def layer0_gnn(nc, st, d, count_table, mask, clear):
    norm_nodes(nc, st, "l0_norm", st.x, st.a, False, scale=st.deg_out)
    aggregate(nc, st, "l0_sum", count_table, st.a, scaled_into(st.b, st.deg_in), clear, count_table, mask)
    transpose_nodes(nc, st, "l0_turn", st.b)
    linear_nodes(nc, st, "l0_linear", d["L0_gnn_W"], d["L0_gnn_b"], D, relu_into(st.b))
    add_unit_rows(nc, st, "l0_unit", st.b)


def layer1_gnn(nc, st, d, weight_table, clear, masked_table, mask):
    norm_nodes(nc, st, "l1_norm", st.x, st.a, True)
    linear_nodes(nc, st, "l1_linear", d["L1_gnn_W"], None, D, scaled_into(st.b, st.deg_weight))
    aggregate(nc, st, "l1_sum", weight_table, st.b, WeightedSum(st.a, st.b, st.deg_weight, d["L1_gnn_b"]), clear, masked_table, mask)
    transpose_nodes(nc, st, "l1_turn1", st.a)
    linear_nodes(nc, st, "l1_head1", d["L1_gnn_W1"], d["L1_gnn_b1"], D, relu_into(st.b))
    transpose_nodes(nc, st, "l1_turn2", st.b)
    linear_nodes(nc, st, "l1_head2", d["L1_gnn_W2"], d["L1_gnn_b2"], D, added_to(st.x))



SLOPE = 0.2


class Attention:

    def __init__(self, st, heads, width):
        self.heads, self.width = heads, width
        self.cols = heads * (width + 1)
        self.values = st.b_flat[:, 0:TILES * self.cols].rearrange("p (t h w) -> p t h w", h=heads, w=width + 1)
        flat = st.b_flat[:, 0:TILES * self.cols].rearrange("p (t c) -> p t c", c=self.cols)
        self.flat = flat
        self.groups = []
        for h in range(heads):
            for o in range(0, width + 1, P):
                self.groups.append((h, h * (width + 1) + o, min(P, width + 1 - o)))


def attention_values(nc, st, stage, att, weight, att_src, att_dst, scores):
    H, W = att.heads, att.width
    HW = H * W
    with ExitStack() as ctx:
        sb, ps, sem = tools(nc, ctx, stage)
        w = sb("weight", [P, KC, HW + 2 * H])
        vectors = sb("vectors", [P, 2, HW])
        work = sb("work", [P, KC, HW])
        acc = ps("acc", [P, 4, CHUNK])
        loaded, chain, folded, multiplied, finished = (sem(n) for n in ("loaded", "chain", "folded", "multiplied", "finished"))
        with nc.Block() as block:

            @block.sync
            def _(sp):
                sp.dma_start(w[:, :, 0:HW], weight.rearrange("(c p) m -> p c m", p=P)).then_inc(loaded, 16)
                for n, a in enumerate((att_src, att_dst)):
                    sp.dma_start(vectors[:, n, :], a.rearrange("h w -> (h w)").partition_broadcast(P)).then_inc(loaded, 16)

            @block.tensor
            def _(pe):
                pe.wait_ge(folded, 1)
                for t in range(TILES):
                    if t >= 4:
                        pe.wait_ge(finished, 2 * (t - 3))
                    for c in range(KC):
                        last = nc.tensor.matmul(acc[:, t % 4, 0:HW + 2 * H], st.aT[:, c, t * P:(t + 1) * P], w[:, c, :],
                                                start=(c == 0), stop=(c == KC - 1))
                    last.then_inc(multiplied, 1)

            @block.vector
            def _(dve):
                link = Chain(dve, chain)
                dve.wait_ge(loaded, 48)
                for n in range(2):
                    link(nc.vector.tensor_tensor(work[:, :, :], w[:, :, 0:HW], vectors[:, n, :].unsqueeze(1).to_broadcast([P, KC, HW]), ALU.mult))
                    for c in range(KC):
                        link(nc.vector.tensor_reduce(w[:, c, HW + n * H:HW + (n + 1) * H],
                                                     work[:, c, :].rearrange("p (h w) -> p h w", h=H), AX, ALU.add))
                nc.vector.memset(att.values[:, :, :, W], 1.0).then_inc(folded, 1)
                for t in range(TILES):
                    dve.wait_ge(multiplied, t + 1)
                    nc.vector.tensor_copy(att.values[:, t, :, 0:W], acc[:, t % 4, 0:HW].rearrange("p (h w) -> p h w", h=H)).then_inc(finished, 1)
                    nc.vector.tensor_copy(scores[:, t, :, :], acc[:, t % 4, HW:HW + 2 * H].rearrange("p (n h) -> p n h", n=2)).then_inc(finished, 1)


def attention_maxima(nc, st, stage, att, mask, scores, shifts):
    H = att.heads
    with ExitStack() as ctx:
        sb, ps, sem = tools(nc, ctx, stage)
        more = sb("rows", [P, 2, NP]) if H > 2 else None
        row = [st.aT[:, h, :] if h < 2 else more[:, h - 2, :] for h in range(H)]
        mask_in = sb("mask_in", [P, 3, NP], BF16)
        junk = sb("junk", [P, NP], BF16)
        top = sb("top", [P, TILES, H])
        turned = ps("turned", [P, 4, 512])
        loaded = [sem(f"loaded{k}") for k in range(3)]
        chain, transposed, copied, reduced = (sem(n) for n in ("chain", "transposed", "copied", "reduced"))
        with nc.Block() as block:

            @block.sync
            def _(sp):
                for t in range(TILES):
                    if t >= 3:
                        sp.wait_ge(reduced, (t - 2) * H)
                    sp.dma_start(mask_in[:, t % 3, :], mask[t * P:(t + 1) * P, :]).then_inc(loaded[t % 3], 16)

            @block.tensor
            def _(pe):
                n = 0
                for h in range(H):
                    for at, w in CHUNKS:
                        if n >= 4:
                            pe.wait_ge(copied, n - 3)
                        for j in range(w // P):
                            last = nc.tensor.transpose(turned[:, n % 4, j * P:(j + 1) * P],
                                                       scores[:, at // P + j, 0, h:h + 1].to_broadcast([P, P]), st.ident[:, :])
                        last.then_inc(transposed, 1)
                        n += 1

            @block.scalar
            def _(act):
                n = 0
                for h in range(H):
                    for at, w in CHUNKS:
                        act.wait_ge(transposed, n + 1)
                        nc.scalar.copy(row[h][:, at:at + w], turned[:, n % 4, 0:w]).then_inc(copied, 1)
                        n += 1

            @block.vector
            def _(dve):
                link = Chain(dve, chain)
                dve.wait_ge(copied, H * len(CHUNKS))
                n = 0
                for t in range(TILES):
                    dve.wait_ge(loaded[t % 3], 16 * (t // 3 + 1))
                    for h in range(H):
                        if n >= 1:
                            dve.wait_ge(reduced, n)
                        nc.vector.tensor_tensor_reduce(junk[:, :], row[h], mask_in[:, t % 3, :], 1.0, -3e38, ALU.add, ALU.max,
                                                       top[:, t, h:h + 1]).then_inc(reduced, 1)
                        n += 1
                dve.wait_ge(reduced, n)
                src, dst = scores[:, :, 0, :], scores[:, :, 1, :]
                link(nc.vector.tensor_tensor(top[:, :, :], top[:, :, :], dst, ALU.add))
                link(nc.vector.scalar_tensor_tensor(out=top[:, :, :], in0=top[:, :, :], scalar=SLOPE, in1=top[:, :, :], op0=ALU.mult, op1=ALU.max))
                link(nc.vector.tensor_tensor(shifts[:, :, 0, :], dst, top[:, :, :], ALU.subtract))
                link(nc.vector.scalar_tensor_tensor(out=shifts[:, :, 1, :], in0=dst, scalar=SLOPE, in1=top[:, :, :], op0=ALU.mult, op1=ALU.subtract))
                link(nc.vector.tensor_scalar(dst, src, SLOPE, None, ALU.mult))


def attention_sums(nc, st, stage, att, table, scores, shifts, finish):
    H, G = att.heads, len(att.groups)
    HU = min(H, 2)
    U = H // HU
    SLOTS = 6
    DRAIN, TURN, SHIFT, LAG = 0, 1, 6, 3
    NC = len(CHUNKS)
    view = table[0:NP * NP, :].rearrange("(r d) o -> r (d o)", d=NP)
    with ExitStack() as ctx:
        sb, ps, sem = tools(nc, ctx, stage)
        lent = st.aT[:, :, :].rearrange("p c n -> p (c n)")[:, 0:3 * H * CHUNK].rearrange("p (s h n) -> p s h n", s=3, h=H)
        own_row = sb("row", [P, H, CHUNK])
        rows = [[lent[:, q * 2 + k, :, :] if q * 2 + k < 3 else own_row[:, :, :] for k in range(2)] for q in range(2)]
        count_in = sb("count_in", [P, 4, CHUNK])
        e = sb("e", [P, SLOTS, 2, HU, CHUNK])
        outT = sb("outT", [P, G, CHUNK])
        alone = H == 1
        total = sb("total", [P, 2, CHUNK]) if alone else None
        acc = ps("acc", [P, 4, 512])
        turned = ps("turned", [P, 2, 512])
        final = ps("final", [P, 2, 512])
        loaded = [sem(f"loaded{k}") for k in range(4)]
        chain, transposed, copied, exped, maxed, weighed, summed, drained, final_ready, finished = (
            sem(n) for n in ("chain", "transposed", "copied", "exped", "maxed", "weighed", "summed", "drained", "final_ready", "finished"))
        totaled = sem("totaled")
        extra = finish.prepare(nc, ctx, stage) if hasattr(finish, "prepare") else None
        rows_at = lambda q, c: range((q + 1) * 2 * H + c - SHIFT, (q + 1) * 2 * H + c - SHIFT + 1) if q + 1 < NC and SHIFT <= c < SHIFT + 2 * H else ()
        with nc.Block() as block:

            @block.sync
            def _(sp):
                if extra is not None:
                    finish.load(sp, extra)
                n = 0
                for at, w in CHUNKS:
                    for c in range(TILES):
                        if n >= 4:
                            sp.wait_ge(weighed, (n - 3) * U)
                        sp.dma_start(count_in[:, n % 4, 0:w], view[c * P:(c + 1) * P, at:at + w]).then_inc(loaded[n % 4], 16)
                        n += 1

            @block.tensor
            def _(pe):
                def turn_shifts(r):
                    (at, w), k, h = CHUNKS[r // (2 * H)], r % (2 * H) // H, r % H
                    if r >= 2:
                        pe.wait_ge(copied, r - 1)
                    for j in range(w // P):
                        last = nc.tensor.transpose(turned[:, r % 2, j * P:(j + 1) * P],
                                                   shifts[:, at // P + j, k, h:h + 1].to_broadcast([P, P]), st.ident[:, :])
                    last.then_inc(transposed, 1)

                def turn_chunk(q):
                    at, w = CHUNKS[q]
                    for t in range(at // P, (at + w) // P):
                        if t >= 2:
                            pe.wait_ge(finished, t - 1)
                        for g, (h, col, m) in enumerate(att.groups):
                            last = nc.tensor.transpose(final[:, t % 2, col:col + m], outT[0:m, g, t * P - at:(t + 1) * P - at], st.ident[0:m, 0:m])
                        last.then_inc(final_ready, 1)

                for r in range(2 * H):
                    turn_shifts(r)
                n = 0
                for q, (at, w) in enumerate(CHUNKS):
                    for c in range(TILES):
                        for r in rows_at(q, c):
                            turn_shifts(r)
                        if c == TURN and q:
                            turn_chunk(q - 1)
                        for u in range(U):
                            pe.wait_ge(weighed, n + 1)
                            if c == 0 and u == 0 and q > 0:
                                pe.wait_ge(drained, q * G)
                            for g, (h, col, m) in enumerate(att.groups):
                                if alone and m == 1:
                                    if c == TILES - 1:
                                        pe.wait_ge(totaled, n + 1)
                                        last = nc.tensor.matmul(acc[0:1, g, 0:w], att.flat[:, c, col:col + 1], total[:, q % 2, 0:w],
                                                                start=True, stop=True)
                                elif h // HU == u:
                                    last = nc.tensor.matmul(acc[0:m, g, 0:w], att.flat[:, c, col:col + m], e[:, n % SLOTS, 0, h % HU, 0:w],
                                                            start=(c == 0), stop=(c == TILES - 1))
                            last.then_inc(summed, 1)
                            n += 1
                pe.wait_ge(drained, NC * G)
                turn_chunk(NC - 1)

            if alone:
                @block.gpsimd
                def _(pool):
                    for n in range(NC * TILES):
                        q, c = n // TILES, n % TILES
                        w = CHUNKS[q][1]
                        pool.wait_ge(weighed, n + 1)
                        sum_now, weights = total[:, q % 2, 0:w], e[:, n % SLOTS, 0, 0, 0:w]
                        if c == 0:
                            if q >= 2:
                                pool.wait_ge(summed, (q - 1) * TILES)
                            nc.gpsimd.tensor_copy(sum_now, weights).then_inc(totaled, 1)
                        else:
                            pool.wait_ge(totaled, n)
                            nc.gpsimd.tensor_tensor(sum_now, sum_now, weights, ALU.add).then_inc(totaled, 1)

            @block.scalar
            def _(act):
                def copy_shifts(r):
                    q, k, h = r // (2 * H), r % (2 * H) // H, r % H
                    w = CHUNKS[q][1]
                    act.wait_ge(transposed, r + 1)
                    nc.scalar.copy(rows[q % 2][k][:, h, 0:w], turned[:, r % 2, 0:w]).then_inc(copied, 1)

                for r in range(2 * H):
                    copy_shifts(r)
                n = 0
                for q, (at, w) in enumerate(CHUNKS):
                    act.wait_ge(copied, (q + 1) * 2 * H)
                    for c in range(TILES):
                        for u in range(U):
                            if n >= SLOTS:
                                act.wait_ge(summed, n - SLOTS + 1)
                                if alone:
                                    act.wait_ge(totaled, n - SLOTS + 1)
                            for k in range(2):
                                for j in range(HU):
                                    h = u * HU + j
                                    last = nc.scalar.activation(e[:, n % SLOTS, k, j, 0:w], rows[q % 2][k][:, h, 0:w], ACT.Exp,
                                                                bias=scores[:, c, k, h:h + 1])
                            last.then_inc(exped, 1)
                            n += 1
                        for r in rows_at(q, c - LAG):
                            act.wait_ge(exped, q * TILES * U)
                            copy_shifts(r)

            @block.vector
            def _(dve):
                link = Chain(dve, chain)
                if extra is not None:
                    finish.wait(dve, extra)

                def drain_chunk(q):
                    at, w = CHUNKS[q]
                    dve.wait_ge(summed, (q + 1) * TILES * U)
                    if q:
                        dve.wait_ge(final_ready, at // P)
                    for g, (h, col, m) in enumerate(att.groups):
                        nc.vector.tensor_copy(outT[0:m, g, 0:w], acc[0:m, g, 0:w]).then_inc(drained, 1)

                def finish_chunk(q):
                    at, w = CHUNKS[q]
                    for t in range(at // P, (at + w) // P):
                        dve.wait_ge(final_ready, t + 1)
                        finish(nc, link, t, final[:, t % 2, 0:att.cols].rearrange("p (h w) -> p h w", h=H), extra).then_inc(finished, 1)

                def weigh(n):
                    (at, w), c, u = CHUNKS[n // U // TILES], n // U % TILES, n % U
                    slot = n // U % 4
                    if u == 0:
                        dve.wait_ge(loaded[slot], 16 * (n // U // 4 + 1))
                        if at <= c * P < at + w:
                            own = count_in[:, slot, c * P - at:(c + 1) * P - at]
                            link(nc.vector.tensor_tensor(own, own, st.ident[:, :], ALU.add))
                    dve.wait_ge(maxed, n + 1)
                    nc.vector.scalar_tensor_tensor(out=e[:, n % SLOTS, 0, :, 0:w], in0=e[:, n % SLOTS, 0, :, 0:w], scalar=1.0,
                                                   in1=count_in[:, slot, 0:w].unsqueeze(1).to_broadcast([P, HU, w]),
                                                   op0=ALU.min, op1=ALU.mult).then_inc(weighed, 1)

                n = 0
                for q, (at, w) in enumerate(CHUNKS):
                    for c in range(TILES):
                        for u in range(U):
                            dve.wait_ge(exped, n + 1)
                            nc.vector.tensor_tensor(e[:, n % SLOTS, 0, :, 0:w], e[:, n % SLOTS, 0, :, 0:w], e[:, n % SLOTS, 1, :, 0:w], ALU.max).then_inc(maxed, 1)
                            if n:
                                weigh(n - 1)
                            n += 1
                        if c == DRAIN and q:
                            drain_chunk(q - 1)
                        if c == TURN and q:
                            finish_chunk(q - 1)
                weigh(n - 1)
                drain_chunk(NC - 1)
                finish_chunk(NC - 1)


class Averaged:

    def __init__(self, att, target, bias, add=False):
        self.att, self.target, self.bias, self.add = att, target, bias, add

    def prepare(self, nc, ctx, stage):
        width = self.att.heads * self.att.width
        return (ctx.enter_context(nc.sbuf_tensor(f"{stage}_bias_rows", [P, width], F32)),
                SEMAPHORES.take(nc, ctx, stage, begins=False)("bias_loaded"),
                ctx.enter_context(nc.sbuf_tensor(f"{stage}_inverse", [P, self.att.heads], F32)),
                ctx.enter_context(nc.sbuf_tensor(f"{stage}_average", [P, width], F32)))

    def load(self, sp, extra):
        sp.dma_start(extra[0][:, :], self.bias.partition_broadcast(P)).then_inc(extra[1], 16)

    def wait(self, dve, extra):
        dve.wait_ge(extra[1], 16)

    def __call__(self, nc, link, t, psum, extra):
        H, W = self.att.heads, self.att.width
        bias, _, inverse, average = extra
        out = self.target[:, t, :]
        link(nc.vector.tensor_scalar(inverse[:, :], psum[:, :, W], 1e-16, None, ALU.add))
        link(nc.vector.reciprocal(inverse[:, :], inverse[:, :]))
        link(nc.vector.tensor_tensor(average[:, :].rearrange("p (h w) -> p h w", h=H), psum[:, :, 0:W],
                                     inverse[:, :].unsqueeze(2).to_broadcast([P, H, W]), ALU.mult))
        if self.add:
            link(nc.vector.tensor_tensor(out, out, bias[:, :], ALU.add))
            last = nc.vector.tensor_tensor(out, out, average[:, :], ALU.add)
        else:
            last = nc.vector.tensor_tensor(out, average[:, :], bias[:, :], ALU.add)
        return last


def elu_nodes(nc, st, stage):
    with ExitStack() as ctx:
        sb, ps, sem = tools(nc, ctx, stage)
        chain, clipped, exped = sem("chain"), sem("clipped"), sem("exped")
        with nc.Block() as block:

            @block.vector
            def _(dve):
                link = Chain(dve, chain)
                for t in range(0, TILES, 5):
                    nc.vector.tensor_scalar(st.b[:, t:t + 5, :], st.a[:, t:t + 5, :], 0.0, None, ALU.min).then_inc(clipped, 1)
                for n, t in enumerate(range(0, TILES, 5)):
                    dve.wait_ge(exped, n + 1)
                    a = st.a[:, t:t + 5, :].rearrange("p t d -> p (t d)")
                    b = st.b[:, t:t + 5, :].rearrange("p t d -> p (t d)")
                    link(nc.vector.scalar_tensor_tensor(out=a, in0=a, scalar=0.0, in1=b, op0=ALU.max, op1=ALU.add))
                    link(nc.vector.tensor_scalar(a, a, -1.0, None, ALU.add))

            @block.scalar
            def _(act):
                for n, t in enumerate(range(0, TILES, 5)):
                    act.wait_ge(clipped, n + 1)
                    nc.scalar.activation(st.b[:, t:t + 5, :], st.b[:, t:t + 5, :], ACT.Exp).then_inc(exped, 1)


def attend(nc, st, stage, att, table, mask, weight, att_src, att_dst, finish):
    with ExitStack() as ctx:
        sb, ps, sem = tools(nc, ctx, stage)
        scores = sb("scores", [P, TILES, 2, att.heads])
        shifts = sb("shifts", [P, TILES, 2, att.heads])
        attention_values(nc, st, stage + "v", att, weight, att_src, att_dst, scores)
        attention_maxima(nc, st, stage + "m", att, mask, scores, shifts)
        attention_sums(nc, st, stage + "s", att, table, scores, shifts, finish)


def layer3_gnn(nc, st, d, table, mask):
    norm_nodes(nc, st, "l3_norm", st.x, st.a, True)
    for n in range(2):
        att = Attention(st, 4, D // 4)
        attend(nc, st, f"l3_{n}", att, table, mask, d[f"L3_gnn_W{n}"], d[f"L3_gnn_as{n}"], d[f"L3_gnn_ad{n}"],
               Averaged(att, st.a, d[f"L3_gnn_b{n}"]))
        elu_nodes(nc, st, f"l3_{n}elu")
        transpose_nodes(nc, st, f"l3_{n}turn", st.a)
    att = Attention(st, 1, D)
    attend(nc, st, "l3_2", att, table, mask, d["L3_gnn_W2"], d["L3_gnn_as2"], d["L3_gnn_ad2"],
           Averaged(att, st.x, d["L3_gnn_b2"], add=True))



TYPES, RELATIONS, HEADS = 4, 8, 8
HEAD = D // HEADS
SEGMENTS = NP * RELATIONS
SUMS = D + HEADS
AHEAD = 3


def typed_linear(nc, st, stage, type_masks, typesT, weight, bias, dst):
    with ExitStack() as ctx:
        sb, ps, sem = tools(nc, ctx, stage)
        w = sb("weight", [P, TYPES, KC, D])
        b = sb("bias", [TYPES, D])
        acc = ps("acc", [P, 2, TYPES, 2, D])
        loaded, chain, multiplied, finished = sem("loaded"), sem("chain"), sem("multiplied"), sem("finished")
        with nc.Block() as block:

            @block.sync
            def _(sp):
                sp.dma_start(b[:, :], bias).then_inc(loaded, 16)
                for k in range(TYPES):
                    sp.dma_start(w[:, k, :, :], weight[k].rearrange("(c p) m -> p c m", p=P)).then_inc(loaded, 16)

            @block.tensor
            def _(pe):
                pe.wait_ge(loaded, 16 * (1 + TYPES))
                for t in range(TILES):
                    if t >= 2:
                        pe.wait_ge(finished, t - 1)
                    nc.tensor.matmul(acc[:, t % 2, 0, 1, :], typesT[:, t * P:(t + 1) * P], b[:, :], start=True, stop=True)
                    for k in range(TYPES):
                        for c in range(KC):
                            last = nc.tensor.matmul(acc[:, t % 2, k, 0, :], st.aT[:, c, t * P:(t + 1) * P], w[:, k, c, :],
                                                    start=(c == 0), stop=(c == KC - 1))
                        last.then_inc(multiplied, 1)

            @block.vector
            def _(dve):
                link = Chain(dve, chain)
                for t in range(TILES):
                    dve.wait_ge(multiplied, t * TYPES + 1)
                    link(nc.vector.tensor_copy(dst[:, t, :], acc[:, t % 2, 0, 1, :]))
                    for k in range(TYPES):
                        dve.wait_ge(multiplied, t * TYPES + k + 1)
                        last = nc.vector.scalar_tensor_tensor(out=dst[:, t, :], in0=acc[:, t % 2, k, 0, :], scalar=type_masks[:, k, t:t + 1],
                                                              in1=dst[:, t, :], op0=ALU.mult, op1=ALU.add)
                        if k < TYPES - 1:
                            link(last)
                        else:
                            last.then_inc(finished, 1)


def load_types(nc, st, stage, node_type, skip, type_masks, typesT, keep):
    with ExitStack() as ctx:
        sb, ps, sem = tools(nc, ctx, stage)
        kinds = sb("kinds", [P, TILES], I32)
        kinds_f = sb("kinds_f", [P, TILES])
        gate = sb("gate", [P, TYPES])
        turned = ps("turned", [TYPES, 2, 512])
        cleared, loaded, chain, gated, masked, transposed, copied = (
            sem(n) for n in ("cleared", "loaded", "chain", "gated", "masked", "transposed", "copied"))
        with nc.Block() as block:

            @block.sync
            def _(sp):
                sp.wait_ge(cleared, 1)
                full = N - LAST
                with nc.allow_non_contiguous_dma("types by tile"):
                    sp.dma_start(kinds[:, 0:TILES - 1], node_type[0:full].rearrange("(t p) -> p t", p=P)).then_inc(loaded, 16)
                    sp.dma_start(kinds[0:LAST, TILES - 1:TILES], node_type[full:N].rearrange("(p o) -> p o", o=1)).then_inc(loaded, 16)
                sp.dma_start(gate[:, :], skip.partition_broadcast(P)).then_inc(loaded, 16)

            @block.tensor
            def _(pe):
                pe.wait_ge(masked, TYPES)
                for t in range(TILES):
                    if t >= 2:
                        pe.wait_ge(copied, t - 1)
                    nc.tensor.transpose(turned[:, t % 2, 0:P], type_masks[:, :, t], st.ident[:, :]).then_inc(transposed, 1)

            @block.scalar
            def _(act):
                act.wait_ge(loaded, 48)
                nc.scalar.activation(gate[:, :], gate[:, :], ACT.Sigmoid).then_inc(gated, 1)

            @block.vector
            def _(dve):
                link = Chain(dve, chain)
                nc.vector.memset(kinds[:, :], 0).then_inc(cleared, 1)
                dve.wait_ge(loaded, 48)
                link(nc.vector.tensor_copy(kinds_f[:, :], kinds[:, :]))
                for k in range(TYPES):
                    nc.vector.tensor_scalar(type_masks[:, k, :], kinds_f[:, :], float(k), None, ALU.is_equal).then_inc(masked, 1)
                dve.wait_ge(masked, TYPES)
                for t in range(TILES):
                    dve.wait_ge(transposed, t + 1)
                    nc.vector.tensor_copy(typesT[:, t * P:(t + 1) * P], turned[:, t % 2, 0:P]).then_inc(copied, 1)
                dve.wait_ge(gated, 1)
                link(nc.vector.tensor_scalar(keep[:, :], type_masks[:, 0, :], gate[:, 0:1], None, ALU.mult))
                for k in range(1, TYPES):
                    link(nc.vector.scalar_tensor_tensor(out=keep[:, :], in0=type_masks[:, k, :], scalar=gate[:, k:k + 1],
                                                        in1=keep[:, :], op0=ALU.mult, op1=ALU.add))


def store_rows(nc, st, stage, src, table):
    with ExitStack() as ctx:
        sb, ps, sem = tools(nc, ctx, stage)
        stored = sem("stored")
        with nc.Block() as block:

            @block.sync
            def _(sp):
                sp.dma_start(table.rearrange("(t p) f -> p t f", p=P), src[:, :, :]).then_inc(stored, 16)
                sp.wait_ge(stored, 16)


def relate_rows(nc, st, stage, relation, priority, table):
    with ExitStack() as ctx:
        sb, ps, sem = tools(nc, ctx, stage)
        blocks = sb("blocks", [P, KC, RELATIONS, P])
        pri = sb("pri", [P, RELATIONS, HEADS])
        rows = sb("rows", [P, 2, RELATIONS, D])
        acc = ps("acc", [P, 2, 4, 512])
        cleared, loaded, ready, chain, multiplied = (sem(n) for n in ("cleared", "loaded", "ready", "chain", "multiplied"))
        stored = [sem(f"stored{k}") for k in range(2)]
        copied = [sem("copied_by_act"), sem("copied_by_dve")]
        PER = P // HEAD
        with nc.Block() as block:

            @block.sync
            def _(sp):
                sp.wait_ge(cleared, 1)
                for h in range(HEADS):
                    c, o = h // PER, h % PER * HEAD
                    sp.dma_start(blocks[o:o + HEAD, c, :, o:o + HEAD], relation[:, h, :, :].rearrange("r d e -> d r e")).then_inc(loaded, 16)
                if priority is not None:
                    sp.dma_start(pri[:, :, :], priority.rearrange("r h -> (r h)").partition_broadcast(P).rearrange("p (r h) -> p r h", h=HEADS)).then_inc(loaded, 16)
                out = table[0:SEGMENTS, :].rearrange("(t p r) f -> t p r f", p=P, r=RELATIONS)
                for t in range(TILES):
                    for s in copied:
                        sp.wait_ge(s, 2 * (t + 1))
                    sp.dma_start(out[t], rows[:, t % 2, :, :]).then_inc(stored[t % 2], 16)
                for k in range(2):
                    sp.wait_ge(stored[k], 16 * ((TILES + 1 - k) // 2))

            @block.tensor
            def _(pe):
                pe.wait_ge(ready, 1)
                for t in range(TILES):
                    if t >= 2:
                        for s in copied:
                            pe.wait_ge(s, 2 * (t - 1))
                    for c in range(KC):
                        for half in range(2):
                            nc.tensor.matmul(acc[:, t % 2, c * 2 + half, :], st.aT[:, c, t * P:(t + 1) * P],
                                             blocks[:, c, half * 4:half * 4 + 4, :].rearrange("p r e -> p (r e)"),
                                             start=True, stop=True).then_inc(multiplied, 1)

            def copy_half(eng, op, mine, t, c):
                for half in range(2):
                    eng.wait_ge(multiplied, t * 4 + c * 2 + half + 1)
                    op(rows[:, t % 2, half * 4:half * 4 + 4, c * P:(c + 1) * P],
                       acc[:, t % 2, c * 2 + half, :].rearrange("p (r e) -> p r e", e=P)).then_inc(mine, 1)

            @block.scalar
            def _(act):
                for t in range(TILES):
                    if t >= 2:
                        act.wait_ge(stored[t % 2], 16 * (t // 2))
                    copy_half(act, nc.scalar.copy, copied[0], t, 0)

            @block.vector
            def _(dve):
                link = Chain(dve, chain)
                nc.vector.memset(blocks[:, :, :, :], 0.0).then_inc(cleared, 1)
                dve.wait_ge(loaded, 16 * (HEADS + (priority is not None)))
                if priority is not None:
                    link(nc.vector.tensor_scalar(pri[:, :, :], pri[:, :, :], float(HEAD) ** -0.5, None, ALU.mult))
                    for c in range(KC):
                        own = blocks[:, c, :, :].rearrange("p r (h e) -> p r h e", e=HEAD)
                        link(nc.vector.tensor_tensor(own, own, pri[:, :, c * PER:(c + 1) * PER].unsqueeze(3).to_broadcast([P, RELATIONS, PER, HEAD]), ALU.mult))
                dve.sem_inc(ready, 1)
                for t in range(TILES):
                    if t >= 2:
                        dve.wait_ge(stored[t % 2], 16 * (t // 2))
                    copy_half(dve, nc.vector.tensor_copy, copied[1], t, 1)


def fill_tables(nc, stage, tables, value, parts):
    run = tables[0].shape[0] * tables[0].shape[1] // P // parts
    assert run * P * parts == tables[0].shape[0] * tables[0].shape[1]
    with ExitStack() as ctx:
        sb, ps, sem = tools(nc, ctx, stage)
        fill = sb("fill", [P, run])
        cleared, stored = sem("cleared"), sem("stored")
        with nc.Block() as block:

            @block.vector
            def _(dve):
                nc.vector.memset(fill[:, :], value).then_inc(cleared, 1)

            @block.sync
            def _(sp):
                sp.wait_ge(cleared, 1)
                for table in tables:
                    rows = table.rearrange("(p r) f -> p (r f)", p=P)
                    for k in range(parts):
                        sp.dma_start(rows[:, k * run:(k + 1) * run], fill[:, :]).then_inc(stored, 16)
                sp.wait_ge(stored, 16 * parts * len(tables))


def edge_lists(nc, st, stage, src, dst, kind, lists):
    edges = src.shape[0]
    cols = edge_columns(edges)
    full, rest = edges // cols, edges % cols
    with ExitStack() as ctx:
        sb, ps, sem = tools(nc, ctx, stage)
        raw = [sb(n, [P, cols + AHEAD], I32) for n in ("src_raw", "dst_raw", "kind_raw")]
        value = [sb(n, [P, cols + AHEAD]) for n in ("src_value", "dst_value", "kind_value")]
        cleared, loaded, chain = sem("cleared"), sem("loaded"), sem("chain")
        with nc.Block() as block:

            @block.sync
            def _(sp):
                sp.wait_ge(cleared, 3)
                for a, r in zip((src, dst, kind), raw):
                    sp.dma_start(r[0:full, 0:cols], a[0:full * cols].rearrange("(p c) -> p c", c=cols)).then_inc(loaded, 16)
                    if rest:
                        sp.dma_start(r[full:full + 1, 0:rest], a[full * cols:edges].rearrange("(o c) -> o c", o=1)).then_inc(loaded, 16)

            @block.vector
            def _(dve):
                link = Chain(dve, chain)
                for r, fill in zip(raw, (N, N, 0)):
                    nc.vector.memset(r[:, :], fill).then_inc(cleared, 1)
                dve.wait_ge(loaded, 16 * 3 * (2 if rest else 1))
                for v, r in zip(value, raw):
                    link.mark(nc.vector.tensor_copy(v[:, :], r[:, :]))
                link.mark(nc.vector.tensor_copy(lists[:, :, 1], raw[1][:, :]))
                link.settle()
                for v, n in ((value[0], 0), (value[1], 2)):
                    link.mark(nc.vector.scalar_tensor_tensor(out=lists[:, :, n], in0=v[:, :], scalar=float(RELATIONS), in1=value[2][:, :],
                                                             op0=ALU.mult, op1=ALU.add))


def segment_maxima(nc, st, stage, lists, cells, scores, q_table, k_table, max_tables):
    RING = len(max_tables)
    cols = lists.shape[1] - AHEAD
    assert cols % RING == 0
    with ExitStack() as ctx:
        sb, ps, sem = tools(nc, ctx, stage)
        spare_i = sb("spare_i", [P, 1], I32)
        spare = sb("spare", [P, 1])
        below = sb("below", [P, P])
        far = sb("far", [P, HEADS])
        index = sb("index", [P, RING, 3], I32)
        key = sb("key", [P, RING, 1])
        k_in = sb("k_in", [P, RING, D])
        q_in = sb("q_in", [P, RING, D])
        product = sb("product", [P, RING, D])
        score = sb("score", [P, RING, HEADS])
        same = sb("same", [P, RING, P])
        apart = sb("apart", [P, RING, P])
        junk = sb("junk", [P, 1 + HEADS, P])
        repeated = sb("repeated", [P, RING, 2])
        aside = sb("aside", [P, RING, 1])
        cell = sb("cell", [P, RING, 1], I32)
        local = sb("local", [P, RING, HEADS])
        old = sb("old", [P, RING, HEADS])
        new = sb("new", [P, RING, HEADS])
        keyrow = ps("keyrow", [P, 512])
        spread = ps("spread", [P, 2, HEADS, P])
        tick, consts, chain, both_ready, maxed = (sem(n) for n in ("tick", "consts", "chain", "both_ready", "maxed"))
        listed, scored, row_ready, compared, apart_ready, spread_ready, spread_used, new_ready, steps = (
            sem(n) for n in ("listed", "scored", "row_ready", "compared", "apart_ready", "spread_ready", "spread_used",
                             "new_ready", "steps"))
        gathered, old_ready, written = ([sem(f"{n}{k}", pool_dma=True) for k in range(RING)] for n in ("gathered", "old_ready", "written"))
        STEPS, CELL_STEP = 5, 4
        with nc.Block() as block:

            @block.gpsimd
            def _(pool):
                nc.gpsimd.iota(spare_i[:, :], pattern=[[0, 1]], base=SEGMENTS, channel_multiplier=1).then_inc(tick, 1)
                nc.gpsimd.memset(below[:, :], 1.0).then_inc(tick, 1)
                nc.gpsimd.memset(far[:, :], FAR).then_inc(tick, 1)
                pool.wait_ge(tick, 3)
                nc.gpsimd.affine_select(out=below[:, :], in_=below[:, :], compare_op=ALU.is_gt, fill=0.0, base=0,
                                        pattern=[[-1, P]], channel_multiplier=1).then_inc(consts, 1)
                for k in range(RING):
                    pool.indirect_dma_start(out=max_tables[k], out_offset=bass.IndirectOffsetOnAxis(ap=spare_i[:, 0:1], axis=0),
                                            in_=far[:, :], in_offset=None).then_inc(written[k], 16)

                def gather_rows(c, k):
                    pool.wait_ge(listed, c * 2 + 2)
                    pool.sem_inc(tick, 1)
                    pool.indirect_dma_start(out=k_in[:, k, :], out_offset=None, in_=k_table,
                                            in_offset=bass.IndirectOffsetOnAxis(ap=index[:, k, 0:1], axis=0)).then_inc(gathered[k], 16)
                    pool.indirect_dma_start(out=q_in[:, k, :], out_offset=None, in_=q_table,
                                            in_offset=bass.IndirectOffsetOnAxis(ap=index[:, k, 1:2], axis=0)).then_inc(gathered[k], 16)

                def gather_maxima(k, round):
                    pool.wait_ge(written[k], round * 16 + 16)
                    pool.sem_inc(tick, 1)
                    pool.indirect_dma_start(out=old[:, k, :], out_offset=None, in_=max_tables[k],
                                            in_offset=bass.IndirectOffsetOnAxis(ap=index[:, k, 2:3], axis=0)).then_inc(old_ready[k], 16)

                for k in range(3):
                    gather_rows(k, k)
                for k in range(2):
                    gather_maxima(k, 0)
                with pool.Fori(0, cols // RING) as i:
                    for k in range(RING):
                        c = i * RING + k
                        gather_rows(c + 3, (k + 3) % RING)
                        gather_maxima((k + 2) % RING, i + (k + 2) // RING)
                        pool.wait_ge(new_ready, c + 3)
                        pool.sem_inc(tick, 1)
                        pool.indirect_dma_start(out=max_tables[k], out_offset=bass.IndirectOffsetOnAxis(ap=cell[:, k, 0:1], axis=0),
                                                in_=new[:, k, :], in_offset=None).then_inc(written[k], 16)
                for k in range(RING):
                    pool.wait_ge(written[k], 16 + 16 * (cols // RING))
                    pool.wait_ge(gathered[k], 32 * (cols // RING + (k < 3)))
                    pool.wait_ge(old_ready[k], 16 * (cols // RING + (k < 2)))

            @block.tensor
            def _(pe):
                def turn_keys(c, k):
                    pe.wait_ge(listed, c * 2 + 2)
                    pe.wait_ge(compared, c + 1)
                    nc.tensor.transpose(keyrow[:, 0:P], key[:, k, 0:1].to_broadcast([P, P]), st.ident[:, :]).then_inc(row_ready, 1)

                turn_keys(0, 0)
                with pe.Fori(0, cols // RING) as i:
                    for k in range(RING):
                        c = i * RING + k
                        turn_keys(c + 1, (k + 1) % RING)
                        pe.wait_ge(scored, c + 1)
                        pe.wait_ge(spread_used, c + 1)
                        for h in range(HEADS):
                            last = nc.tensor.transpose(spread[:, k % 2, h, :], score[:, k, h:h + 1].to_broadcast([P, P]), st.ident[:, :])
                        last.then_inc(spread_ready, 1)

            @block.scalar
            def _(act):
                def put_lists(c, k):
                    nc.scalar.copy(index[:, k, :], lists[:, bass.ds(c, 1), :].rearrange("p o n -> p (o n)")).then_inc(listed, 1)
                    nc.scalar.copy(key[:, k, :], lists[:, bass.ds(c, 1), 2]).then_inc(listed, 1)

                def keep_column(c, k):
                    act.wait_ge(compared, c + 2)
                    nc.scalar.activation(apart[:, k, :], same[:, k, :], ACT.Copy, bias=FAR, scale=-FAR).then_inc(apart_ready, 1)
                    act.wait_ge(scored, c + 1)
                    nc.scalar.copy(scores[:, bass.ds(c, 1), :].rearrange("p o h -> p (o h)"), score[:, k, :])
                    act.wait_ge(steps, c * STEPS + CELL_STEP)
                    nc.scalar.copy(cells[:, bass.ds(c, 1)], cell[:, k, :])

                for k in range(3):
                    put_lists(k, k)
                keep_column(0, 0)
                with act.Fori(0, cols // RING) as i:
                    for k in range(RING):
                        c = i * RING + k
                        act.wait_ge(new_ready, c + 2)
                        put_lists(c + 3, (k + 3) % RING)
                        keep_column(c + 1, (k + 1) % RING)

            @block.vector
            def _(dve):
                def score_column(c, k, round):
                    link = Chain(dve, steps, c * STEPS)
                    dve.wait_ge(row_ready, c + 1)
                    nc.vector.tensor_scalar(same[:, k, :], keyrow[:, 0:P], key[:, k, 0:1], None, ALU.is_equal).then_inc(compared, 1)
                    dve.wait_ge(written[k], round * 16 + 16)
                    dve.wait_ge(compared, c + 2)
                    link.mark(nc.vector.tensor_tensor_reduce(junk[:, HEADS, :], same[:, k, :], below[:, :], 1.0, 0.0, ALU.mult, ALU.add,
                                                             repeated[:, k, 0:1]))
                    link(nc.vector.tensor_scalar(aside[:, k, :], key[:, k, :], -1.0, spare[:, 0:1], ALU.mult, ALU.add))
                    link(nc.vector.tensor_scalar(repeated[:, k, 1:2], repeated[:, k, 0:1], 0.0, None, ALU.is_gt))
                    link.mark(nc.vector.scalar_tensor_tensor(out=cell[:, k, :], in0=aside[:, k, :], scalar=repeated[:, k, 1:2],
                                                             in1=key[:, k, :], op0=ALU.mult, op1=ALU.add))
                    dve.wait_ge(gathered[k], round * 32 + 32)
                    link(nc.vector.tensor_tensor(product[:, k, :], q_in[:, k, :], k_in[:, k, :], ALU.mult))
                    nc.vector.tensor_reduce(score[:, k, :], product[:, k, :].rearrange("p (h e) -> p h e", e=HEAD), AX, ALU.add).then_inc(scored, 1)

                dve.wait_ge(tick, 3)
                link = Chain(dve, chain)
                link(nc.vector.tensor_copy(spare[:, :], spare_i[:, :]))
                dve.wait_ge(consts, 1)
                dve.sem_inc(compared, 1)
                dve.sem_inc(spread_used, 2)
                dve.sem_inc(new_ready, 2)
                score_column(0, 0, 0)
                with dve.Fori(0, cols // RING) as i:
                    for k in range(RING):
                        c = i * RING + k
                        score_column(c + 1, (k + 1) % RING, i + (k + 1) // RING)
                        dve.wait_ge(apart_ready, c + 1)
                        dve.wait_ge(spread_ready, c + 1)
                        dve.sem_inc(both_ready, 1)
                        link = Chain(dve, maxed, c * HEADS)
                        for h in range(HEADS):
                            link.mark(nc.vector.tensor_tensor_reduce(junk[:, h, :], spread[:, k % 2, h, :], apart[:, k, :], 1.0, -3e38,
                                                                     ALU.add, ALU.max, local[:, k, h:h + 1]))
                        link.settle()
                        dve.sem_inc(spread_used, 1)
                        dve.wait_ge(old_ready[k], i * 16 + 16)
                        nc.vector.tensor_tensor(new[:, k, :], local[:, k, :], old[:, k, :], ALU.max).then_inc(new_ready, 1)


def merge_maxima(nc, st, stage, max_tables):
    run = SEGMENTS // P * HEADS
    view = lambda table: table[0:SEGMENTS, :].rearrange("(p r) h -> p (r h)", p=P)
    with ExitStack() as ctx:
        sb, ps, sem = tools(nc, ctx, stage)
        part = sb("part", [P, len(max_tables), run])
        loaded, chain, stored = sem("loaded"), sem("chain"), sem("stored")
        with nc.Block() as block:

            @block.sync
            def _(sp):
                for k, table in enumerate(max_tables):
                    sp.dma_start(part[:, k, :], view(table)).then_inc(loaded, 16)
                sp.wait_ge(chain, len(max_tables) - 1)
                sp.dma_start(view(max_tables[0]), part[:, 0, :]).then_inc(stored, 16)
                sp.wait_ge(stored, 16)

            @block.vector
            def _(dve):
                link = Chain(dve, chain)
                dve.wait_ge(loaded, 16 * len(max_tables))
                for k in range(1, len(max_tables)):
                    link(nc.vector.tensor_tensor(part[:, 0, :], part[:, 0, :], part[:, k, :], ALU.max))


def segment_sums(nc, st, stage, lists, cells, scores, v_table, max_table, sum_tables):
    RING = 4
    cols = lists.shape[1] - AHEAD
    assert cols % RING == 0 and len(sum_tables) == 2
    with ExitStack() as ctx:
        sb, ps, sem = tools(nc, ctx, stage)
        spare_i = sb("spare_i", [P, 1], I32)
        zeros = sb("zeros", [P, SUMS])
        index = sb("index", [P, RING, 3], I32)
        cell = sb("cell", [P, RING, 1], I32)
        key = sb("key", [P, RING, 1])
        v_in = sb("v_in", [P, RING, D])
        top = sb("top", [P, RING, HEADS])
        same = sb("same", [P, RING, P])
        term = sb("term", [P, RING, SUMS])
        merged = sb("merged", [P, RING, SUMS])
        keyrow = ps("keyrow", [P, 512])
        sums = ps("sums", [P, 2, 512])
        tick, consts, steps = sem("tick"), sem("consts"), sem("steps")
        gathered = [sem(f"gathered{k}", pool_dma=True) for k in range(RING)]
        added = [sem(f"added{k}", pool_dma=True) for k in range(2)]
        indexed, row_ready, compared, shifted, exped, term_ready, sum_ready, merged_ready = (
            sem(n) for n in ("indexed", "row_ready", "compared", "shifted", "exped", "term_ready", "sum_ready", "merged_ready"))
        with nc.Block() as block:

            @block.gpsimd
            def _(pool):
                nc.gpsimd.iota(spare_i[:, :], pattern=[[0, 1]], base=SEGMENTS, channel_multiplier=1).then_inc(consts, 1)
                nc.gpsimd.memset(zeros[:, :], 0.0).then_inc(consts, 1)
                pool.wait_ge(consts, 2)
                for n in range(2):
                    for k in range(2):
                        if n:
                            pool.wait_ge(added[k], 16)
                        pool.indirect_dma_start(out=sum_tables[k], out_offset=bass.IndirectOffsetOnAxis(ap=spare_i[:, 0:1], axis=0),
                                                in_=zeros[:, :], in_offset=None, compute_op=ALU.add).then_inc(added[k], 16)

                def gather(c, k):
                    pool.wait_ge(indexed, c + 1)
                    pool.sem_inc(tick, 1)
                    pool.indirect_dma_start(out=v_in[:, k, :], out_offset=None, in_=v_table,
                                            in_offset=bass.IndirectOffsetOnAxis(ap=index[:, k, 0:1], axis=0)).then_inc(gathered[k], 16)
                    pool.indirect_dma_start(out=top[:, k, :], out_offset=None, in_=max_table,
                                            in_offset=bass.IndirectOffsetOnAxis(ap=index[:, k, 2:3], axis=0)).then_inc(gathered[k], 16)

                gather(0, 0)
                gather(1, 1)
                with pool.Fori(0, cols // RING) as i:
                    for pair in (0, 2):
                        for k in (pair, pair + 1):
                            gather(i * RING + k + 2, (k + 2) % RING)
                        for k in (pair, pair + 1):
                            pool.wait_ge(merged_ready, i * RING + k + 3)
                            pool.wait_ge(added[k % 2], i * 32 + pair * 8 + 32)
                            pool.sem_inc(tick, 1)
                            pool.indirect_dma_start(out=sum_tables[k % 2], out_offset=bass.IndirectOffsetOnAxis(ap=cell[:, k, 0:1], axis=0),
                                                    in_=merged[:, k, :], in_offset=None, compute_op=ALU.add).then_inc(added[k % 2], 16)
                for k in range(2):
                    pool.wait_ge(added[k], 32 + 16 * (cols // 2))
                for k in range(RING):
                    pool.wait_ge(gathered[k], 32 * (cols // RING + (k < 2)))

            @block.tensor
            def _(pe):
                with pe.Fori(0, cols // RING) as i:
                    for pair in (0, 2):
                        for k in (pair, pair + 1):
                            c = i * RING + k
                            pe.wait_ge(indexed, c + 1)
                            pe.wait_ge(compared, c + 1)
                            nc.tensor.transpose(keyrow[:, 0:P], key[:, k, 0:1].to_broadcast([P, P]), st.ident[:, :]).then_inc(row_ready, 1)
                        for k in (pair, pair + 1):
                            c = i * RING + k
                            pe.wait_ge(term_ready, c + 2)
                            pe.wait_ge(merged_ready, c + 1)
                            nc.tensor.matmul(sums[:, k % 2, 0:SUMS], same[:, k, :], term[:, k, :], start=True, stop=True).then_inc(sum_ready, 1)

            @block.scalar
            def _(act):
                act.sem_inc(merged_ready, 2)
                with act.Fori(0, cols // RING) as i:
                    for pair in (0, 2):
                        for k in (pair, pair + 1):
                            act.wait_ge(shifted, i * RING + k + 1)
                            nc.scalar.activation(term[:, k, D:SUMS], top[:, k, :], ACT.Exp).then_inc(exped, 1)
                        for k in (pair, pair + 1):
                            act.wait_ge(sum_ready, i * RING + k + 1)
                            act.wait_ge(added[k % 2], i * 32 + pair * 8 + 16)
                            nc.scalar.copy(merged[:, k, :], sums[:, k % 2, 0:SUMS]).then_inc(merged_ready, 1)

            @block.vector
            def _(dve):
                STEPS = 3
                dve.sem_inc(compared, 1)
                dve.sem_inc(term_ready, 1)

                def fetch_lists(c, k, before):
                    nc.vector.tensor_copy(key[:, k, :], lists[:, bass.ds(c, 1), 2]).then_inc(steps, 1)
                    nc.vector.tensor_copy(index[:, k, :], lists[:, bass.ds(c, 1), :].rearrange("p o n -> p (o n)")).then_inc(steps, 1)
                    dve.wait_ge(steps, before + 2)
                    dve.sem_inc(indexed, 1)

                fetch_lists(0, 0, 0)
                fetch_lists(1, 1, 2)
                with dve.Fori(0, cols // RING) as i:
                    for pair in (0, 2):
                        dve.wait_ge(term_ready, i * RING + pair + 1)
                        for n in range(2):
                            k = pair + n
                            fetch_lists(i * RING + k + 2, (k + 2) % RING, (i * RING + pair) * STEPS + 4 + 2 * n)
                        for n in range(2):
                            k = pair + n
                            c = i * RING + k
                            dve.wait_ge(added[k % 2], i * 32 + pair * 8 + 16)
                            nc.vector.tensor_copy(cell[:, k, :], cells[:, bass.ds(c, 1)]).then_inc(steps, 1)
                            dve.wait_ge(row_ready, c + 1)
                            nc.vector.tensor_scalar(same[:, k, :], keyrow[:, 0:P], key[:, k, 0:1], None, ALU.is_equal).then_inc(compared, 1)
                        for n in range(2):
                            k = pair + n
                            dve.wait_ge(gathered[k], i * 32 + 32)
                            nc.vector.tensor_tensor(top[:, k, :], scores[:, bass.ds(i * RING + k, 1), :].rearrange("p o h -> p (o h)"), top[:, k, :],
                                                    ALU.subtract).then_inc(shifted, 1)
                        for n in range(2):
                            k = pair + n
                            dve.wait_ge(exped, i * RING + k + 1)
                            nc.vector.tensor_tensor(term[:, k, 0:D].rearrange("p (h e) -> p h e", e=HEAD), v_in[:, k, :].rearrange("p (h e) -> p h e", e=HEAD),
                                                    term[:, k, D:SUMS].unsqueeze(2).to_broadcast([P, HEADS, HEAD]), ALU.mult).then_inc(term_ready, 1)


def average_segments(nc, st, stage, sum_tables, dst):
    view = [table[0:SEGMENTS, :].rearrange("(t p r) f -> t p r f", p=P, r=RELATIONS) for table in sum_tables]
    with ExitStack() as ctx:
        sb, ps, sem = tools(nc, ctx, stage)
        s = sb("sums_in", [P, 3, RELATIONS, SUMS])
        more = sb("more_in", [P, 3, RELATIONS, SUMS])
        inverse = sb("inverse", [P, RELATIONS, HEADS])
        present = sb("present", [P, RELATIONS])
        count = sb("count", [P, 1])
        loaded = [sem(f"loaded{k}") for k in range(3)]
        chain, used, summed = sem("chain"), sem("used"), sem("summed")
        with nc.Block() as block:

            @block.sync
            def _(sp):
                for t in range(TILES):
                    if t >= 3:
                        sp.wait_ge(used, t - 2)
                    sp.dma_start(s[:, t % 3, :, :], view[0][t]).then_inc(loaded[t % 3], 16)
                    sp.dma_start(more[:, t % 3, :, :], view[1][t]).then_inc(loaded[t % 3], 16)

            @block.gpsimd
            def _(pool):
                for t in range(TILES):
                    pool.wait_ge(loaded[t % 3], 32 * (t // 3 + 1))
                    nc.gpsimd.tensor_tensor(s[:, t % 3, :, :], s[:, t % 3, :, :], more[:, t % 3, :, :], ALU.add).then_inc(summed, 1)

            @block.vector
            def _(dve):
                link = Chain(dve, chain)
                for t in range(TILES):
                    dve.wait_ge(summed, t + 1)
                    weights = s[:, t % 3, :, D:SUMS]
                    link.mark(nc.vector.tensor_scalar(present[:, :], weights[:, :, 0], 0.0, None, ALU.is_gt))
                    link(nc.vector.tensor_scalar(inverse[:, :, :], weights, 1e-30, None, ALU.max))
                    link.mark(nc.vector.tensor_reduce(count[:, :], present[:, :], AX, ALU.add))
                    link(nc.vector.reciprocal(inverse[:, :, :], inverse[:, :, :]))
                    link(nc.vector.tensor_scalar(count[:, :], count[:, :], 1.0, None, ALU.max))
                    link(nc.vector.reciprocal(count[:, :], count[:, :]))
                    own = s[:, t % 3, :, 0:D].rearrange("p r (h e) -> p r h e", e=HEAD)
                    link(nc.vector.tensor_tensor(own, own, inverse[:, :, :].unsqueeze(3).to_broadcast([P, RELATIONS, HEADS, HEAD]), ALU.mult))
                    nc.vector.tensor_reduce(dst[:, t, :], s[:, t % 3, :, 0:D].rearrange("p r f -> p f r"), AX, ALU.add).then_inc(used, 1)
                    dve.wait_ge(used, t + 1)
                    link(nc.vector.tensor_scalar(dst[:, t, :], dst[:, t, :], count[:, 0:1], None, ALU.mult))


def blend_nodes(nc, st, stage, trans, keep):
    with ExitStack() as ctx:
        sb, ps, sem = tools(nc, ctx, stage)
        rest = sb("rest", [P, TILES])
        chain = sem("chain")
        with nc.Block() as block:

            @block.vector
            def _(dve):
                link = Chain(dve, chain)
                link(nc.vector.tensor_scalar(rest[:, :], keep[:, :], -1.0, 1.0, ALU.mult, ALU.add))
                for t in range(TILES):
                    link.mark(nc.vector.scalar_tensor_tensor(out=st.x[:, t, :], in0=trans[:, t, :], scalar=keep[:, t:t + 1],
                                                             in1=st.x[:, t, :], op0=ALU.mult, op1=ALU.add))
                link.settle()
                for t in range(TILES):
                    link.mark(nc.vector.scalar_tensor_tensor(out=st.x[:, t, :], in0=st.a[:, t, :], scalar=rest[:, t:t + 1],
                                                             in1=st.x[:, t, :], op0=ALU.mult, op1=ALU.add))


def layer2_gnn(nc, st, d, max_tables, sum_tables):
    dram = lambda name, rows, cols: nc.dram_tensor(name, (rows, cols), F32, kind="Internal").ap()
    q_table = dram("query_rows", NP, D)
    k_table = dram("key_rows", SEGMENTS, D)
    v_table = dram("value_rows", SEGMENTS, D)
    cols = edge_columns(d["src"].shape[0])
    norm_nodes(nc, st, "l2_norm", st.x, st.a, True)
    with ExitStack() as ctx:
        sb, ps, sem = tools(nc, ctx, "l2")
        type_masks, keep = sb("type_masks", [P, TYPES, TILES]), sb("keep", [P, TILES])
        typesT = sb("types_transposed", [TYPES, NP])
        load_types(nc, st, "l2_types", d["node_type_4"], d["L2_gnn_skip"], type_masks, typesT, keep)
        with ExitStack() as values:
            v = values.enter_context(nc.sbuf_tensor("l2_values", [P, TILES, D], F32))
            typed_linear(nc, st, "l2_query", type_masks, typesT, d["L2_gnn_Wq"], d["L2_gnn_bq"], st.b)
            store_rows(nc, st, "l2_query_rows", st.b, q_table)
            typed_linear(nc, st, "l2_value", type_masks, typesT, d["L2_gnn_Wv"], d["L2_gnn_bv"], v)
            typed_linear(nc, st, "l2_key", type_masks, typesT, d["L2_gnn_Wk"], d["L2_gnn_bk"], st.b)
            transpose_nodes(nc, st, "l2_turn_key", st.b)
            relate_rows(nc, st, "l2_relate_key", d["L2_gnn_rel_att"], d["L2_gnn_rel_pri"], k_table)
            transpose_nodes(nc, st, "l2_turn_value", v)
            relate_rows(nc, st, "l2_relate_value", d["L2_gnn_rel_msg"], None, v_table)
        with ExitStack() as edges:
            own = lambda name, shape, dt=F32: edges.enter_context(nc.sbuf_tensor(f"l2_{name}", shape, dt))
            lists = own("lists", [P, cols + AHEAD, 3], I32)
            cells, scores = own("cells", [P, cols + 1], I32), own("scores", [P, cols + 1, HEADS])
            edge_lists(nc, st, "l2_lists", d["src"], d["dst"], d["edge_type_8"], lists)
            segment_maxima(nc, st, "l2_maxima", lists, cells, scores, q_table, k_table, max_tables)
            merge_maxima(nc, st, "l2_merge", max_tables)
            segment_sums(nc, st, "l2_sums", lists, cells, scores, v_table, max_tables[0], sum_tables)
        average_segments(nc, st, "l2_average", sum_tables, st.b)
        transpose_nodes(nc, st, "l2_turn_average", st.b)
        typed_linear(nc, st, "l2_out", type_masks, typesT, d["L2_gnn_Wa"], d["L2_gnn_ba"], st.b)
        blend_nodes(nc, st, "l2_blend", st.b, keep)


def score_experts(nc, st, stage, agg, gamma, beta, scores, heads, experts):
    W = heads * experts
    with ExitStack() as ctx:
        sb, ps, sem = tools(nc, ctx, stage)
        g, b = sb("gamma", [P, W]), sb("beta", [P, W])
        mean, rstd = sb("mean", [P, TILES]), sb("rstd", [P, TILES])
        square = sb("square", [P, TILES, W])
        loaded, chain, floored, rooted = sem("loaded"), sem("chain"), sem("floored"), sem("rooted")
        with nc.Block() as block:

            @block.sync
            def _(sp):
                sp.dma_start(g[:, :], gamma.partition_broadcast(P)).then_inc(loaded, 16)
                sp.dma_start(b[:, :], beta.partition_broadcast(P)).then_inc(loaded, 16)

            @block.scalar
            def _(act):
                act.wait_ge(floored, 1)
                nc.scalar.activation(rstd[:, :], rstd[:, :], ACT.Sqrt).then_inc(rooted, 1)

            @block.vector
            def _(dve):
                link = Chain(dve, chain)
                by_node = lambda a: a[:, :].unsqueeze(2).to_broadcast([P, TILES, W])
                by_column = lambda a: a[:, :].unsqueeze(1).to_broadcast([P, TILES, W])
                v = agg[:, :, :]
                link(nc.vector.tensor_reduce(mean[:, :], v, AX, ALU.add))
                link(nc.vector.tensor_scalar(mean[:, :], mean[:, :], 1.0 / W, None, ALU.mult))
                link(nc.vector.tensor_tensor(v, v, by_node(mean), ALU.subtract))
                link(nc.vector.tensor_tensor(square[:, :, :], v, v, ALU.mult))
                link(nc.vector.tensor_reduce(rstd[:, :], square[:, :, :], AX, ALU.add))
                nc.vector.tensor_scalar(rstd[:, :], rstd[:, :], 1.0 / W, LN_EPS, ALU.mult, ALU.add).then_inc(floored, 1)
                dve.wait_ge(rooted, 1)
                link(nc.vector.reciprocal(rstd[:, :], rstd[:, :]))
                link(nc.vector.tensor_tensor(v, v, by_node(rstd), ALU.mult))
                dve.wait_ge(loaded, 32)
                link(nc.vector.tensor_tensor(v, v, by_column(g), ALU.mult))
                link(nc.vector.tensor_tensor(v, v, by_column(b), ALU.add))
                link(nc.vector.tensor_reduce(scores[:, :, :], agg[:, :, :].rearrange("p t (h e) -> p t e h", h=heads), AX, ALU.add))
                link(nc.vector.tensor_scalar(scores[:, :, :], scores[:, :, :], 1.0 / heads, None, ALU.mult))


def mixture(nc, st, stage, ex, acc):
    with ExitStack() as ctx:
        gates = ctx.enter_context(nc.sbuf_tensor(f"{stage}_gates", [P, ex.experts, TILES], F32))
        gate_nodes(nc, st, stage + "_gate", ex, gates)
        mix_experts(nc, st, stage + "_mix", ex, gates, acc)


def layer0_ffn(nc, st, d, slots):
    ex = Experts(16, 512, d["L0_ffn_gate_w"], d["L0_ffn_gate_b"], [(d["L0_ffn_w1"], d["L0_ffn_b1"])],
                 d["L0_ffn_w2"], d["L0_ffn_b2"], True, ACT.Relu)
    norm_nodes(nc, st, "f0_norm", st.x, st.a, True)
    best_two(nc, st, "f0", ex, *slots, st.a)
    norm_add(nc, st, "f0_add", d["L0_ffn_gamma"], d["L0_ffn_beta"])


def layer1_ffn(nc, st, d, slots):
    ex = Experts(8, 512, d["L1_ffn_Wg"], d["L1_ffn_bg"], [(d["L1_ffn_W1"], d["L1_ffn_b1"])],
                 d["L1_ffn_W2"], d["L1_ffn_b2"], True, ACT.Relu, router_bias2=d["L1_ffn_bias"])
    norm_nodes(nc, st, "f1_norm", st.x, st.a, True)
    best_two(nc, st, "f1", ex, *slots, st.x)


def layer2_ffn(nc, st, d):
    norms = [[d[f"L2_ffn_{a}{l}"] for a in ("g", "be", "m", "v")] for l in (1, 2)]
    ex = Experts(8, 256, d["L2_ffn_Wr"], d["L2_ffn_br"],
                 [(d["L2_ffn_W1"], d["L2_ffn_b1"]), (d["L2_ffn_W2"], d["L2_ffn_b2"])],
                 d["L2_ffn_Wo"], d["L2_ffn_bo"], False, ACT.Relu, norms=norms)
    norm_nodes(nc, st, "f2_norm", st.x, st.a, True)
    mixture(nc, st, "f2", ex, st.x)


def layer3_ffn(nc, st, d, table, mask, slots):
    heads, experts = d["L3_ffn_att_src"].shape
    ex = Experts(experts, 512, None, None, [(d["L3_ffn_W1"], d["L3_ffn_b1"])],
                 d["L3_ffn_W2"], d["L3_ffn_b2"], True, ACT.Gelu)
    norm_nodes(nc, st, "f3_norm", st.x, st.a, True)
    att = Attention(st, heads, experts)
    with ExitStack() as ctx:
        sb, ps, sem = tools(nc, ctx, "f3")
        agg, scores = sb("agg", [P, TILES, heads * experts]), sb("expert_scores", [P, TILES, experts])
        attend(nc, st, "f3a", att, table, mask, d["L3_ffn_W_gat"], d["L3_ffn_att_src"], d["L3_ffn_att_dst"],
               Averaged(att, agg, d["L3_ffn_b_gat"]))
        score_experts(nc, st, "f3_scores", agg, d["L3_ffn_ln_gamma"], d["L3_ffn_ln_beta"], scores, heads, experts)
        best_two(nc, st, "f3", ex, *slots, st.x, given=scores)


def network(nc, d, out):
    SEMAPHORES.__init__()
    with ExitStack() as ctx:
        dram = lambda name, shape, dt=F32: nc.dram_tensor(name, shape, dt, kind="Internal").ap()
        count_table, weight_table, count_table2 = (dram(n, (CELLS, 1)) for n in ("edge_counts", "edge_weights", "edge_counts2"))
        mask, mask2 = dram("edge_mask", (NP, NP), BF16), dram("edge_mask2", (NP, NP), BF16)
        max_tables = [dram(f"segment_maxima{k}", (SEGMENTS + P, HEADS)) for k in range(4)]
        sum_tables = [dram(f"segment_sums{k}", (SEGMENTS + P, SUMS)) for k in range(2)]
        slots = dram("slot_rows", ((WINDOWS + RING3) * P, D)), dram("slot_outs", (WINDOWS * P, D))
        st = State(nc, ctx, d)
        load_nodes(nc, st, "load", d["x"])
        fill_tables(nc, "clear", [count_table, weight_table, count_table2], 0.0, 10)
        pairs = d["L3_ffn_edge_index"]
        build_tables(nc, st, "build", d["src"], d["dst"], d["edge_weight"], pairs[0, :], pairs[1, :],
                     count_table, weight_table, count_table2,
                     slots[:1], max_tables)
        degree_factors(nc, st, "factors")
        layer0_gnn(nc, st, d, count_table, mask, sum_tables[0])
        layer0_ffn(nc, st, d, slots)
        layer1_gnn(nc, st, d, weight_table, sum_tables[1], count_table2, mask2)
        layer1_ffn(nc, st, d, slots)
        layer2_gnn(nc, st, d, max_tables, sum_tables)
        layer2_ffn(nc, st, d)
        layer3_gnn(nc, st, d, count_table, mask)
        layer3_ffn(nc, st, d, count_table2, mask2, slots)
        store_nodes(nc, st, "store", out)
        SEMAPHORES.clear(nc)




def kernel(**inputs):
    import numpy as _np
    import concourse.bacc as _bacc
    from concourse import mybir as _mybir
    from concourse.bass_utils import run_bass_kernel_spmd as _run

    nc = _bacc.Bacc("TRN2", target_bir_lowering=False, num_devices=1)
    arrays, d = {}, {}
    for name, value in inputs.items():
        a = _np.ascontiguousarray(value)
        arrays[f"in_{name}"] = a
        d[name] = nc.dram_tensor(f"in_{name}", a.shape, _mybir.dt.from_np(a.dtype), kind="ExternalInput").ap()
    out = nc.dram_tensor("out_nodes", inputs["x"].shape, _mybir.dt.float32, kind="ExternalOutput").ap()
    network(nc, d, out)
    r = _run(nc, [arrays], core_ids=[0])
    return r.results[0]["out_nodes"]



RING3 = 3
windows_of = lambda experts: -(-((2 * TILES * P + experts * (P - 1)) // P) // RING3) * RING3
WINDOWS = windows_of(16)


class Picks:

    def __init__(self, nc, ctx, stage, experts):
        sb = lambda name, shape, dt=F32: ctx.enter_context(nc.sbuf_tensor(f"{stage}_{name}", shape, dt))
        self.windows = windows_of(experts)
        self.hot = sb("hot", [P, 2, TILES, experts])
        self.gate = sb("gate", [P, 2, TILES])
        self.place = sb("place", [P, 2, TILES], I32)
        self.owners = sb("owners", [P, self.windows + RING3])


def number_slots(nc, st, stage, ex, picks):
    E, W = ex.experts, picks.windows + RING3
    TE = TILES * E
    with ExitStack() as ctx:
        sb, ps, sem = tools(nc, ctx, stage)
        both = sb("both", [P, TILES, E])
        before = sb("before", [P, P])
        ones = sb("ones", [P, P])
        numbers_i, numbers = sb("numbers_i", [P, W], I32), sb("numbers", [P, W])
        lane_i, lane = sb("lane_i", [P, 1], I32), sb("lane", [P, 1])
        starts = sb("starts", [P, TILES + 1, E])
        beyond = sb("beyond", [P, E, TILES])
        used = sb("used", [P, E])
        first = sb("first", [P, E + 1])
        rank = sb("rank", [P, TILES, E])
        slot = sb("slot", [P, 2, TILES])
        passed = sb("passed", [P, W, E])
        ranks, totals = ps("ranks", [P, 512]), ps("totals", [P, 512])
        consts, chain, summed, counted = sem("consts"), sem("chain"), sem("summed"), sem("counted")
        with nc.Block() as block:

            @block.gpsimd
            def _(pool):
                nc.gpsimd.iota(numbers_i[:, :], pattern=[[1, W]], base=0, channel_multiplier=0).then_inc(consts, 1)
                nc.gpsimd.iota(lane_i[:, :], pattern=[[0, 1]], base=0, channel_multiplier=1).then_inc(consts, 1)
                nc.gpsimd.memset(ones[:, :], 1.0).then_inc(consts, 1)
                nc.gpsimd.memset(before[:, :], 1.0).then_inc(consts, 1)
                pool.wait_ge(consts, 4)
                nc.gpsimd.affine_select(out=before[:, :], in_=before[:, :], compare_op=ALU.is_gt, fill=0.0, base=0,
                                        pattern=[[1, P]], channel_multiplier=-1).then_inc(consts, 1)

            @block.tensor
            def _(pe):
                pe.wait_ge(consts, 5)
                pe.wait_ge(counted, 1)
                flat = both[:, :, :].rearrange("p t e -> p (t e)")
                nc.tensor.matmul(ranks[:, 0:TE], before[:, :], flat, start=True, stop=True).then_inc(summed, 1)
                nc.tensor.matmul(totals[:, 0:TE], ones[:, :], flat, start=True, stop=True).then_inc(summed, 1)

            @block.vector
            def _(dve):
                link = Chain(dve, chain)
                nc.vector.tensor_tensor(both[:, :, :], picks.hot[:, 0, :, :], picks.hot[:, 1, :, :], ALU.add).then_inc(counted, 1)
                link.mark(nc.vector.memset(starts[:, 0, :], 0.0))
                link.mark(nc.vector.memset(first[:, 0:1], 0.0))
                dve.wait_ge(consts, 5)
                link.mark(nc.vector.tensor_copy(numbers[:, :], numbers_i[:, :]))
                link.mark(nc.vector.tensor_copy(lane[:, :], lane_i[:, :]))
                link.settle()
                dve.wait_ge(summed, 2)
                for t in range(TILES):
                    link(nc.vector.tensor_tensor(starts[:, t + 1, :], starts[:, t, :], totals[:, t * E:(t + 1) * E], ALU.add))
                link(nc.vector.tensor_scalar(beyond[:, 0, :], numbers[:, 0:TILES], float(P), None, ALU.mult))
                for e in range(E - 1, -1, -1):
                    link(nc.vector.tensor_scalar(beyond[:, e, :], beyond[:, 0, :], starts[:, TILES, e:e + 1], None, ALU.is_lt))
                link(nc.vector.tensor_reduce(used[:, :], beyond[:, :, :], AX, ALU.add))
                for e in range(E):
                    link(nc.vector.tensor_tensor(first[:, e + 1:e + 2], first[:, e:e + 1], used[:, e:e + 1], ALU.add))
                link(nc.vector.tensor_tensor(rank[:, :, :], starts[:, 0:TILES, :], ranks[:, 0:TE].rearrange("p (t e) -> p t e", e=E), ALU.add))
                link(nc.vector.tensor_scalar(used[:, :], first[:, 0:E], float(P), None, ALU.mult))
                link(nc.vector.tensor_tensor(rank[:, :, :], rank[:, :, :], used[:, :].unsqueeze(1).to_broadcast([P, TILES, E]), ALU.add))
                for j in range(2):
                    link(nc.vector.tensor_tensor(both[:, :, :], picks.hot[:, j, :, :], rank[:, :, :], ALU.mult))
                    link(nc.vector.tensor_reduce(slot[:, j, :], both[:, :, :], AX, ALU.add))
                link(nc.vector.tensor_copy(picks.place[:, :, :], slot[:, :, :]))
                link(nc.vector.tensor_copy(passed[:, :, :], first[:, 1:E + 1].unsqueeze(1).to_broadcast([P, W, E])))
                link(nc.vector.tensor_tensor(passed[:, :, :], passed[:, :, :], numbers[:, :].unsqueeze(2).to_broadcast([P, W, E]), ALU.is_le))
                link(nc.vector.tensor_reduce(numbers[:, :], passed[:, :, :], AX, ALU.add))
                link(nc.vector.tensor_scalar(numbers[:, :], numbers[:, :], float(E - 1), None, ALU.min))
                link(nc.vector.tensor_scalar(picks.owners[:, :], numbers[:, :], float(P), lane[:, 0:1], ALU.mult, ALU.add))


def send_nodes(nc, st, stage, picks, slot_rows):
    with ExitStack() as ctx:
        sb, ps, sem = tools(nc, ctx, stage)
        sent = sem("sent", pool_dma=True)
        with nc.Block() as block:

            @block.gpsimd
            def _(pool):
                for t in range(TILES):
                    for j in range(2):
                        pool.indirect_dma_start(out=slot_rows, out_offset=bass.IndirectOffsetOnAxis(ap=picks.place[:, j, t:t + 1], axis=0),
                                                in_=st.a[:, t, :], in_offset=None).then_inc(sent, 16)
                pool.wait_ge(sent, 16 * 2 * TILES)


def expert_windows(nc, st, stage, ex, picks, slot_rows, slot_outs):
    H = ex.hidden
    HC = H // P
    W = picks.windows
    first_rows = ex.layers[0][0].rearrange("e (p c) h -> (e p) (c h)", c=KC)
    last_rows = ex.w_out.rearrange("e (p j) d -> (e p) (j d)", j=HC)
    bias_rows = ex.layers[0][1].rearrange("e (p j) -> (e p) j", j=HC)
    with ExitStack() as ctx:
        sb, ps, sem = tools(nc, ctx, stage)
        index_first = sb("index_first", [P, RING3, 1], I32)
        index_last = sb("index_last", [P, RING3, 1], I32)
        w_first = sb("w_first", [P, RING3, KC, H])
        w_last = sb("w_last", [P, RING3, HC, D])
        b_first = sb("b_first", [P, RING3, HC])
        rows = sb("rows", [P, RING3, D])
        rowsT = sb("rows_transposed", [P, RING3, KC, P])
        hidden = sb("hidden", [P, RING3, HC, P])
        y = sb("y", [P, RING3, D])
        turned = ps("turned", [P, 512])
        pre = ps("pre", [P, RING3, 512])
        post = ps("post", [P, RING3, 512])
        listed_first, listed_last, tick, rows_turned, turned_out, pre_ready, hidden_ready, post_ready, y_ready = (
            sem(n) for n in ("listed_first", "listed_last", "tick", "rows_turned", "turned_out", "pre_ready", "hidden_ready", "post_ready", "y_ready"))
        rows_loaded = [sem(f"rows_loaded{k}") for k in range(RING3)]
        stored = [sem(f"stored{k}") for k in range(RING3)]
        first_fetched = [sem(f"first_fetched{k}", pool_dma=True) for k in range(RING3)]
        last_fetched = [sem(f"last_fetched{k}", pool_dma=True) for k in range(RING3)]
        window = lambda table, w: table[bass.ds(w * P, P), :]
        with nc.Block() as block:

            @block.sync
            def _(sp):
                for k in range(RING3):
                    sp.sem_inc(stored[k], 16)
                    sp.dma_start(rows[:, k, :], slot_rows[k * P:(k + 1) * P, :]).then_inc(rows_loaded[k], 16)
                with sp.Fori(0, W // RING3) as i:
                    for k in range(RING3):
                        w = i * RING3 + k
                        sp.wait_ge(rows_turned, w + 1)
                        sp.dma_start(rows[:, k, :], window(slot_rows, w + 3)).then_inc(rows_loaded[k], 16)
                        sp.wait_ge(y_ready, w + 4)
                        sp.dma_start(window(slot_outs, w), y[:, k, :]).then_inc(stored[k], 16)
                for k in range(RING3):
                    sp.wait_ge(rows_loaded[k], 16 * (W // RING3 + 1))
                    sp.wait_ge(stored[k], 16 * (W // RING3 + 1))

            @block.gpsimd
            def _(pool):
                def fetch(out, table, index, fetched):
                    pool.indirect_dma_start(out=out, out_offset=None, in_=table,
                                            in_offset=bass.IndirectOffsetOnAxis(ap=index, axis=0)).then_inc(fetched, 16)

                def fetch_first(k):
                    fetch(w_first[:, k, :, :].rearrange("p c h -> p (c h)"), first_rows, index_first[:, k, 0:1], first_fetched[k])
                    fetch(b_first[:, k, :], bias_rows, index_first[:, k, 0:1], first_fetched[k])

                def fetch_last(k):
                    fetch(w_last[:, k, :, :].rearrange("p j d -> p (j d)"), last_rows, index_last[:, k, 0:1], last_fetched[k])

                for k in range(RING3):
                    pool.wait_ge(listed_first, k + 1)
                    fetch_first(k)
                    if k < 2:
                        pool.wait_ge(listed_last, k + 1)
                        fetch_last(k)
                with pool.Fori(0, W // RING3) as i:
                    for k in range(RING3):
                        w = i * RING3 + k
                        pool.wait_ge(listed_first, w + 4)
                        pool.wait_ge(hidden_ready, w + 1)
                        pool.sem_inc(tick, 1)
                        fetch_first(k)
                        pool.wait_ge(listed_last, w + 3)
                        pool.wait_ge(y_ready, w + 3)
                        pool.sem_inc(tick, 1)
                        fetch_last((k + 2) % RING3)
                for k in range(RING3):
                    pool.wait_ge(first_fetched[k], 32 * (W // RING3 + 1))
                    pool.wait_ge(last_fetched[k], 16 * (W // RING3 + (k < 2)))

            @block.tensor
            def _(pe):
                def turn(w, k, round):
                    pe.wait_ge(rows_loaded[k], round * 16 + 16)
                    pe.wait_ge(turned_out, w + 1)
                    for c in range(KC):
                        last = nc.tensor.transpose(turned[:, c * P:(c + 1) * P], rows[:, k, c:D:KC], st.ident[:, :])
                    last.then_inc(rows_turned, 1)

                def first_layer(w, k, round):
                    pe.wait_ge(turned_out, w + 2)
                    pe.wait_ge(first_fetched[k], round * 32 + 32)
                    for j in range(HC):
                        for c in range(KC):
                            last = nc.tensor.matmul(pre[:, k, j * P:(j + 1) * P], w_first[:, k, c, j:H:HC], rowsT[:, k, c, :],
                                                    start=(c == 0), stop=(c == KC - 1))
                    last.then_inc(pre_ready, 1)

                pe.sem_inc(pre_ready, 1)
                pe.sem_inc(post_ready, 3)
                turn(0, 0, 0)
                turn(1, 1, 0)
                first_layer(0, 0, 0)
                with pe.Fori(0, W // RING3) as i:
                    for k in range(RING3):
                        w = i * RING3 + k
                        first_layer(w + 1, (k + 1) % RING3, i + (k + 1) // RING3)
                        turn(w + 2, (k + 2) % RING3, i + (k + 2) // RING3)
                        pe.wait_ge(hidden_ready, w + 1)
                        pe.wait_ge(last_fetched[k], i * 16 + 16)
                        pe.wait_ge(y_ready, w + 1)
                        for j in range(HC):
                            last = nc.tensor.matmul(post[:, k, 0:D], hidden[:, k, j, :], w_last[:, k, j, :],
                                                    start=(j == 0), stop=(j == HC - 1))
                        last.then_inc(post_ready, 1)

            @block.scalar
            def _(act):
                def list_first(w, k):
                    nc.scalar.copy(index_first[:, k, :], picks.owners[:, bass.ds(w, 1)]).then_inc(listed_first, 1)

                def list_last(w, k):
                    nc.scalar.copy(index_last[:, k, :], picks.owners[:, bass.ds(w, 1)]).then_inc(listed_last, 1)

                def activate(w, k):
                    act.wait_ge(pre_ready, w + 2)
                    act.wait_ge(post_ready, w + 1)
                    for j in range(HC):
                        last = nc.scalar.activation(hidden[:, k, j, :], pre[:, k, j * P:(j + 1) * P], ex.func, bias=b_first[:, k, j:j + 1])
                    last.then_inc(hidden_ready, 1)

                for k in range(RING3):
                    list_first(k, k)
                    if k < 2:
                        list_last(k, k)
                activate(0, 0)
                with act.Fori(0, W // RING3) as i:
                    for k in range(RING3):
                        w = i * RING3 + k
                        list_first(w + 3, k)
                        activate(w + 1, (k + 1) % RING3)
                        list_last(w + 2, (k + 2) % RING3)

            @block.vector
            def _(dve):
                def take_turned(w, k):
                    dve.wait_ge(rows_turned, w + 1)
                    nc.vector.tensor_copy(rowsT[:, k, :, :].rearrange("p c n -> p (c n)"), turned[:, 0:D]).then_inc(turned_out, 1)

                dve.sem_inc(turned_out, 1)
                dve.sem_inc(y_ready, 3)
                take_turned(0, 0)
                take_turned(1, 1)
                with dve.Fori(0, W // RING3) as i:
                    for k in range(RING3):
                        w = i * RING3 + k
                        dve.wait_ge(pre_ready, w + 1)
                        take_turned(w + 2, (k + 2) % RING3)
                        dve.wait_ge(post_ready, w + 4)
                        dve.wait_ge(stored[k], i * 16 + 16)
                        nc.vector.tensor_copy(y[:, k, :], post[:, k, 0:D]).then_inc(y_ready, 1)


def collect_nodes(nc, st, stage, ex, picks, slot_outs, acc):
    RING = 4
    E = ex.experts
    with ExitStack() as ctx:
        sb, ps, sem = tools(nc, ctx, stage)
        got = sb("got", [P, RING, 2, D])
        b_last = sb("b_last", [E, D])
        gates = sb("gates", [P, 2, TILES, E])
        gatesT = sb("gates_transposed", [E, 2, P])
        turned = ps("turned", [E, 2, 512])
        biased = ps("biased", [P, 2, 512])
        gathered = [sem(f"gathered{k}", pool_dma=True) for k in range(RING)]
        chain, used, loaded, spread, transposed, copied, biases_ready = (
            sem(n) for n in ("chain", "used", "loaded", "spread", "transposed", "copied", "biases_ready"))
        with nc.Block() as block:

            @block.sync
            def _(sp):
                sp.dma_start(b_last[:, :], ex.b_out).then_inc(loaded, 16)

            @block.gpsimd
            def _(pool):
                for t in range(TILES):
                    if t >= RING:
                        pool.wait_ge(used, t - RING + 1)
                    for j in range(2):
                        pool.indirect_dma_start(out=got[:, t % RING, j, :], out_offset=None, in_=slot_outs,
                                                in_offset=bass.IndirectOffsetOnAxis(ap=picks.place[:, j, t:t + 1], axis=0)).then_inc(gathered[t % RING], 16)

            @block.tensor
            def _(pe):
                pe.wait_ge(loaded, 16)
                pe.wait_ge(spread, 1)
                for t in range(TILES):
                    if t >= 2:
                        pe.wait_ge(copied, t - 1)
                    nc.tensor.transpose(turned[:, t % 2, 0:P], gates[:, 0, t, :], st.ident[:, :]).then_inc(transposed, 1)
                    pe.wait_ge(copied, t + 1)
                    if t >= 2:
                        pe.wait_ge(used, t - 1)
                    nc.tensor.matmul(biased[:, t % 2, 0:D], gatesT[:, t % 2, :], b_last[:, :], start=True, stop=True).then_inc(biases_ready, 1)

            @block.scalar
            def _(act):
                for t in range(TILES):
                    act.wait_ge(transposed, t + 1)
                    if t >= 2:
                        act.wait_ge(biases_ready, t - 1)
                    nc.scalar.copy(gatesT[:, t % 2, :], turned[:, t % 2, 0:P]).then_inc(copied, 1)

            @block.vector
            def _(dve):
                link = Chain(dve, chain)
                for j in range(2):
                    link(nc.vector.tensor_tensor(gates[:, j, :, :], picks.hot[:, j, :, :],
                                                 picks.gate[:, j, :].unsqueeze(2).to_broadcast([P, TILES, E]), ALU.mult))
                nc.vector.tensor_tensor(gates[:, 0, :, :], gates[:, 0, :, :], gates[:, 1, :, :], ALU.add).then_inc(spread, 1)
                for t in range(TILES):
                    dve.wait_ge(gathered[t % RING], 32 * (t // RING + 1))
                    for j in range(2):
                        link(nc.vector.scalar_tensor_tensor(out=acc[:, t, :], in0=got[:, t % RING, j, :], scalar=picks.gate[:, j, t:t + 1],
                                                            in1=acc[:, t, :], op0=ALU.mult, op1=ALU.add))
                    dve.wait_ge(biases_ready, t + 1)
                    nc.vector.tensor_tensor(acc[:, t, :], acc[:, t, :], biased[:, t % 2, 0:D], ALU.add).then_inc(used, 1)


def best_two(nc, st, stage, ex, slot_rows, slot_outs, acc, given=None):
    with ExitStack() as ctx:
        picks = Picks(nc, ctx, stage, ex.experts)
        slot_outs = slot_outs[0:picks.windows * P, :]
        gate_nodes(nc, st, stage + "_gate", ex, picks, given)
        number_slots(nc, st, stage + "_number", ex, picks)
        send_nodes(nc, st, stage + "_send", picks, slot_rows)
        expert_windows(nc, st, stage + "_experts", ex, picks, slot_rows, slot_outs)
        collect_nodes(nc, st, stage + "_collect", ex, picks, slot_outs, acc)
```
